# Optimizing a Trainium2 kernel written in Bass

```python
import numpy as np
import jax
import jax.numpy as jnp

def _softmax(x, axis=-1):
    return jax.nn.softmax(x, axis=axis)

def _gelu(x):
    return jax.nn.gelu(x, approximate=True)

def _silu(x):
    return jax.nn.silu(x)

def _sigmoid(x):
    return jax.nn.sigmoid(x)

def _layernorm(x, axis=-1, eps=1e-05):
    m = jnp.mean(x, axis=axis, keepdims=True)
    v = jnp.var(x, axis=axis, keepdims=True)
    return (x - m) / jnp.sqrt(v + eps)

def _scatter_add(tgt, idx, src, axis=0):
    return tgt.at[idx].add(src)

def _segment_sum(src, seg, n):
    return jax.ops.segment_sum(src, seg, n)
kernel_name = 'mk_flamingo_gated_d1_seqx_r8_294fa8'

def setup_inputs(seed: int=0):
    np.random.seed(seed)
    _w = jnp.asarray

    def _rec_inputs():
        import jax
        import jax.numpy as jnp
        _rk = jax.random.key(seed)
        x = -0.0002928 + 1 * jax.random.normal(jax.random.fold_in(_rk, 1), (8, 256, 128), jnp.float32)
        _lenS = 256 - jax.random.randint(jax.random.fold_in(_rk, 7), (8,), 0, max(1, 256 // 4) + 1, jnp.int32)
        _lenS2 = 256 - jax.random.randint(jax.random.fold_in(_rk, 8), (8,), 0, max(1, 256 // 4) + 1, jnp.int32)
        _ctx_1024P = jax.random.normal(jax.random.fold_in(_rk, 11), (8, 16, 128), jnp.float32)
        _ctx_1024c = jax.random.dirichlet(jax.random.fold_in(_rk, 511), 0.3 * jnp.ones((16,), jnp.float32), (8, 256))
        _ctx_1024t = jnp.einsum('bsk,bkd->bsd', _ctx_1024c, _ctx_1024P)
        _ctx_1024t = _ctx_1024t * jax.lax.rsqrt(jnp.mean(jnp.square(_ctx_1024t)) + 1e-12) * 0.953939
        ctx_1024 = -1.39393e-06 + 0.999914 * (_ctx_1024t + 0.3 * jax.random.normal(jax.random.fold_in(_rk, 611), (8, 256, 128), jnp.float32))
        _g = jax.random.normal(jax.random.fold_in(_rk, 9001), (2, 1), jnp.float32)
        _g = jnp.sign(_g) * jnp.maximum(jnp.abs(_g), 1.0) + (_g == 0) * 1.0
        g_xattn = _g[0]
        g_ffn = _g[1]
        return (x, ctx_1024, g_xattn, g_ffn)
    x, ctx_1024, g_xattn, g_ffn = _rec_inputs()

    def _L0_xattn_setup():
        import jax, jax.numpy as jnp
        import numpy as np
        H = 16
        D_MODEL = 128
        D_K = D_MODEL // H

        def _mha(query, key, value, Wq, bq, Wk, bk, Wv, bv, Wo, bo):
            B, S, _ = query.shape
            q = query @ Wq.T + bq
            k = key @ Wk.T + bk
            v = value @ Wv.T + bv
            q = q.reshape(B, S, H, D_K).transpose(0, 2, 1, 3)
            k = k.reshape(B, S, H, D_K).transpose(0, 2, 1, 3)
            v = v.reshape(B, S, H, D_K).transpose(0, 2, 1, 3)
            scores = jnp.einsum('bhqd,bhkd->bhqk', q, k) / jnp.sqrt(jnp.float32(D_K))
            stable = scores - jnp.max(scores, axis=-1, keepdims=True)
            e = jnp.exp(stable)
            attn = e / jnp.sum(e, axis=-1, keepdims=True)
            ctx = jnp.einsum('bhqk,bhkd->bhqd', attn, v)
            ctx = ctx.transpose(0, 2, 1, 3).reshape(B, S, H * D_K)
            return ctx @ Wo.T + bo
        key = jax.random.key(seed)
        ks = jax.random.split(key, 11)
        B, S = (2, 256)
        scale = 1.0 / np.sqrt(D_MODEL)
        inp = {'query': jax.random.normal(ks[0], (B, S, D_MODEL), dtype=jnp.float32), 'key': jax.random.normal(ks[1], (B, S, D_MODEL), dtype=jnp.float32), 'value': jax.random.normal(ks[2], (B, S, D_MODEL), dtype=jnp.float32), 'Wq': jax.random.normal(ks[3], (D_MODEL, D_MODEL), dtype=jnp.float32) * scale, 'bq': jnp.zeros((D_MODEL,), dtype=jnp.float32), 'Wk': jax.random.normal(ks[4], (D_MODEL, D_MODEL), dtype=jnp.float32) * scale, 'bk': jnp.zeros((D_MODEL,), dtype=jnp.float32), 'Wv': jax.random.normal(ks[5], (D_MODEL, D_MODEL), dtype=jnp.float32) * scale, 'bv': jnp.zeros((D_MODEL,), dtype=jnp.float32), 'Wo': jax.random.normal(ks[6], (D_MODEL, D_MODEL), dtype=jnp.float32) * scale, 'bo': jnp.zeros((D_MODEL,), dtype=jnp.float32)}
        return inp
    _L0_xattn_all = _L0_xattn_setup()
    _L0_xattn_in = {k: v for k, v in _L0_xattn_all.items() if k in ('Wq', 'bq', 'Wk', 'bk', 'Wv', 'bv', 'Wo', 'bo')}
    del _L0_xattn_all

    def _L0_ffn_setup():
        import jax, jax.numpy as jnp
        import numpy as np
        B, S, D = (2, 256, 128)
        E, G, K = (32, 8, 4)
        H, SH = (256, 256)
        CAP_FACTOR = 1.25

        def _l2norm(v):
            n = jnp.linalg.norm(v, axis=-1, keepdims=True)
            return v / jnp.maximum(n, 1e-12)
        key = jax.random.key(seed)
        ks = jax.random.split(key, 10)
        x = jax.random.normal(ks[0], (B, S, D), jnp.float32)
        group_centroids = jax.random.normal(ks[1], (G, D), jnp.float32) * 0.02
        expert_centroids = jax.random.normal(ks[2], (E, D), jnp.float32) * 0.02
        bias = jnp.zeros((E,), jnp.float32)
        sd_in = 1.0 / np.sqrt(D).astype(np.float32)
        sd_h = 1.0 / np.sqrt(H).astype(np.float32)
        wg = jax.random.normal(ks[3], (E, D, H), jnp.float32) * sd_in
        wu = jax.random.normal(ks[4], (E, D, H), jnp.float32) * sd_in
        wd = jax.random.normal(ks[5], (E, H, D), jnp.float32) * sd_h
        sg = jax.random.normal(ks[6], (D, SH), jnp.float32) * sd_in
        su = jax.random.normal(ks[7], (D, SH), jnp.float32) * sd_in
        sd_w = jax.random.normal(ks[8], (SH, D), jnp.float32) * sd_h
        return dict(x=x, group_centroids=group_centroids, expert_centroids=expert_centroids, bias=bias, wg=wg, wu=wu, wd=wd, sg=sg, su=su, sd=sd_w)
    _L0_ffn_all = _L0_ffn_setup()
    _L0_ffn_in = {k: v for k, v in _L0_ffn_all.items() if k in ('group_centroids', 'expert_centroids', 'bias', 'wg', 'wu', 'wd', 'sg', 'su', 'sd')}
    del _L0_ffn_all
    return {'x': x, 'ctx_1024': ctx_1024, 'g_xattn': g_xattn, 'g_ffn': g_ffn, 'L0_xattn_Wq': _L0_xattn_in['Wq'], 'L0_xattn_bq': _L0_xattn_in['bq'], 'L0_xattn_Wk': _L0_xattn_in['Wk'], 'L0_xattn_bk': _L0_xattn_in['bk'], 'L0_xattn_Wv': _L0_xattn_in['Wv'], 'L0_xattn_bv': _L0_xattn_in['bv'], 'L0_xattn_Wo': _L0_xattn_in['Wo'], 'L0_xattn_bo': _L0_xattn_in['bo'], 'L0_ffn_group_centroids': _L0_ffn_in['group_centroids'], 'L0_ffn_expert_centroids': _L0_ffn_in['expert_centroids'], 'L0_ffn_bias': _L0_ffn_in['bias'], 'L0_ffn_wg': _L0_ffn_in['wg'], 'L0_ffn_wu': _L0_ffn_in['wu'], 'L0_ffn_wd': _L0_ffn_in['wd'], 'L0_ffn_sg': _L0_ffn_in['sg'], 'L0_ffn_su': _L0_ffn_in['su'], 'L0_ffn_sd': _L0_ffn_in['sd']}

def reference(x, ctx_1024, g_xattn, g_ffn, L0_xattn_Wq, L0_xattn_bq, L0_xattn_Wk, L0_xattn_bk, L0_xattn_Wv, L0_xattn_bv, L0_xattn_Wo, L0_xattn_bo, L0_ffn_group_centroids, L0_ffn_expert_centroids, L0_ffn_bias, L0_ffn_wg, L0_ffn_wu, L0_ffn_wd, L0_ffn_sg, L0_ffn_su, L0_ffn_sd):
    import jax
    import jax.numpy as jnp

    def _L0_xattn_ref(query, key, value, Wq, bq, Wk, bk, Wv, bv, Wo, bo):
        import jax, jax.numpy as jnp
        import numpy as np
        H = 16
        D_MODEL = 128
        D_K = D_MODEL // H

        def _mha(query, key, value, Wq, bq, Wk, bk, Wv, bv, Wo, bo):
            B, S, _ = query.shape
            q = query @ Wq.T + bq
            k = key @ Wk.T + bk
            v = value @ Wv.T + bv
            q = q.reshape(B, S, H, D_K).transpose(0, 2, 1, 3)
            k = k.reshape(B, S, H, D_K).transpose(0, 2, 1, 3)
            v = v.reshape(B, S, H, D_K).transpose(0, 2, 1, 3)
            scores = jnp.einsum('bhqd,bhkd->bhqk', q, k) / jnp.sqrt(jnp.float32(D_K))
            stable = scores - jnp.max(scores, axis=-1, keepdims=True)
            e = jnp.exp(stable)
            attn = e / jnp.sum(e, axis=-1, keepdims=True)
            ctx = jnp.einsum('bhqk,bhkd->bhqd', attn, v)
            ctx = ctx.transpose(0, 2, 1, 3).reshape(B, S, H * D_K)
            return ctx @ Wo.T + bo
        return _mha(query, key, value, Wq, bq, Wk, bk, Wv, bv, Wo, bo)

    def _L0_ffn_ref(x, group_centroids, expert_centroids, bias, wg, wu, wd, sg, su, sd):
        import jax, jax.numpy as jnp
        import numpy as np
        B, S, D = (2, 256, 128)
        E, G, K = (32, 8, 4)
        H, SH = (256, 256)
        CAP_FACTOR = 1.25

        def _l2norm(v):
            n = jnp.linalg.norm(v, axis=-1, keepdims=True)
            return v / jnp.maximum(n, 1e-12)
        b, s, d = x.shape
        xf = x.reshape(-1, d)
        N = xf.shape[0]
        shared = jax.nn.silu(xf @ sg) * (xf @ su) @ sd
        xn = _l2norm(xf)
        group_scores = xn @ _l2norm(group_centroids).T
        n_top_groups = max(1, G // 2)
        _, top_group_idx = jax.lax.top_k(group_scores, n_top_groups)
        expert_scores = xn @ _l2norm(expert_centroids).T + bias
        expert_to_group = jnp.arange(E) // (E // G)
        sel = jnp.zeros((N, G), xf.dtype).at[jnp.arange(N)[:, None], top_group_idx].set(1.0)
        group_mask = sel[:, expert_to_group]
        masked = expert_scores * group_mask + (1.0 - group_mask) * -1000000000.0
        top_scores, top_idx = jax.lax.top_k(masked, K)
        gates = jax.nn.softmax(top_scores, axis=-1)
        capacity = max(1, int(N / E * K * CAP_FACTOR))
        flat_e = top_idx.reshape(-1)
        flat_g = gates.reshape(-1)
        tok = jnp.repeat(jnp.arange(N), K)
        onehot = jax.nn.one_hot(flat_e, E, dtype=jnp.int32)
        pos = jnp.cumsum(onehot, axis=0)[jnp.arange(N * K), flat_e] - 1
        keep = pos < capacity
        e_s = jnp.where(keep, flat_e, E)
        p_s = jnp.where(keep, pos, 0)
        buf = jnp.zeros((E + 1, capacity, d), xf.dtype).at[e_s, p_s].set(xf[tok])[:E]
        h = jax.nn.silu(jnp.einsum('ecd,edh->ech', buf, wg)) * jnp.einsum('ecd,edh->ech', buf, wu)
        out_e = jnp.einsum('ech,ehd->ecd', h, wd)
        gathered = out_e[flat_e, jnp.minimum(pos, capacity - 1)]
        contrib = gathered * (flat_g * keep.astype(xf.dtype))[:, None]
        routed = jnp.zeros_like(xf).at[tok].add(contrib)
        return (shared + routed).reshape(b, s, d)
    x = x + jnp.tanh(g_xattn[0]) * _L0_xattn_ref(_layernorm(x, axis=-1), ctx_1024, ctx_1024, L0_xattn_Wq, L0_xattn_bq, L0_xattn_Wk, L0_xattn_bk, L0_xattn_Wv, L0_xattn_bv, L0_xattn_Wo, L0_xattn_bo)
    x = x + jnp.tanh(g_ffn[0]) * _L0_ffn_ref(_layernorm(x, axis=-1), L0_ffn_group_centroids, L0_ffn_expert_centroids, L0_ffn_bias, L0_ffn_wg, L0_ffn_wu, L0_ffn_wd, L0_ffn_sg, L0_ffn_su, L0_ffn_sd)
    return x

_drawn_inputs = setup_inputs


def setup_inputs(seed=0):
    import zlib

    import numpy as np

    out = dict(_drawn_inputs(seed))
    spreads = {'L0_xattn_bq': (0.0, 0.1),
     'L0_xattn_bk': (0.0, 0.1),
     'L0_xattn_bv': (0.0, 0.1),
     'L0_xattn_bo': (0.0, 0.1),
     'L0_ffn_bias': (0.0, 0.1)}
    factors = {}
    for name, (base, spread) in spreads.items():
        noise = np.random.default_rng([zlib.crc32(name.encode()), seed]).standard_normal(out[name].shape)
        drawn = base * np.exp(spread * noise) if base else spread * noise
        out[name] = jnp.asarray(drawn.astype(out[name].dtype))
    for name, factor in factors.items():
        out[name] = (out[name] * factor).astype(out[name].dtype)
    return out
```

```python
import concourse.bass as bass
from concourse import mybir
from contextlib import ExitStack

B, S, D = 8, 256, 128
H, DK = 16, 8
N = B * S
E, G, K = 32, 8, 4
F = 256
CAP = int(N / E * K * 1.25)
P = 128
EG = E // G
ROW = D + 4
COL_TOKEN, COL_GATE = D, D + 1
DUMP = CAP
NG = H // 4
M_ROW, M_STEP = 15, 16


class Batch:

    def __init__(self, i, k):
        self.half, self.par = i + k // 2, k % 2
        self.n = 2 * i + k
        self.i, self.k = i, k

    def __add__(self, d):
        return Batch(self.i, self.k + d)

    def exists(self):
        return not isinstance(self.n, int) or 0 <= self.n < B


class Chain:

    def __init__(self, eng, sem, start):
        self.eng, self.sem, self.start, self.n = eng, sem, start, 0

    def add(self, ins):
        ins.then_inc(self.sem, 1)
        self.n += 1

    def wait(self):
        self.eng.wait_ge(self.sem, self.start + self.n)


def reached(eng, sem, value):
    if not isinstance(value, int) or value > 0:
        eng.wait_ge(sem, value)


def gated_attention_and_experts(
    nc, x, ctx_in, g_xattn, g_ffn, wq_t, bq, wk_t, bk, wv_t, bv, wo_t, bo,
    group_centroids, expert_centroids, bias, w_all, sg, su, sd, out, dispatch, sums, loops=True,
):
    fp32, fp32r, bf16 = mybir.dt.float32, mybir.dt.float32r, mybir.dt.bfloat16
    u32, i32 = mybir.dt.uint32, mybir.dt.int32
    ALU, ACT, AX = mybir.AluOpType, mybir.ActivationFunctionType, mybir.AxisListType
    SCALE = float(DK) ** -0.5

    ctx = ExitStack()
    with ctx:
        def sb(name, shape, dt=fp32):
            return ctx.enter_context(nc.sbuf_tensor(name, shape, dt))

        def sem(name):
            return ctx.enter_context(nc.semaphore(name))

        def f32(ap):
            return ap.bitcast(fp32)

        def spread(ap, axis, n):
            ap = ap.unsqueeze(axis)
            shape = list(ap.shape)
            shape[axis] = n
            return ap.to_broadcast(shape)

        wq_sb, wk_sb, wv_sb, wo_sb = (sb(n, [P, D]) for n in ("wq_sb", "wk_sb", "wv_sb", "wo_sb"))
        bq_sb, bk_sb, bv_sb = (sb(n, [P, 1]) for n in ("bq_sb", "bk_sb", "bv_sb"))
        bo_bc, bias_bc = sb("bo_bc", [P, D]), sb("bias_bc", [P, E])
        gates_in, gates = sb("gates_in", [P, 2]), sb("gates", [P, 2])
        tanh_x, tanh_f = gates[:, 0:1], gates[:, 1:2]
        ident = sb("ident", [P, P])
        iden_r = sb("iden_r", [P, P])
        m_ones = sb("m_ones", [P, 1])
        pick = sb("pick", [P, 4, NG, P], fp32r)
        before = sb("before", [P, P], bf16)
        ones = sb("ones", [P, P], bf16)
        iota_i, iota_f = sb("iota_i", [P, E], i32), sb("iota_f", [P, E])
        tok_i, tok_f = sb("tok_i", [P, 2], i32), sb("tok_f", [P, 2])
        neg_half = sb("neg_half", [P, 2])
        cents, cent_sq, cent_n = sb("cents", [G + E, D]), sb("cent_sq", [G + E, D]), sb("cent_n", [G + E, 2])
        cent_t = sb("cent_t", [P, G + E])
        blank, blank_i = sb("blank", [P, 3, ROW]), sb("blank_i", [P, 3], i32)

        x_sb = [sb(f"x_sb{i}", [P, 2, D]) for i in range(2)]
        c_sb = [sb(f"c_sb{i}", [P, 2, D]) for i in range(2)]
        xb = [sb(f"xb{i}", [P, 2, D]) for i in range(2)]
        stat1, aggr1, rstd1 = sb("stat1", [P, 2, 6]), sb("aggr1", [P, 2, 2]), sb("rstd1", [P, 2])
        h1 = sb("h1", [P, 2, D])
        hc_t = sb("hc_t", [P, 4, P])
        qk = sb("qk", [P, 2, S])
        qk_hi, qk_lo = sb("qk_hi", [P, 2, S], fp32r), sb("qk_lo", [P, 2, S], fp32r)
        q_rows = [sb(f"q_rows{i}", [P, 2, S], fp32r) for i in range(4)]
        k_rows = [sb(f"k_rows{i}", [P, 2, S], fp32r) for i in range(4)]
        v_ext = [sb(f"v_ext{i}", [P, 2, H, DK + 1]) for i in range(2)]
        neg_max = [sb(f"neg_max{i}", [P, 2, 2, 4]) for i in range(2)]
        neg_hl = [sb(f"neg_hl{i}", [P, 2, 2, 4, 2], fp32r) for i in range(2)]
        max_t = [sb(f"max_t{i}", [16, S], fp32r) for i in range(2)]
        probs = [sb(f"probs{i}", [P, 2, 2, 2, S]) for i in range(2)]
        inv_sum = sb("inv_sum", [P, 2, H])
        heads = sb("heads", [P, 2, D])
        heads_t = sb("heads_t", [P, 2, P])

        x1 = [sb(f"x1_{i}", [P, 2, D]) for i in range(2)]
        stat2, aggr2, rstd2 = sb("stat2", [P, 2, 6]), sb("aggr2", [P, 2, 2]), sb("rstd2", [P, 2])
        norm2 = sb("norm2", [P, 3, 2])
        h2_rows = [sb(f"h2_rows{i}", [P, 2, K, ROW]) for i in range(2)]
        h2_t = [sb(f"h2_t{i}", [P, 2, P]) for i in range(2)]
        top_g, top_gi = sb("top_g", [P, 2, 8]), sb("top_gi", [P, 2, 8], u32)
        is_g, mask_g, gap_g = sb("is_g", [P, 2, G, K]), sb("mask_g", [P, 2, G]), sb("gap_g", [P, 2, G])
        score, masked = sb("score", [P, 2, E]), sb("masked", [P, 2, E])
        top_e, top_ei = sb("top_e", [P, 2, 8]), sb("top_ei", [P, 2, 8], u32)
        chosen = sb("chosen", [P, 2, K, E])
        chosen_any = sb("chosen_any", [P, 2, E], bf16)
        earlier = [sb(f"earlier{i}", [P, E], bf16) for i in range(2)]
        diff, expd, gate = sb("diff", [P, 2, K]), sb("expd", [P, 2, K]), sb("gate", [P, 2, K])
        gate_sum, gate_inv = sb("gate_sum", [P, 2]), sb("gate_inv", [P, 2])
        at_slot, pos, slot_f = sb("at_slot", [P, 2, K, E]), sb("pos", [P, 2, K]), sb("slot_f", [P, 2, K])
        keep = sb("keep", [P, 2, K])
        slot_i = [sb(f"slot_i{i}", [P, 2, K], u32) for i in range(2)]
        x1_all, h2t_all = sb("x1_all", [P, N // P, D]), sb("h2t_all", [P, N])

        WR = 4
        sg_sb, su_sb, sd_sb = sb("sg_sb", [P, F]), sb("su_sb", [P, F]), sb("sd_sb", [P, 2, D])
        w_sb = [sb(f"w_sb{i}", [P, 6, P]) for i in range(WR)]
        e_rows = [sb(f"e_rows{i}", [P, 3, ROW]) for i in range(WR)]
        e_t = [sb(f"e_t{i}", [P, CAP]) for i in range(2)]
        silu_g = sb("silu_g", [P, 2, 512])
        hid = [sb(f"hid{i}", [P, 2, 512]) for i in range(2)]
        y_sb = [sb(f"y_sb{i}", [P, 3, D]) for i in range(2)]
        base = [sb(f"base{i}", [P, 4, D]) for i in range(2)]

        ps = ctx.enter_context(nc.psum_tensor("ps", [P, 8, 512], fp32))
        score_t = [ps[:, 2 * i:2 * i + 2, :] for i in range(2)]
        score_n = [ps[:, 4 + i, :] for i in range(2)]
        heads_ps = ps[:, 6, 0:2 * H * (DK + 1)].rearrange("p (c h d) -> p c h d", c=2, d=DK + 1)
        misc = ps[:, 7, :]

        in_x, in_c = [sem(f"in_x{i}") for i in range(2)], [sem(f"in_c{i}") for i in range(2)]
        in_w, in_shared = sem("in_w"), sem("in_shared")
        set_pool, set_dve, set_act, set_pe = sem("set_pool"), sem("set_dve"), sem("set_act"), sem("set_pe")
        pool_const = sem("pool_const")
        consts = sem("consts")
        blanked = sem("blanked")
        var1, rstd1_ready, h1_ready, xb_ready = sem("var1"), sem("rstd1_ready"), sem("h1_ready"), sem("xb_ready")
        t_full, t_out = sem("t_full"), sem("t_out")
        qk_full, qk_out = sem("qk_full"), sem("qk_out")
        qk_split, split_own = sem("qk_split"), sem("split_own")
        v_full, v_out = sem("v_full"), sem("v_out")
        rows_full, rows_out = sem("rows_full"), sem("rows_out")
        sn_full, sn_max = sem("sn_full"), sem("sn_max")
        neg_own, neg_ready = sem("neg_own"), sem("neg_ready")
        mt_full, mt_out = sem("mt_full"), sem("mt_out")
        m_landed = [sem(f"m_landed{i}") for i in range(2)]
        st_full, exp_done = sem("st_full"), sem("exp_done")
        pv_done = sem("pv_done")
        inv_own, heads_ready = sem("inv_own"), sem("heads_ready")
        ht_full, ht_out = sem("ht_full"), sem("ht_out")
        wo_full, x1_ready = sem("wo_full"), sem("x1_ready")
        ln_own, var2, rstd2_ready, h2_ready = sem("ln_own"), sem("var2"), sem("rstd2_ready"), sem("h2_ready")
        pool_ln1, pool_ln2 = sem("pool_ln1"), sem("pool_ln2")
        h2t_full, h2t_out = sem("h2t_full"), sem("h2t_out")
        kept_x, kept_h = [sem(f"kept_x{i}") for i in range(2)], [sem(f"kept_h{i}") for i in range(2)]
        sc_full, sc_used, route_own = sem("sc_full"), sem("sc_used"), sem("route_own")
        chosen_ready, diff_ready, exp_ready = sem("chosen_ready"), sem("diff_ready"), sem("exp_ready")
        earlier_own, earlier_ready = sem("earlier_own"), sem("earlier_ready")
        cnt_full, cnt_used, place_own, slots_ready = sem("cnt_full"), sem("cnt_used"), sem("place_own"), sem("slots_ready")
        token_written, tok_next = sem("token_written"), sem("tok_next")
        scattered = [sem(f"scattered{i}") for i in range(2)]
        sh_g, sh_u, sh_silu, sh_hid, sh_y, sh_out = (sem(n) for n in ("sh_g", "sh_u", "sh_silu", "sh_hid", "sh_y", "sh_out"))
        base_out = [sem(f"base_out{i}") for i in range(2)]
        w_in, rows_in = [sem(f"w_in{i}") for i in range(WR)], [sem(f"rows_in{i}") for i in range(WR)]
        et_full, et_out, g_full, u_full = sem("et_full"), sem("et_out"), sem("g_full"), sem("u_full")
        silu_done, hid_ready, y_full, y_out = sem("silu_done"), sem("hid_ready"), sem("y_full"), sem("y_out")
        added, written = sem("added"), sem("written")
        passed = sem("passed")
        stat_own1, stat_own2, norm_ready, set_dve2 = sem("stat_own1"), sem("stat_own2"), sem("norm_ready"), sem("set_dve2")
        ROUTE_OPS, PLACE_OPS = 14, 8
        FAR = 1048576.0

        SLOTS = 16
        FIRST, LAST = -2, B
        LOOP_FROM, LOOP_PAIRS = 1, 2

        ROUNDS = [(1, "max1", 0), (2, "v", 1), (3, "heads", -1), (4, "wo", -1), (5, "q1", 1), (6, "k1", 1),
                  (7, "t", 2), (8, "h2", -1), (9, "qk", 2), (10, "max0", 1), (11, "score", -1),
                  (12, "q0", 2), (13, "k0", 2), (14, "count", -1)]

        def emptied(name, b):
            n = b.n
            return {"max0": (mt_out, 2 * n + 1), "max1": (mt_out, 2 * n + 2), "v": (v_out, n + 1),
                    "heads": (ht_out, n + 1), "wo": (x1_ready, n + 1), "t": (t_out, n + 1),
                    "q0": (rows_out, 4 * n + 1), "k0": (rows_out, 4 * n + 2),
                    "q1": (rows_out, 4 * n + 3), "k1": (rows_out, 4 * n + 4),
                    "h2": (h2t_out, n + 1), "qk": (qk_out, 2 * n + 2), "score": (sc_used, n + 1),
                    "count": (cnt_used, n + 1)}[name]

        def round_before(t, at):
            while True:
                at -= 1
                if at < 0:
                    at, t = len(ROUNDS) - 1, t + -1
                _, name, off = ROUNDS[at]
                b = t + off
                if isinstance(t.n, int) and t.n < FIRST:
                    return set_act, 2
                if b.exists():
                    return emptied(name, b)

        def settle(eng):
            eng.sem_inc(passed, 1)

        def steps(eng, step):
            t = FIRST
            while t <= LAST:
                if t == LOOP_FROM and loops:
                    with eng.Fori(0, LOOP_PAIRS) as i:
                        for k in range(2):
                            step(Batch(i, LOOP_FROM + k))
                    t += 2 * LOOP_PAIRS
                else:
                    step(Batch(0, t))
                    t += 1

        def expert_steps(eng, expert):
            if loops:
                with eng.Fori(0, E // WR - 1) as i:
                    for k in range(2, WR + 2):
                        expert(i, k)
            else:
                for i in range(E // WR - 1):
                    for k in range(2, WR + 2):
                        expert(i, k)

        block = ctx.enter_context(nc.Block())

        @block.sync
        def _(sp):
            def load(b):
                if b.exists():
                    reached(sp, h1_ready, b.n - 1)
                    reached(sp, xb_ready, b.n - 1)
                    sp.dma_start(x_sb[b.par][:], x[b.n].rearrange("(c p) d -> p c d", p=P)).then_inc(in_x[b.par], 16)
                    reached(sp, t_full, b.n - 1)
                    sp.dma_start(c_sb[b.par][:], ctx_in[b.n].rearrange("(c p) d -> p c d", p=P)).then_inc(in_c[b.par], 16)

            def max_rows(b, gh):
                if b.exists():
                    reached(sp, mt_out, 2 * b.n + gh + 1)
                    for g in range(2):
                        dst = q_rows[2 * b.par + gh][M_ROW:P:M_STEP, g, :]
                        sp.dma_start(f32(dst), f32(max_t[gh][8 * g:8 * g + 8, :])).then_inc(m_landed[gh], 16)

            def step(t):
                for s in range(SLOTS):
                    if s == 1:
                        max_rows(t, 1)
                    if s == 7:
                        load(t + 3)
                    if s == 9 and (t + -1).exists():
                        b = t + -1
                        reached(sp, x1_ready, b.n + 1)
                        sp.dma_start(x1_all[:, bass.ds(2 * b.n, 2), :], x1[b.par][:]).then_inc(kept_x[b.par], 16)
                        reached(sp, h2t_out, b.n + 1)
                        sp.dma_start(h2t_all[:, bass.ds(S * b.n, S)],
                                     h2_t[b.par][:].rearrange("p c t -> p (c t)")).then_inc(kept_h[b.par], 16)
                    if s == 10:
                        max_rows(t + 1, 0)

            load(Batch(0, 0))
            for dst, src in ((wq_sb, wq_t), (wk_sb, wk_t), (wv_sb, wv_t), (wo_sb, wo_t),
                             (bq_sb, bq.rearrange("(p o) -> p o", o=1)), (bk_sb, bk.rearrange("(p o) -> p o", o=1)),
                             (bv_sb, bv.rearrange("(p o) -> p o", o=1)),
                             (bo_bc, bo.partition_broadcast(P)), (bias_bc, bias.partition_broadcast(P)),
                             (gates_in[:, 0:1], g_xattn.partition_broadcast(P)),
                             (gates_in[:, 1:2], g_ffn.partition_broadcast(P)),
                             (cents[0:G, :], group_centroids), (cents[G:G + E, :], expert_centroids)):
                sp.dma_start(dst[:], src).then_inc(in_w, 16)
            sp.dma_start(sg_sb[:], sg).then_inc(in_shared, 16)
            sp.dma_start(su_sb[:], su).then_inc(in_shared, 16)
            sp.dma_start(sd_sb[:], sd.rearrange("(c p) d -> p c d", p=P)).then_inc(in_shared, 16)
            sp.wait_ge(consts, 1)
            rows = dispatch.rearrange("(e r) w -> e r w", r=CAP)
            sp.dma_start(rows[:, 0:2 * P, :].rearrange("e (p c) w -> p e (c w)", c=2),
                         spread(blank[:, 0:2, :].rearrange("p c w -> p (c w)"), 1, E)).then_inc(blanked, 16)
            sp.dma_start(rows[:, 2 * P:CAP, :].rearrange("e p w -> p e w"),
                         spread(blank[0:CAP - 2 * P, 2, :], 1, E)).then_inc(blanked, 16)
            sp.dma_start(sums[N:N + DUMP, :].rearrange("(p r) d -> p r d", p=64), spread(blank[0:64, 0, 0:D], 1, DUMP // 64)).then_inc(blanked, 16)
            steps(sp, step)

            def load_expert(i, r, ahead):
                e = WR * i + r
                if ahead:
                    sp.wait_ge(y_full, e - WR + 1)
                sp.dma_start(w_sb[r][:], w_all[e]).then_inc(w_in[r], 16)
                if ahead:
                    sp.wait_ge(added, 48 * (e - WR + 1))
                rows_of(sp, e, r)

            def rows_of(sp, e, r):
                rows_e = dispatch[bass.ds(e * CAP, CAP), :]
                sp.dma_start(e_rows[r][:, 0:2, :], rows_e[0:2 * P, :].rearrange("(p c) w -> p c w", c=2)).then_inc(rows_in[r], 16)
                sp.dma_start(e_rows[r][0:CAP - 2 * P, 2, :], rows_e[2 * P:CAP, :]).then_inc(rows_in[r], 16)

            for r in range(WR):
                sp.dma_start(w_sb[r][:], w_all[r]).then_inc(w_in[r], 16)
            for i in range(2):
                sp.wait_ge(scattered[i], 16 * 2 * K * (B // 2))
            for r in range(WR):
                rows_of(sp, r, r)
            if loops:
                with sp.Fori(1, E // WR) as i:
                    for r in range(WR):
                        load_expert(i, r, True)
            else:
                for i in range(1, E // WR):
                    for r in range(WR):
                        load_expert(i, r, True)
            sp.wait_ge(added, 48 * E)
            sp.dma_start(out.rearrange("b s d -> (b s) d"), sums[0:N, :]).then_inc(written, 16)
            sp.wait_ge(written, 16)

        @block.tensor
        def _(pe):
            def mm(dst, lhs_t, rhs, start=True, stop=True):
                return nc.tensor.matmul(dst, lhs_t, rhs, start=start, stop=stop)

            def rows_round(kind, gh):
                for g2 in range(2):
                    g = 2 * gh + g2
                    dst = misc[:, g2 * S:(g2 + 1) * S]
                    mm(dst, pick[:, 2 * kind, g, :], qk_hi[:, kind, :], True, False)
                    last = mm(dst, pick[:, 2 * kind + 1, g, :], qk_lo[:, kind, :], False, True)
                last.then_inc(rows_full, 1)

            def max_round(b, gh):
                reached(pe, neg_ready, 2 * b.n + gh + 1)
                for qc in range(2):
                    last = nc.tensor.transpose(misc[0:16, qc * P:(qc + 1) * P],
                                               f32(neg_hl[gh][:, qc].rearrange("p g j t -> p (g j t)")), ident[:])
                last.then_inc(mt_full, 1)

            def do_round(name, b):
                if name in ("max0", "max1"):
                    max_round(b, int(name[-1]))
                elif name == "t":
                    reached(pe, h1_ready, b.n + 1)
                    pe.wait_ge(in_c[b.par], 16 * (b.half + 1))
                    for c in range(4):
                        src = h1[:, c, :] if c < 2 else c_sb[b.par][:, c - 2, :]
                        last = nc.tensor.transpose(misc[:, c * P:(c + 1) * P], src, ident[:])
                    last.then_inc(t_full, 1)
                elif name == "qk":
                    reached(pe, t_out, b.n + 1)
                    mm(misc[:, 0:S], wq_sb[:], hc_t[:, 0:2, :].rearrange("p c t -> p (c t)"))
                    mm(misc[:, S:2 * S], wk_sb[:], hc_t[:, 2:4, :].rearrange("p c t -> p (c t)")).then_inc(qk_full, 1)
                elif name == "v":
                    for c in range(2):
                        last = mm(misc[:, c * P:(c + 1) * P], hc_t[:, 2 + c, :], wv_sb[:])
                    last.then_inc(v_full, 1)
                elif name in ("q0", "q1", "k0", "k1"):
                    reached(pe, qk_split, b.n + 1)
                    rows_round("qk".index(name[0]), int(name[1]))
                elif name == "heads":
                    reached(pe, heads_ready, b.n + 1)
                    for c in range(2):
                        last = nc.tensor.transpose(misc[:, c * P:(c + 1) * P], heads[:, c, :], ident[:])
                    last.then_inc(ht_full, 1)
                elif name == "wo":
                    reached(pe, ht_out, b.n + 1)
                    for c in range(2):
                        last = mm(misc[:, c * P:(c + 1) * P], heads_t[:, c, :], wo_sb[:])
                    last.then_inc(wo_full, 1)
                elif name == "h2":
                    reached(pe, h2_ready, b.n + 1)
                    for c in range(2):
                        last = nc.tensor.transpose(misc[:, c * P:(c + 1) * P], h2_rows[b.par][:, c, 0, 0:D], ident[:])
                    last.then_inc(h2t_full, 1)
                elif name == "score":
                    reached(pe, h2t_out, b.n + 1)
                    for c in range(2):
                        last = mm(misc[:, c * (G + E):(c + 1) * (G + E)], h2_t[b.par][:, c, :], cent_t[:])
                    last.then_inc(sc_full, 1)
                elif name == "count":
                    reached(pe, chosen_ready, b.n + 1)
                    reached(pe, earlier_ready, b.n)
                    mm(misc[:, 0:E], before[:], chosen_any[:, 0, :], True, False)
                    mm(misc[:, 0:E], ones[:], earlier[b.par][:], False, True)
                    mm(misc[:, E:2 * E], before[:], chosen_any[:, 1, :], True, False)
                    mm(misc[:, E:2 * E], ones[:], chosen_any[:, 0, :], False, False)
                    mm(misc[:, E:2 * E], ones[:], earlier[b.par][:], False, True).then_inc(cnt_full, 1)

            def scores_for_max(b, s):
                gh, j, qc = s // 8, (s % 8) // 2, s % 2
                q, k = q_rows[2 * b.par + gh], k_rows[2 * b.par + gh]
                if s % 8 == 0:
                    reached(pe, rows_out, 4 * b.n + 2 * gh + 2)
                reached(pe, sn_max, 16 * b.n + s - 1)
                for g2 in range(2):
                    last = mm(score_n[s % 2][:, g2 * S:(g2 + 1) * S], q[32 * j:32 * j + 32, g2, qc * P:(qc + 1) * P],
                              k[32 * j:32 * j + 32, g2, :])
                last.then_inc(sn_full, 1)

            def scores_for_exp(b, u):
                gh, jp, kc = u // 4, (u // 2) % 2, u % 2
                q, k = q_rows[2 * b.par + gh], k_rows[2 * b.par + gh]
                if u % 4 == 0:
                    reached(pe, m_landed[gh], 32 * (b.n + 1))
                reached(pe, exp_done, 8 * b.n + u - 1)
                for g2 in range(2):
                    for jj in range(2):
                        r = 32 * (2 * jp + jj)
                        last = mm(score_t[u % 2][:, jj, g2 * S:(g2 + 1) * S], k[r:r + 32, g2, kc * P:(kc + 1) * P],
                                  q[r:r + 32, g2, :])
                last.then_inc(st_full, 1)

            def times_values(b, piece):
                w, r = piece // 4, piece % 4
                gh, jp, jj, g2 = w // 2, w % 2, r // 2, r % 2
                h = 4 * (2 * jp + jj) + 2 * gh + g2
                if piece == 0:
                    reached(pe, v_out, b.n + 1)
                    reached(pe, heads_ready, b.n)
                if r == 0:
                    reached(pe, exp_done, 8 * b.n + 2 * w + 2)
                for qc in range(2):
                    for kc in range(2):
                        last = mm(heads_ps[:, qc, h, :], probs[w % 2][:, kc, jj, g2, qc * P:(qc + 1) * P],
                                  v_ext[b.par][:, kc, h, :], kc == 0, kc == 1)
                last.then_inc(pv_done, 1)

            def step(t):
                for s in range(SLOTS):
                    if (t + 1).exists():
                        scores_for_max(t + 1, s)
                    if t.exists() and s % 2 == 0:
                        scores_for_exp(t, s // 2)
                    if s < 2 and (t + -1).exists():
                        times_values(t + -1, 12 + 2 * s)
                        times_values(t + -1, 13 + 2 * s)
                    if s >= 4 and t.exists():
                        times_values(t, s - 4)
                    for at, (slot, name, off) in enumerate(ROUNDS):
                        if slot == s and (t + off).exists():
                            reached(pe, *round_before(t, at))
                            do_round(name, t + off)

            pe.wait_ge(set_dve, 3)
            pe.wait_ge(pool_const, 1)
            nc.tensor.transpose(misc[:, 0:G + E], cents[:], ident[0:G + E, 0:G + E]).then_inc(set_pe, 1)
            pe.wait_ge(consts, 1)
            pe.wait_ge(in_w, 16 * 13)
            steps(pe, step)

            g_ps, u_ps = ps[:, 0:2, :], ps[:, 2:4, :]
            y_ps = [ps[:, 6 + i, :] for i in range(2)]
            x_ps = [ps[:, 4 + i, :] for i in range(2)]
            pe.wait_ge(in_shared, 48)
            pe.wait_ge(exp_done, 8 * B)
            pe.wait_ge(cnt_used, B)
            for i in range(2):
                pe.wait_ge(kept_h[i], 16 * (B // 2))
            NQ = N // 512

            def shared_down(q):
                pe.wait_ge(sh_hid, q + 1)
                reached(pe, sh_out, q - 1)
                for tile in range(4):
                    for c in range(2):
                        last = mm(y_ps[q % 2][:, tile * D:(tile + 1) * D], hid[q % 2][:, c, tile * P:(tile + 1) * P],
                                  sd_sb[:, c, :], c == 0, c == 1)
                last.then_inc(sh_y, 1)

            for q in range(NQ):
                reached(pe, sh_silu, q)
                for c in range(2):
                    last = mm(g_ps[:, c, :], sg_sb[:, c * P:(c + 1) * P], h2t_all[:, q * 512:(q + 1) * 512])
                last.then_inc(sh_g, 1)
                reached(pe, sh_hid, q)
                for c in range(2):
                    last = mm(u_ps[:, c, :], su_sb[:, c * P:(c + 1) * P], h2t_all[:, q * 512:(q + 1) * 512])
                last.then_inc(sh_u, 1)
                if q:
                    shared_down(q - 1)
            shared_down(NQ - 1)
            pe.wait_ge(sh_out, NQ)

            def transposes(i, k):
                e, r = WR * i + k, k % WR
                pe.wait_ge(rows_in[r], 32 * (i + k // WR + 1))
                reached(pe, et_out, e - 1)
                for c, n in ((0, P), (1, P), (2, CAP - 2 * P)):
                    last = nc.tensor.transpose(x_ps[k % 2][:, c * P:c * P + n], e_rows[r][0:n, c, 0:D], ident[0:n, 0:n])
                last.then_inc(et_full, 1)

            def gate_up(i, k):
                e, r = WR * i + k, k % WR
                pe.wait_ge(w_in[r], 16 * (i + k // WR + 1))
                pe.wait_ge(et_out, e + 1)
                reached(pe, silu_done, e)
                for c in range(2):
                    last = mm(g_ps[:, c, 0:CAP], w_sb[r][:, c, :], e_t[k % 2][:])
                last.then_inc(g_full, 1)
                reached(pe, hid_ready, e)
                for c in range(2):
                    last = mm(u_ps[:, c, 0:CAP], w_sb[r][:, 2 + c, :], e_t[k % 2][:])
                last.then_inc(u_full, 1)

            def down(i, k):
                e, r = WR * i + k, k % WR
                pe.wait_ge(hid_ready, e + 1)
                reached(pe, y_out, e - 1)
                for tile, n in ((0, P), (1, P), (2, CAP - 2 * P)):
                    for c in range(2):
                        last = mm(y_ps[k % 2][0:n, tile * D:(tile + 1) * D], hid[k % 2][:, c, tile * P:tile * P + n],
                                  w_sb[r][:, 4 + c, :], c == 0, c == 1)
                last.then_inc(y_full, 1)

            def expert(i, k):
                gate_up(i, k)
                down(i, k - 1)
                transposes(i, k + 1)

            transposes(0, 0)
            gate_up(0, 0)
            transposes(0, 1)
            expert(0, 1)
            expert_steps(pe, expert)
            for k in range(E - 2, E):
                gate_up(0, k)
                down(0, k - 1)
                if k + 1 < E:
                    transposes(0, k + 1)
            down(0, E - 1)

        @block.scalar
        def _(act):
            def copy_out(dst, src, full, count, done, bias=None):
                reached(act, full, count)
                if bias is None:
                    nc.scalar.activation(dst, src, ACT.Copy).then_inc(done, 1)
                else:
                    nc.scalar.activation(dst, src, ACT.Identity, bias=bias).then_inc(done, 1)

            def do_round(name, b):
                n = b.n
                if name in ("max0", "max1"):
                    gh = int(name[-1])
                    reached(act, m_landed[gh], 32 * n)
                    copy_out(max_t[gh][:], misc[0:16, 0:S], mt_full, 2 * n + gh + 1, mt_out)
                elif name == "v":
                    reached(act, pv_done, 16 * (n - 1))
                    copy_out(v_ext[b.par][:, :, :, 0:DK],
                             misc[:, 0:2 * D].rearrange("p (c h d) -> p c h d", c=2, d=DK), v_full, n + 1, v_out)
                elif name == "t":
                    copy_out(hc_t[:].rearrange("p c t -> p (c t)"), misc, t_full, n + 1, t_out)
                elif name == "qk":
                    reached(act, qk_split, n)
                    copy_out(qk[:, 0, :], misc[:, 0:S], qk_full, n + 1, qk_out, bias=bq_sb[:])
                    copy_out(qk[:, 1, :], misc[:, S:2 * S], qk_full, n + 1, qk_out, bias=bk_sb[:])
                elif name in ("q0", "q1", "k0", "k1"):
                    gh, is_k = int(name[1]), name[0] == "k"
                    reached(act, st_full, 8 * (n - 2) + 4 * gh + 4)
                    dst = (k_rows if is_k else q_rows)[2 * b.par + gh][:].rearrange("p g t -> p (g t)")
                    copy_out(dst, misc, rows_full, 4 * n + 2 * gh + is_k + 1, rows_out, bias=m_ones[:] if is_k else None)
                elif name == "heads":
                    copy_out(heads_t[:].rearrange("p c t -> p (c t)"), misc[:, 0:S], ht_full, n + 1, ht_out, bias=bv_sb[:])
                elif name == "h2":
                    reached(act, kept_h[b.par], 16 * b.half)
                    copy_out(h2_t[b.par][:].rearrange("p c t -> p (c t)"), misc[:, 0:S], h2t_full, n + 1, h2t_out)

            def exp_unit(b, u):
                w, kc = u // 2, u % 2
                reached(act, st_full, 8 * b.n + u + 1)
                reached(act, pv_done, 16 * b.n + 4 * w - 4)
                nc.scalar.activation(probs[w % 2][:, kc].rearrange("p j g t -> p (j g t)"),
                                     score_t[u % 2].rearrange("p j n -> p (j n)"), ACT.Exp,
                                     scale=SCALE).then_inc(exp_done, 1)

            def step(t):
                for s in range(SLOTS):
                    if t.exists() and s % 2 == 0:
                        exp_unit(t, s // 2)
                    for slot, name, off in ROUNDS:
                        if slot == s and (t + off).exists():
                            do_round(name, t + off)
                    if s == 13 and (t + -1).exists():
                        b = t + -1
                        reached(act, diff_ready, b.n + 1)
                        nc.scalar.activation(expd[:], diff[:], ACT.Exp).then_inc(exp_ready, 1)

            act.wait_ge(in_w, 16 * 13)
            nc.scalar.activation(gates[:], gates_in[:], ACT.Tanh).then_inc(set_act, 1)
            act.wait_ge(set_pe, 1)
            nc.scalar.activation(cent_t[:], misc[:, 0:G + E], ACT.Copy).then_inc(set_act, 1)
            steps(act, step)

            for q in range(N // 512):
                act.wait_ge(sh_g, q + 1)
                reached(act, sh_hid, q)
                nc.scalar.activation(silu_g[:], ps[:, 0:2, :], ACT.Silu).then_inc(sh_silu, 1)

            def copy_rows(i, k):
                e = WR * i + k
                act.wait_ge(et_full, e + 1)
                reached(act, u_full, e - 1)
                nc.scalar.activation(e_t[k % 2][:], ps[:, 4 + k % 2, 0:CAP], ACT.Copy).then_inc(et_out, 1)

            def silu(i, k):
                e = WR * i + k
                act.wait_ge(g_full, e + 1)
                reached(act, hid_ready, e)
                nc.scalar.activation(silu_g[:, :, 0:CAP], ps[:, 0:2, 0:CAP], ACT.Silu).then_inc(silu_done, 1)

            def expert(i, k):
                silu(i, k)
                copy_rows(i, k + 1)

            act.wait_ge(sh_hid, N // 512)
            copy_rows(0, 0)
            silu(0, 0)
            copy_rows(0, 1)
            expert(0, 1)
            expert_steps(act, expert)
            for k in range(E - 2, E):
                silu(0, k)
                if k + 1 < E:
                    copy_rows(0, k + 1)

        @block.vector
        def _(dve):
            V = nc.vector

            def max_unit(b, s):
                gh, j, qc = s // 8, (s % 8) // 2, s % 2
                if s % 8 == 0:
                    reached(dve, neg_ready, 2 * (b.n - 1) + gh + 1)
                reached(dve, sn_full, 16 * b.n + s + 1)
                V.tensor_reduce(neg_max[gh][:, qc, :, j], score_n[s % 2].rearrange("p (g t) -> p g t", g=2),
                                AX.X, ALU.max, negate=True).then_inc(sn_max, 1)

            def max_parts(b, gh):
                dve.wait_ge(sn_max, 16 * b.n + 8 * gh + 8)
                reached(dve, mt_full, 2 * (b.n - 1) + gh + 1)
                V.tensor_copy(neg_hl[gh][:, :, :, :, 0], neg_max[gh][:]).then_inc(neg_own, 1)
                dve.wait_ge(neg_own, 2 * b.n + gh + 1)
                V.tensor_tensor(neg_hl[gh][:, :, :, :, 1], neg_max[gh][:], f32(neg_hl[gh][:, :, :, :, 0]),
                                ALU.subtract).then_inc(neg_ready, 1)

            def norm_stats(b, src, stat, aggr, own, done):
                for c in range(2):
                    V.bn_stats(stat[:, c, :], src[:, c, :]).then_inc(own, 1)
                dve.wait_ge(own, 2 * b.n + 2)
                settle(dve)
                for c in range(2):
                    last = V.bn_aggr(aggr[:, c, :], stat[:, c, :])
                    last.then_inc(done, 1)

            def step(t):
                o, p, m = t + -1, t + 2, t + 1
                for s in range(SLOTS):
                    if s == 0 and t.exists():
                        max_parts(t, 1)
                    if m.exists():
                        if s == 8:
                            max_parts(m, 0)
                        max_unit(m, s)
                    if s == 2 and o.exists():
                        normalise(o)
                    if s == 3 and p.exists():
                        dve.wait_ge(in_x[p.par], 16 * (p.half + 1))
                        reached(dve, rstd1_ready, p.n)
                        norm_stats(p, x_sb[p.par], stat1, aggr1, stat_own1, var1)
                    if s == 5 and p.exists():
                        dve.wait_ge(rstd1_ready, p.n + 1)
                        reached(dve, t_full, p.n)
                        dve.wait_ge(var1, 2 * p.n + 2)
                        V.tensor_scalar(h1[:, 0, :], x_sb[p.par][:, 0, :], aggr1[:, 0, 0:1], rstd1[:, 0:1],
                                        ALU.subtract, ALU.mult)
                        V.tensor_scalar(h1[:, 1, :], x_sb[p.par][:, 1, :], aggr1[:, 1, 0:1], rstd1[:, 1:2],
                                        ALU.subtract, ALU.mult).then_inc(h1_ready, 1)
                    if s == 4 and o.exists():
                        residual(o)
                    if s == 7 and o.exists():
                        second_norm(o)
                    if s == 11 and o.exists():
                        route(o)
                    if s == 14 and o.exists():
                        place(o)

            def normalise(b):
                dve.wait_ge(pv_done, 16 * (b.n + 1))
                V.reciprocal(inv_sum[:], heads_ps[:, :, :, DK]).then_inc(inv_own, 1)
                dve.wait_ge(inv_own, b.n + 1)
                reached(dve, ht_full, b.n)
                V.tensor_tensor(heads[:].rearrange("p c (h d) -> p c h d", d=DK), heads_ps[:, :, :, 0:DK],
                                spread(inv_sum[:], 3, DK), ALU.mult).then_inc(heads_ready, 1)

            def residual(b):
                dve.wait_ge(wo_full, b.n + 1)
                dve.wait_ge(xb_ready, b.n + 1)
                reached(dve, kept_x[b.par], 16 * b.half)
                V.scalar_tensor_tensor(x1[b.par][:], misc[:, 0:2 * D].rearrange("p (c d) -> p c d", c=2), tanh_x,
                                       xb[b.par][:], ALU.mult, ALU.add).then_inc(x1_ready, 1)
                dve.wait_ge(x1_ready, b.n + 1)
                reached(dve, rstd2_ready, b.n)
                norm_stats(b, x1[b.par], stat2, aggr2, stat_own2, var2)

            def second_norm(b):
                dve.wait_ge(rstd2_ready, b.n + 1)
                reached(dve, scattered[b.par], 16 * 2 * K * b.half)
                dve.wait_ge(var2, 2 * b.n + 2)
                for c in range(2):
                    ins = V.tensor_scalar(h2_rows[b.par][:, c, :, 0:D], spread(x1[b.par][:, c, :], 1, K),
                                          aggr2[:, c, 0:1], rstd2[:, c:c + 1], ALU.subtract, ALU.mult)
                ins.then_inc(h2_ready, 1)

            def route(b):
                own = Chain(dve, route_own, ROUTE_OPS * b.n)
                sc = misc[:, 0:2 * (G + E)].rearrange("p (c n) -> p c n", c=2)
                dve.wait_ge(sc_full, b.n + 1)
                settle(dve)
                for c in range(2):
                    own.add(V.max(top_g[:, c, :], sc[:, c, 0:G]))
                own.wait()
                settle(dve)
                for c in range(2):
                    own.add(V.max_index(top_gi[:, c, :], top_g[:, c, :], sc[:, c, 0:G]))
                dve.wait_ge(norm_ready, b.n + 1)
                for c in range(2):
                    last = V.scalar_tensor_tensor(score[:, c, :], sc[:, c, G:G + E], norm2[:, 2, c:c + 1], bias_bc[:],
                                                  ALU.mult, ALU.add)
                    if c:
                        last.then_inc(sc_used, 1)
                own.wait()
                own.add(V.tensor_tensor(is_g[:], spread(top_gi[:, :, 0:K], 2, G),
                                        spread(spread(iota_i[:, 0:G], 1, 2), 3, K), ALU.is_equal))
                own.wait()
                own.add(V.tensor_reduce(mask_g[:], is_g[:], AX.X, ALU.max))
                own.wait()
                own.add(V.tensor_scalar(gap_g[:], mask_g[:], 1e9, -1e9, ALU.mult, ALU.add))
                dve.wait_ge(sc_used, b.n + 1)
                own.add(V.tensor_tensor(masked[:].rearrange("p c (g i) -> p c g i", g=G),
                                        score[:].rearrange("p c (g i) -> p c g i", g=G), spread(mask_g[:], 3, EG), ALU.mult))
                own.wait()
                own.add(V.tensor_tensor(masked[:].rearrange("p c (g i) -> p c g i", g=G),
                                        masked[:].rearrange("p c (g i) -> p c g i", g=G), spread(gap_g[:], 3, EG), ALU.add))
                own.wait()
                settle(dve)
                for c in range(2):
                    own.add(V.max(top_e[:, c, :], masked[:, c, :]))
                own.wait()
                settle(dve)
                for c in range(2):
                    own.add(V.max_index(top_ei[:, c, :], top_e[:, c, :], masked[:, c, :]))
                reached(dve, exp_ready, b.n)
                V.tensor_tensor(diff[:], top_e[:, :, 0:K], top_e[:, :, 0:1].to_broadcast([P, 2, K]),
                                ALU.subtract).then_inc(diff_ready, 1)
                own.wait()
                own.add(V.tensor_tensor(chosen[:], spread(top_ei[:, :, 0:K], 3, E),
                                        spread(spread(iota_i[:], 1, 2), 1, K).rearrange("p k c e -> p c k e"), ALU.is_equal))
                own.wait()
                reached(dve, cnt_full, b.n)
                reached(dve, earlier_ready, b.n)
                with nc.allow_low_precision(reason="zeros and ones"):
                    V.tensor_reduce(chosen_any[:], chosen[:].rearrange("p c k e -> p c e k"), AX.X, ALU.max).then_inc(chosen_ready, 1)
                assert own.n == ROUTE_OPS, own.n

            def place(b):
                own = Chain(dve, place_own, PLACE_OPS * b.n)
                dve.wait_ge(exp_ready, b.n + 1)
                own.add(V.tensor_reduce(gate_sum[:], expd[:], AX.X, ALU.add))
                own.wait()
                own.add(V.reciprocal(gate_inv[:], gate_sum[:]))
                own.wait()
                own.add(V.tensor_tensor(gate[:], expd[:], spread(gate_inv[:], 2, K), ALU.mult))
                dve.wait_ge(cnt_full, b.n + 1)
                dve.wait_ge(route_own, ROUTE_OPS * (b.n + 1))
                V.tensor_tensor(at_slot[:], chosen[:],
                                spread(misc[:, 0:2 * E].rearrange("p (c e) -> p c e", c=2), 2, K), ALU.mult).then_inc(cnt_used, 1)
                dve.wait_ge(cnt_used, b.n + 1)
                own.add(V.tensor_reduce(pos[:], at_slot[:], AX.X, ALU.add))
                own.wait()
                own.add(V.scalar_tensor_tensor(slot_f[:], top_ei[:, :, 0:K], float(CAP), pos[:], ALU.mult, ALU.add))
                own.add(V.tensor_scalar(keep[:], pos[:], float(CAP), None, ALU.is_lt))
                own.wait()
                own.add(V.scalar_tensor_tensor(slot_f[:], keep[:], -FAR, slot_f[:], ALU.mult, ALU.add))
                reached(dve, scattered[b.par], 16 * 2 * K * b.half)
                own.add(V.scalar_tensor_tensor(h2_rows[b.par][:, :, :, COL_GATE], gate[:], tanh_f, keep[:], ALU.mult, ALU.mult))
                own.wait()
                V.tensor_scalar(slot_i[b.par][:], slot_f[:], FAR, None, ALU.add).then_inc(slots_ready, 1)
                assert own.n == PLACE_OPS, own.n

            dve.wait_ge(pool_const, 1)
            V.memset(pick[:].bitcast(fp32), 0.0).then_inc(set_dve, 1)
            dve.wait_ge(in_w, 16 * 13)
            V.tensor_tensor(cent_sq[:], cents[:], cents[:], ALU.mult).then_inc(set_dve2, 1)
            dve.wait_ge(set_dve2, 1)
            V.tensor_reduce(cent_n[:, 0:1], cent_sq[:], AX.X, ALU.add).then_inc(set_dve, 1)
            dve.wait_ge(pool_const, 2)
            V.tensor_scalar(cents[:], cents[:], cent_n[:, 1:2], None, ALU.mult).then_inc(set_dve, 1)
            dve.wait_ge(set_dve, 1)
            cols = ident[:].rearrange("p (j g d) -> p g j d", j=4, d=DK)
            def put(kind, at, first, n):
                dst = pick[:, kind].rearrange("p g (j r) -> p g j r", j=4)[:, :, :, at:at + n]
                return V.tensor_copy(dst, cols[:, :, :, first:first + n])
            for kind in (0, 2):
                put(kind, 0, 0, 8)
            for kind in (1, 2):
                put(kind, 8, 0, 7)
                put(kind, 16, 7, 1)
            for kind in (0, 3):
                put(kind, 17, 0, 8)
            V.tensor_reduce(m_ones[:], ident[:, M_ROW:P:M_STEP], AX.X, ALU.add)
            V.memset(ones[:], 1.0)
            V.memset(neg_half[:], -0.5)
            V.memset(earlier[0][:], 0.0)
            V.tensor_copy(blank[:, :, COL_TOKEN].bitcast(u32), blank_i[:])
            for i in range(2):
                V.memset(v_ext[i][:, :, :, DK], 1.0)
                last = V.memset(h2_rows[i][:, :, :, D:ROW], 0.0)
            last.then_inc(consts, 1)
            dve.wait_ge(consts, 1)
            steps(dve, step)

            def shared_out(q):
                dve.wait_ge(sh_y, q + 1)
                if q >= 2:
                    dve.wait_ge(base_out[q % 2], 16 * (q // 2))
                V.scalar_tensor_tensor(base[q % 2][:], ps[:, 6 + q % 2, :].rearrange("p (t d) -> p t d", d=D), tanh_f,
                                       x1_all[:, 4 * q:4 * q + 4, :], ALU.mult, ALU.add).then_inc(sh_out, 1)

            for i in range(2):
                dve.wait_ge(kept_x[i], 16 * (B // 2))
            for q in range(N // 512):
                dve.wait_ge(sh_silu, q + 1)
                dve.wait_ge(sh_u, q + 1)
                reached(dve, sh_y, q - 1)
                V.tensor_tensor(hid[q % 2][:], silu_g[:], ps[:, 2:4, :], ALU.mult).then_inc(sh_hid, 1)
                if q:
                    shared_out(q - 1)
            shared_out(N // 512 - 1)

            def hidden(i, k):
                e = WR * i + k
                dve.wait_ge(silu_done, e + 1)
                dve.wait_ge(u_full, e + 1)
                reached(dve, y_full, e - 1)
                V.tensor_tensor(hid[k % 2][:, :, 0:CAP], silu_g[:, :, 0:CAP], ps[:, 2:4, 0:CAP], ALU.mult).then_inc(hid_ready, 1)

            def scale_out(i, k):
                e, r = WR * i + k, k % WR
                dve.wait_ge(y_full, e + 1)
                reached(dve, added, 48 * (e - 1))
                for tile, n in ((0, P), (1, P), (2, CAP - 2 * P)):
                    last = V.tensor_scalar(y_sb[k % 2][0:n, tile, :], ps[0:n, 6 + k % 2, tile * D:(tile + 1) * D],
                                           e_rows[r][0:n, tile, COL_GATE:COL_GATE + 1], None, ALU.mult)
                last.then_inc(y_out, 1)

            def expert(i, k):
                hidden(i, k)
                scale_out(i, k - 1)

            hidden(0, 0)
            expert(0, 1)
            expert_steps(dve, expert)
            for k in range(E - 2, E):
                expert(0, k)
            scale_out(0, E - 1)

        @block.gpsimd
        def _(pool):
            Q = nc.gpsimd

            def step(t):
                o, p, m = t + -1, t + 2, t + 1
                for s in range(SLOTS):
                    if s == 4 and p.exists():
                        own = Chain(pool, pool_ln1, p.n)
                        pool.wait_ge(var1, 2 * p.n + 2)
                        reached(pool, h1_ready, p.n)
                        settle(pool)
                        own.add(Q.tensor_scalar(rstd1[:], aggr1[:, :, 1], 1e-5, None, ALU.add))
                        own.wait()
                        Q.tensor_tensor(rstd1[:], rstd1[:], neg_half[:], ALU.pow).then_inc(rstd1_ready, 1)
                    if s == 5 and o.exists():
                        own = Chain(pool, pool_ln2, 4 * o.n)
                        pool.wait_ge(var2, 2 * o.n + 2)
                        reached(pool, h2_ready, o.n)
                        settle(pool)
                        own.add(Q.tensor_scalar(rstd2[:], aggr2[:, :, 1], 1e-5, None, ALU.add))
                        own.wait()
                        Q.tensor_tensor(rstd2[:], rstd2[:], neg_half[:], ALU.pow).then_inc(rstd2_ready, 1)
                        pool.wait_ge(rstd2_ready, o.n + 1)
                        own.add(Q.tensor_tensor(norm2[:, 0, :], aggr2[:, :, 1], rstd2[:], ALU.mult))
                        own.wait()
                        own.add(Q.tensor_tensor(norm2[:, 1, :], norm2[:, 0, :], rstd2[:], ALU.mult))
                        own.wait()
                        settle(pool)
                        own.add(Q.tensor_scalar(norm2[:, 0, :], norm2[:, 1, :], float(D), 1e-24, ALU.mult, ALU.max))
                        own.wait()
                        reached(pool, sc_used, o.n)
                        Q.tensor_tensor(norm2[:, 2, :], norm2[:, 0, :], neg_half[:], ALU.pow).then_inc(norm_ready, 1)
                        assert own.n == 4
                    if s == 6 and m.exists():
                        pool.wait_ge(in_x[m.par], 16 * (m.half + 1))
                        reached(pool, x1_ready, m.n - 1)
                        Q.tensor_tensor(xb[m.par][:], x_sb[m.par][:], spread(bo_bc[:], 1, 2), ALU.add).then_inc(xb_ready, 1)
                    if s == 10 and p.exists():
                        pool.wait_ge(qk_out, 2 * p.n + 2)
                        reached(pool, rows_full, 4 * p.n)
                        settle(pool)
                        Q.tensor_copy(qk_hi[:], qk[:]).then_inc(split_own, 1)
                        pool.wait_ge(split_own, p.n + 1)
                        Q.tensor_tensor(qk_lo[:], qk[:], f32(qk_hi[:]), ALU.subtract).then_inc(qk_split, 1)
                    if s == 12 and o.exists():
                        pool.wait_ge(chosen_ready, o.n + 1)
                        reached(pool, cnt_full, o.n)
                        old, new = earlier[o.par], earlier[1 - o.par]
                        with nc.allow_low_precision(reason="counts up to 16"):
                            Q.tensor_tensor(new[:], old[:], chosen_any[:, 0, :], ALU.add).then_inc(earlier_own, 1)
                            pool.wait_ge(earlier_own, o.n + 1)
                            Q.tensor_tensor(new[:], new[:], chosen_any[:, 1, :], ALU.add).then_inc(earlier_ready, 1)
                    if s == 15 and o.exists():
                        reached(pool, scattered[o.par], 16 * 2 * K * o.half)
                        settle(pool)
                        Q.tensor_copy(h2_rows[o.par][:, :, :, COL_TOKEN].bitcast(u32), spread(tok_f[:], 2, K)).then_inc(token_written, 1)
                        pool.wait_ge(token_written, o.n + 1)
                        settle(pool)
                        Q.tensor_scalar(tok_f[:], tok_f[:], float(S), None, ALU.add).then_inc(tok_next, 1)
                        pool.wait_ge(tok_next, o.n + 1)
                        pool.wait_ge(h2_ready, o.n + 1)
                        pool.wait_ge(slots_ready, o.n + 1)
                        settle(pool)
                        for c in range(2):
                            for k in range(K):
                                Q.indirect_dma_start(
                                    out=dispatch[:, :], out_offset=bass.IndirectOffsetOnAxis(ap=slot_i[o.par][:, c, k:k + 1], axis=0),
                                    in_=h2_rows[o.par][:, c, k, :], in_offset=None,
                                    bounds_check=E * CAP - 1, oob_is_err=False).then_inc(scattered[o.par], 16)

            own = Chain(pool, set_pool, 0)
            own.add(Q.memset(ident[:], 0.0))
            own.add(Q.memset(before[:], 0.0))
            own.add(Q.memset(blank[:], 0.0))
            own.add(Q.iota(iota_i[:], [[1, E]], base=0, channel_multiplier=0))
            own.add(Q.iota(tok_i[:], [[P, 2]], base=0, channel_multiplier=1))
            own.add(Q.iota(blank_i[:], [[P, 3]], base=N, channel_multiplier=1))
            own.wait()
            own.add(Q.affine_select(out=ident[:], in_=ident[:], compare_op=ALU.not_equal, fill=1.0, base=0,
                                    pattern=[[-1, P]], channel_multiplier=1))
            own.add(Q.affine_select(out=before[:], in_=before[:], compare_op=ALU.is_ge, fill=1.0, base=0,
                                    pattern=[[-1, P]], channel_multiplier=1))
            own.add(Q.tensor_copy(tok_f[:], tok_i[:]))
            own.wait()
            Q.tensor_copy(iota_f[:], iota_i[:]).then_inc(pool_const, 1)
            pool.wait_ge(set_dve, 2)
            own.add(Q.tensor_scalar(cent_n[:, 0:1], cent_n[:, 0:1], 1e-24, None, ALU.max))
            own.add(Q.memset(iden_r[:, 0:1], -0.5))
            own.wait()
            Q.tensor_tensor(cent_n[:, 1:2], cent_n[:, 0:1], iden_r[0:G + E, 0:1], ALU.pow).then_inc(pool_const, 1)
            pool.wait_ge(set_act, 1)
            own.add(Q.tensor_scalar(bo_bc[:], bo_bc[:], tanh_x, None, ALU.mult))
            own.wait()
            pool.wait_ge(consts, 1)
            pool.wait_ge(blanked, 48)
            steps(pool, step)

            def add_rows(i, k):
                e, r = WR * i + k, k % WR
                pool.wait_ge(y_out, e + 1)
                reached(pool, added, 48 * e)
                settle(pool)
                for tile, n in ((0, P), (1, P), (2, CAP - 2 * P)):
                    Q.indirect_dma_start(
                        out=sums[:, :], out_offset=bass.IndirectOffsetOnAxis(
                            ap=e_rows[r][0:n, tile, COL_TOKEN:COL_TOKEN + 1].bitcast(u32), axis=0),
                        in_=y_sb[k % 2][0:n, tile, :], in_offset=None, bounds_check=N + DUMP - 1,
                        compute_op=ALU.add).then_inc(added, 16)

            for q in range(N // 512):
                pool.wait_ge(sh_out, q + 1)
                pool.dma_start(sums[512 * q:512 * (q + 1), :].rearrange("(t p) d -> p t d", p=P),
                               base[q % 2][:]).then_inc(base_out[q % 2], 16)
            for i in range(2):
                pool.wait_ge(base_out[i], 16 * (N // 1024))
            add_rows(0, 0)
            add_rows(0, 1)
            expert_steps(pool, add_rows)
            for k in range(E - 2, E):
                add_rows(0, k)


_ARGS = ["x", "ctx_1024", "g_xattn", "g_ffn", "L0_xattn_Wq", "L0_xattn_bq", "L0_xattn_Wk", "L0_xattn_bk",
         "L0_xattn_Wv", "L0_xattn_bv", "L0_xattn_Wo", "L0_xattn_bo", "L0_ffn_group_centroids",
         "L0_ffn_expert_centroids", "L0_ffn_bias"]


def kernel(**inputs):
    import numpy as np
    import concourse.bacc as bacc
    from concourse.bass_utils import run_bass_kernel_spmd

    nc = bacc.Bacc("TRN2", target_bir_lowering=False, num_devices=1)
    arrays, args = {}, []

    def give(name, a):
        a = np.ascontiguousarray(a)
        arrays[name] = a
        args.append(nc.dram_tensor(name, a.shape, mybir.dt.from_np(a.dtype), kind="ExternalInput").ap())

    for name in _ARGS:
        a = np.asarray(inputs[name])
        give(name, a.T if name.split("_")[-1] in ("Wq", "Wk", "Wv", "Wo") else a)
    wg, wu, wd = (np.asarray(inputs[f"L0_ffn_{n}"]) for n in ("wg", "wu", "wd"))
    wd = wd.reshape(E, 2, P, D).transpose(0, 2, 1, 3)
    give("w_all", np.concatenate([wg.reshape(E, P, 2, P), wu.reshape(E, P, 2, P), wd], axis=2))
    for name in ("sg", "su", "sd"):
        give(name, inputs[f"L0_ffn_{name}"])
    args.append(nc.dram_tensor("out", (B, S, D), mybir.dt.float32, kind="ExternalOutput").ap())
    args.append(nc.dram_tensor("dispatch", (E * CAP, ROW), mybir.dt.float32, kind="Internal").ap())
    args.append(nc.dram_tensor("sums", (N + DUMP, D), mybir.dt.float32, kind="Internal").ap())
    gated_attention_and_experts(nc, *args)
    r = run_bass_kernel_spmd(nc, [arrays], core_ids=[0])
    return r.results[0]["out"]
```

```python
import concourse.bass as bass
from concourse import mybir
from contextlib import ExitStack

B, S, D = 8, 256, 128
H, DK = 16, 8
N = B * S
E, G, K = 32, 8, 4
F = 256
CAP = int(N / E * K * 1.25)
P = 128
EG = E // G
ROW = D + 4
COL_TOKEN, COL_GATE = D, D + 1
DUMP = CAP
NG = H // 4
M_ROW, M_STEP = 15, 16


class Batch:

    def __init__(self, i, k):
        self.half, self.par = i + k // 2, k % 2
        self.n = 2 * i + k
        self.i, self.k = i, k

    def __add__(self, d):
        return Batch(self.i, self.k + d)

    def exists(self):
        return not isinstance(self.n, int) or 0 <= self.n < B


class Chain:

    def __init__(self, eng, sem, start):
        self.eng, self.sem, self.start, self.n = eng, sem, start, 0

    def add(self, ins):
        ins.then_inc(self.sem, 1)
        self.n += 1

    def wait(self):
        self.eng.wait_ge(self.sem, self.start + self.n)


def reached(eng, sem, value):
    if not isinstance(value, int) or value > 0:
        eng.wait_ge(sem, value)


def gated_attention_and_experts(
    nc, x, ctx_in, g_xattn, g_ffn, wq_t, bq, wk_t, bk, wv_t, bv, wo_t, bo,
    group_centroids, expert_centroids, bias, w_all, sg, su, sd, out, dispatch, sums, loops=True,
):
    fp32, fp32r, bf16 = mybir.dt.float32, mybir.dt.float32r, mybir.dt.bfloat16
    u32, i32 = mybir.dt.uint32, mybir.dt.int32
    ALU, ACT, AX = mybir.AluOpType, mybir.ActivationFunctionType, mybir.AxisListType
    SCALE = float(DK) ** -0.5

    ctx = ExitStack()
    with ctx:
        def sb(name, shape, dt=fp32):
            return ctx.enter_context(nc.sbuf_tensor(name, shape, dt))

        def sem(name):
            return ctx.enter_context(nc.semaphore(name))

        def f32(ap):
            return ap.bitcast(fp32)

        def spread(ap, axis, n):
            ap = ap.unsqueeze(axis)
            shape = list(ap.shape)
            shape[axis] = n
            return ap.to_broadcast(shape)

        wq_sb, wk_sb, wv_sb, wo_sb = (sb(n, [P, D]) for n in ("wq_sb", "wk_sb", "wv_sb", "wo_sb"))
        bq_sb, bk_sb, bv_sb = (sb(n, [P, 1]) for n in ("bq_sb", "bk_sb", "bv_sb"))
        bo_bc, bias_bc = sb("bo_bc", [P, D]), sb("bias_bc", [P, E])
        gates_in, gates = sb("gates_in", [P, 2]), sb("gates", [P, 2])
        tanh_x, tanh_f = gates[:, 0:1], gates[:, 1:2]
        ident = sb("ident", [P, P])
        m_ones = sb("m_ones", [P, 1])
        pick = sb("pick", [P, 4, NG, P], fp32r)
        before = sb("before", [P, P], bf16)
        ones = sb("ones", [P, P], bf16)
        iota_i = sb("iota_i", [P, E], i32)
        tok_i, tok_f = sb("tok_i", [P, 2], i32), sb("tok_f", [P, 2])
        neg_half = sb("neg_half", [P, 2])
        cents, cent_sq, cent_n = sb("cents", [G + E, D]), sb("cent_sq", [G + E, D]), sb("cent_n", [G + E, 2])
        cent_t = sb("cent_t", [P, G + E])
        blank, blank_i = sb("blank", [P, 3, ROW]), sb("blank_i", [P, 3], i32)

        x_sb = [sb(f"x_sb{i}", [P, 2, D]) for i in range(2)]
        c_sb = [sb(f"c_sb{i}", [P, 2, D]) for i in range(2)]
        xb = [sb(f"xb{i}", [P, 2, D]) for i in range(2)]
        stat1, aggr1, rstd1 = sb("stat1", [P, 2, 6]), sb("aggr1", [P, 2, 2]), sb("rstd1", [P, 2])
        h1 = sb("h1", [P, 2, D])
        hc_t = sb("hc_t", [P, 4, P])
        qk = sb("qk", [P, 2, S])
        qk_hi, qk_lo = sb("qk_hi", [P, 2, S], fp32r), sb("qk_lo", [P, 2, S], fp32r)
        q_rows = [sb(f"q_rows{i}", [P, 2, S], fp32r) for i in range(4)]
        k_stage = [sb(f"k_stage{i}", [P, 2, S], fp32r) for i in range(2)]
        k_rows = [sb(f"k_rows{i}", [P, 4, 2, S], fp32r) for i in range(4)]
        v_ext = [sb(f"v_ext{i}", [P, 2, H, 32]) for i in range(2)]
        neg_max = [sb(f"neg_max{i}", [P, 2, 2, 4]) for i in range(2)]
        neg_hl = [sb(f"neg_hl{i}", [P, 2, 2, 4, 2], fp32r) for i in range(2)]
        max_t = [sb(f"max_t{i}", [16, S], fp32r) for i in range(2)]
        probs = [sb(f"probs{i}", [P, 2, 2, 2, 2, S]) for i in range(2)]
        heads_raw = [sb(f"heads_raw{i}", [P, 2, S]) for i in range(2)]
        inv_sum = sb("inv_sum", [P, 4, 4])
        heads = sb("heads", [P, 2, D])
        heads_t = sb("heads_t", [P, 2, P])

        x1 = [sb(f"x1_{i}", [P, 2, D]) for i in range(2)]
        stat2, aggr2, rstd2 = sb("stat2", [P, 2, 6]), sb("aggr2", [P, 2, 2]), sb("rstd2", [P, 2])
        norm2 = sb("norm2", [P, 3, 2])
        h2_rows = [sb(f"h2_rows{i}", [P, 2, K, ROW]) for i in range(2)]
        h2_t = [sb(f"h2_t{i}", [P, 2, P]) for i in range(2)]
        top_g, top_gi = sb("top_g", [P, 2, 8]), sb("top_gi", [P, 2, 8], u32)
        is_g, mask_g, gap_g = sb("is_g", [P, 2, G, K]), sb("mask_g", [P, 2, G]), sb("gap_g", [P, 2, G])
        score, masked = sb("score", [P, 2, E]), sb("masked", [P, 2, E])
        top_e, top_ei = sb("top_e", [P, 2, 8]), sb("top_ei", [P, 2, 8], u32)
        chosen = sb("chosen", [P, 2, K, E])
        chosen_any = sb("chosen_any", [P, 2, E], bf16)
        earlier = [sb(f"earlier{i}", [P, E], bf16) for i in range(2)]
        diff, expd, gate = sb("diff", [P, 2, K]), sb("expd", [P, 2, K]), sb("gate", [P, 2, K])
        gate_sum, gate_inv = sb("gate_sum", [P, 2]), sb("gate_inv", [P, 2])
        at_slot, pos, slot_f = sb("at_slot", [P, 2, K, E]), sb("pos", [P, 2, K]), sb("slot_f", [P, 2, K])
        keep = sb("keep", [P, 2, K])
        slot_i = [sb(f"slot_i{i}", [P, 2, K], u32) for i in range(2)]
        x1_all, h2t_all = sb("x1_all", [P, N // P, D]), sb("h2t_all", [P, N])

        WR = 4
        sg_sb, su_sb, sd_sb = sb("sg_sb", [P, F]), sb("su_sb", [P, F]), sb("sd_sb", [P, 2, D])
        w_sb = [sb(f"w_sb{i}", [P, 6, P]) for i in range(WR)]
        e_rows = [sb(f"e_rows{i}", [P, 3, ROW]) for i in range(WR)]
        e_t = [sb(f"e_t{i}", [P, CAP]) for i in range(2)]
        silu_g = sb("silu_g", [P, 2, 512])
        hid = [sb(f"hid{i}", [P, 2, 512]) for i in range(2)]
        y_sb = [sb(f"y_sb{i}", [P, 3, D]) for i in range(2)]
        base = [sb(f"base{i}", [P, 4, D]) for i in range(2)]

        ps = ctx.enter_context(nc.psum_tensor("ps", [P, 8, 512], fp32))
        score_t = [ps[:, i, :] for i in range(2)]
        score_n = [ps[:, 2 + i, :] for i in range(2)]
        heads_ps = ps[:, 7, :]

        in_x, in_c = [sem(f"in_x{i}") for i in range(2)], [sem(f"in_c{i}") for i in range(2)]
        in_w, in_route, in_shared = sem("in_w"), sem("in_route"), sem("in_shared")
        set_pool, set_dve, set_act, set_pe = sem("set_pool"), sem("set_dve"), sem("set_act"), sem("set_pe")
        pool_const, zeroed = sem("pool_const"), sem("zeroed")
        consts = sem("consts")
        blanked = sem("blanked")
        var1, rstd1_ready, h1_ready, xb_ready = sem("var1"), sem("rstd1_ready"), sem("h1_ready"), sem("xb_ready")
        t_full, t_out = sem("t_full"), sem("t_out")
        qk_full, qk_out = sem("qk_full"), sem("qk_out")
        qk_split, split_own = sem("qk_split"), sem("split_own")
        v_full, v_out = sem("v_full"), sem("v_out")
        rows_full, rows_out = sem("rows_full"), sem("rows_out")
        sn_full, sn_max = sem("sn_full"), sem("sn_max")
        neg_own, neg_ready = sem("neg_own"), sem("neg_ready")
        mt_full, mt_out = sem("mt_full"), sem("mt_out")
        k_landed = [sem(f"k_landed{i}") for i in range(2)]
        k_blank = sem("k_blank")
        m_landed = [sem(f"m_landed{i}") for i in range(2)]
        st_full, exp_done = sem("st_full"), sem("exp_done")
        pv_done, raw_out = sem("pv_done"), sem("raw_out")
        hn_full, inv_own = sem("hn_full"), sem("inv_own")
        heads_ready = sem("heads_ready")
        ht_full, ht_out = sem("ht_full"), sem("ht_out")
        wo_full, x1_ready = sem("wo_full"), sem("x1_ready")
        ln_own, var2, rstd2_ready, h2_ready = sem("ln_own"), sem("var2"), sem("rstd2_ready"), sem("h2_ready")
        pool_ln1, pool_ln2 = sem("pool_ln1"), sem("pool_ln2")
        h2t_full, h2t_out = sem("h2t_full"), sem("h2t_out")
        kept_x, kept_h = [sem(f"kept_x{i}") for i in range(2)], [sem(f"kept_h{i}") for i in range(2)]
        x1_free, h2t_free, rows_free = sem("x1_free"), sem("h2t_free"), sem("rows_free")
        sc_full, sc_used, route_own = sem("sc_full"), sem("sc_used"), sem("route_own")
        chosen_ready, diff_ready, exp_ready = sem("chosen_ready"), sem("diff_ready"), sem("exp_ready")
        earlier_own, earlier_ready = sem("earlier_own"), sem("earlier_ready")
        cnt_full, cnt_used, place_own, slots_ready = sem("cnt_full"), sem("cnt_used"), sem("place_own"), sem("slots_ready")
        token_written, tok_next = sem("token_written"), sem("tok_next")
        scattered = [sem(f"scattered{i}") for i in range(2)]
        sh_g, sh_u, sh_silu, sh_hid, sh_y, sh_out = (sem(n) for n in ("sh_g", "sh_u", "sh_silu", "sh_hid", "sh_y", "sh_out"))
        base_out = [sem(f"base_out{i}") for i in range(2)]
        w_in, rows_in = [sem(f"w_in{i}") for i in range(WR)], [sem(f"rows_in{i}") for i in range(WR)]
        et_full, et_out, g_full, u_full = sem("et_full"), sem("et_out"), sem("g_full"), sem("u_full")
        silu_done, hid_ready, y_full, y_out = sem("silu_done"), sem("hid_ready"), sem("y_full"), sem("y_out")
        added, written = sem("added"), sem("written")
        passed = sem("passed")
        stat_own1, stat_own2, norm_ready, set_dve2 = sem("stat_own1"), sem("stat_own2"), sem("norm_ready"), sem("set_dve2")
        ROUTE_OPS, PLACE_OPS = 14, 8
        FAR = 1048576.0

        SLOTS = 16
        FIRST, LAST = -2, B + 1
        LOOP_FROM, LOOP_PAIRS = 2, 2

        ROUNDS = [(0, "score", -2), (2, "k1", 1), (3, "max1", 0), (3, "q1", 1), (4, "v", 1),
                  (5, "t", 2), (5, "count", -2), (6, "norm1", -1), (7, "qk", 2), (8, "heads", -1),
                  (10, "wo", -1), (11, "max0", 1), (12, "k0", 2), (13, "q0", 2), (14, "norm0", 0),
                  (14, "h2", -1)]
        BANKS = 3
        bank = {name: ps[:, 4 + at % BANKS, :] for at, (_, name, _) in enumerate(ROUNDS)}
        TIMES_VALUES = [(1, 1, 1, -1), (2, 1, 2, -1), (3, 1, 3, -1), (6, 0, 0, 0), (9, 0, 1, 0),
                        (10, 0, 2, 0), (11, 0, 3, 0), (14, 1, 0, 0)]
        SCATTERS = {8: (0, 1), 12: (2, 3, 4), 14: (5, 6, 7)}

        def emptied(name, b):
            n = b.n
            return {"max0": (mt_out, 2 * n + 1), "max1": (mt_out, 2 * n + 2), "v": (v_out, n + 1),
                    "heads": (ht_out, n + 1), "wo": (x1_ready, n + 1), "t": (t_out, n + 1),
                    "k0": (rows_out, 4 * n + 1), "q0": (rows_out, 4 * n + 2),
                    "k1": (rows_out, 4 * n + 3), "q1": (rows_out, 4 * n + 4),
                    "norm0": (heads_ready, 2 * n + 1), "norm1": (heads_ready, 2 * n + 2),
                    "h2": (h2t_out, n + 1), "qk": (qk_out, 2 * n + 2), "score": (sc_used, n + 1),
                    "count": (cnt_used, n + 1)}[name]

        def round_before(t, at):
            mine = at % BANKS
            while True:
                at -= 1
                if at < 0:
                    at, t = len(ROUNDS) - 1, t + -1
                _, name, off = ROUNDS[at]
                if isinstance(t.n, int) and t.n < FIRST:
                    return None
                if at % BANKS == mine and (t + off).exists():
                    return emptied(name, t + off)

        def settle(eng):
            eng.sem_inc(passed, 1)

        def steps(eng, step, after_first=None):
            t = FIRST
            while t <= LAST:
                if t == FIRST + 1 and after_first:
                    after_first()
                if t == LOOP_FROM and loops:
                    with eng.Fori(0, LOOP_PAIRS) as i:
                        for k in range(2):
                            step(Batch(i, LOOP_FROM + k))
                    t += 2 * LOOP_PAIRS
                else:
                    step(Batch(0, t))
                    t += 1

        def expert_steps(eng, expert):
            if loops:
                with eng.Fori(0, E // WR - 1) as i:
                    for k in range(3, WR + 3):
                        expert(i, k)
            else:
                for i in range(E // WR - 1):
                    for k in range(3, WR + 3):
                        expert(i, k)

        block = ctx.enter_context(nc.Block())

        @block.sync
        def _(sp):
            def load(b):
                if b.exists():
                    reached(sp, h1_ready, b.n - 1)
                    reached(sp, xb_ready, b.n - 1)
                    sp.dma_start(x_sb[b.par][:], x[b.n].rearrange("(c p) d -> p c d", p=P)).then_inc(in_x[b.par], 16)
                    reached(sp, t_full, b.n - 1)
                    sp.dma_start(c_sb[b.par][:], ctx_in[b.n].rearrange("(c p) d -> p c d", p=P)).then_inc(in_c[b.par], 16)

            def max_rows(b, gh):
                if b.exists():
                    reached(sp, mt_out, 2 * b.n + gh + 1)
                    for g in range(2):
                        dst = q_rows[2 * b.par + gh][M_ROW:P:M_STEP, g, :]
                        sp.dma_start(f32(dst), f32(max_t[gh][8 * g:8 * g + 8, :])).then_inc(m_landed[gh], 16)

            def key_rows(b, gh):
                if b.exists():
                    reached(sp, st_full, 16 * (b.n - 2) + 8 * gh + 8)
                    settle(sp)
                    sp.wait_ge(rows_out, 4 * b.n + 2 * gh + 1)
                    for j in range(4):
                        rows = slice(32 * j, 32 * j + 32)
                        sp.dma_start(f32(k_rows[2 * b.par + gh][rows, j, :, :]),
                                     f32(k_stage[gh][rows, :, :])).then_inc(k_landed[gh], 16)

            def blanks_and_shared():
                sp.wait_ge(consts, 2)
                rows = dispatch.rearrange("(e r) w -> e r w", r=CAP)
                sp.dma_start(rows[:, 0:2 * P, :].rearrange("e (p c) w -> p e (c w)", c=2),
                             spread(blank[:, 0:2, :].rearrange("p c w -> p (c w)"), 1, E)).then_inc(blanked, 16)
                sp.dma_start(rows[:, 2 * P:CAP, :].rearrange("e p w -> p e w"),
                             spread(blank[0:CAP - 2 * P, 2, :], 1, E)).then_inc(blanked, 16)
                sp.dma_start(sums[N:N + DUMP, :].rearrange("(p r) d -> p r d", p=64),
                             spread(blank[0:64, 0, 0:D], 1, DUMP // 64)).then_inc(blanked, 16)
                sp.dma_start(sg_sb[:], sg).then_inc(in_shared, 16)
                sp.dma_start(su_sb[:], su).then_inc(in_shared, 16)
                sp.dma_start(sd_sb[:], sd.rearrange("(c p) d -> p c d", p=P)).then_inc(in_shared, 16)

            def step(t):
                for s in range(SLOTS):
                    if s == 0 and not (isinstance(t.n, int) and t.n + 2 < 2):
                        load(t + 2)
                    if s == 3:
                        key_rows(t + 1, 1)
                        max_rows(t, 1)
                    if s == 8 and (t + -2).exists():
                        b = t + -2
                        sp.wait_ge(kept_x[b.par], 16 * (b.half + 1))
                        sp.sem_inc(x1_free, 1)
                        sp.wait_ge(kept_h[b.par], 16 * (b.half + 1))
                        sp.sem_inc(h2t_free, 1)
                    if s == 11:
                        max_rows(t + 1, 0)
                    if s == 12:
                        key_rows(t + 2, 0)
                    if s == 13 and (t + -1).exists():
                        b = t + -1
                        reached(sp, x1_ready, b.n + 1)
                        sp.dma_start(x1_all[:, bass.ds(2 * b.n, 2), :], x1[b.par][:]).then_inc(kept_x[b.par], 16)
                    if s == 14 and (t + -1).exists():
                        b = t + -1
                        reached(sp, h2t_out, b.n + 1)
                        sp.dma_start(h2t_all[:, bass.ds(S * b.n, S)],
                                     h2_t[b.par][:].rearrange("p c t -> p (c t)")).then_inc(kept_h[b.par], 16)

            load(Batch(0, 0))
            load(Batch(0, 1))
            for dst, src in ((wq_sb, wq_t), (wk_sb, wk_t), (bq_sb, bq.rearrange("(p o) -> p o", o=1)),
                             (bk_sb, bk.rearrange("(p o) -> p o", o=1)), (wv_sb, wv_t), (wo_sb, wo_t),
                             (bv_sb, bv.rearrange("(p o) -> p o", o=1))):
                sp.dma_start(dst[:], src).then_inc(in_w, 16)
            for dst, src in ((gates_in[:, 0:1], g_xattn.partition_broadcast(P)),
                             (gates_in[:, 1:2], g_ffn.partition_broadcast(P)),
                             (bo_bc, bo.partition_broadcast(P)), (bias_bc, bias.partition_broadcast(P)),
                             (cents[0:G, :], group_centroids), (cents[G:G + E, :], expert_centroids)):
                sp.dma_start(dst[:], src).then_inc(in_route, 16)
            sp.sem_inc(x1_free, 1)
            sp.sem_inc(h2t_free, 1)
            sp.wait_ge(k_blank, 1)
            steps(sp, step, blanks_and_shared)

            def load_expert(i, r, ahead):
                e = WR * i + r
                if ahead:
                    sp.wait_ge(y_full, e - WR + 1)
                sp.dma_start(w_sb[r][:], w_all[e]).then_inc(w_in[r], 16)
                if ahead:
                    sp.wait_ge(added, 48 * (e - WR + 1))
                rows_of(sp, e, r)

            def rows_of(sp, e, r):
                rows_e = dispatch[bass.ds(e * CAP, CAP), :]
                sp.dma_start(e_rows[r][:, 0:2, :], rows_e[0:2 * P, :].rearrange("(p c) w -> p c w", c=2)).then_inc(rows_in[r], 16)
                sp.dma_start(e_rows[r][0:CAP - 2 * P, 2, :], rows_e[2 * P:CAP, :]).then_inc(rows_in[r], 16)

            for r in range(WR):
                sp.dma_start(w_sb[r][:], w_all[r]).then_inc(w_in[r], 16)
            for i in range(2):
                sp.wait_ge(scattered[i], 16 * 2 * K * (B // 2))
            for r in range(WR):
                rows_of(sp, r, r)
            if loops:
                with sp.Fori(1, E // WR) as i:
                    for r in range(WR):
                        load_expert(i, r, True)
            else:
                for i in range(1, E // WR):
                    for r in range(WR):
                        load_expert(i, r, True)
            sp.wait_ge(added, 48 * E)
            sp.dma_start(out.rearrange("b s d -> (b s) d"), sums[0:N, :]).then_inc(written, 16)
            sp.wait_ge(written, 16)

        @block.tensor
        def _(pe):
            def mm(dst, lhs_t, rhs, start=True, stop=True):
                return nc.tensor.matmul(dst, lhs_t, rhs, start=start, stop=stop)

            def rows_round(kind, gh):
                misc = bank["qk"[kind] + str(gh)]
                for g2 in range(2):
                    g = 2 * gh + g2
                    dst = misc[:, g2 * S:(g2 + 1) * S]
                    mm(dst, pick[:, 2 * kind, g, :], qk_hi[:, kind, :], True, False)
                    last = mm(dst, pick[:, 2 * kind + 1, g, :], qk_lo[:, kind, :], False, True)
                last.then_inc(rows_full, 1)

            def max_round(b, gh):
                misc = bank["max" + str(gh)]
                reached(pe, neg_ready, 2 * b.n + gh + 1)
                for qc in range(2):
                    last = nc.tensor.transpose(misc[0:16, qc * P:(qc + 1) * P],
                                               f32(neg_hl[gh][:, qc].rearrange("p g j t -> p (g j t)")), ident[:])
                last.then_inc(mt_full, 1)

            def do_round(name, b):
                misc = bank[name]
                if name in ("max0", "max1"):
                    max_round(b, int(name[-1]))
                elif name == "t":
                    reached(pe, h1_ready, b.n + 1)
                    pe.wait_ge(in_c[b.par], 16 * (b.half + 1))
                    for c in range(4):
                        src = h1[:, c, :] if c < 2 else c_sb[b.par][:, c - 2, :]
                        last = nc.tensor.transpose(misc[:, c * P:(c + 1) * P], src, ident[:])
                    last.then_inc(t_full, 1)
                elif name == "qk":
                    reached(pe, t_out, b.n + 1)
                    mm(misc[:, 0:S], wq_sb[:], hc_t[:, 0:2, :].rearrange("p c t -> p (c t)"))
                    mm(misc[:, S:2 * S], wk_sb[:], hc_t[:, 2:4, :].rearrange("p c t -> p (c t)")).then_inc(qk_full, 1)
                elif name == "v":
                    for c in range(2):
                        last = mm(misc[:, c * P:(c + 1) * P], hc_t[:, 2 + c, :], wv_sb[:])
                    last.then_inc(v_full, 1)
                elif name in ("q0", "q1", "k0", "k1"):
                    reached(pe, qk_split, b.n + 1)
                    rows_round("qk".index(name[0]), int(name[1]))
                elif name in ("norm0", "norm1"):
                    gh = int(name[-1])
                    reached(pe, raw_out, 2 * b.n + gh + 1)
                    for g2 in range(2):
                        for qc in range(2):
                            at = 2 * g2 + qc
                            last = nc.tensor.transpose(misc[:, at * P:(at + 1) * P],
                                                       heads_raw[gh][:, g2, qc * P:(qc + 1) * P], ident[:])
                    last.then_inc(hn_full, 1)
                elif name == "heads":
                    reached(pe, heads_ready, 2 * b.n + 2)
                    for c in range(2):
                        last = nc.tensor.transpose(misc[:, c * P:(c + 1) * P], heads[:, c, :], ident[:])
                    last.then_inc(ht_full, 1)
                elif name == "wo":
                    reached(pe, ht_out, b.n + 1)
                    for c in range(2):
                        last = mm(misc[:, c * P:(c + 1) * P], heads_t[:, c, :], wo_sb[:])
                    last.then_inc(wo_full, 1)
                elif name == "h2":
                    reached(pe, h2_ready, b.n + 1)
                    for c in range(2):
                        last = nc.tensor.transpose(misc[:, c * P:(c + 1) * P], h2_rows[b.par][:, c, 0, 0:D], ident[:])
                    last.then_inc(h2t_full, 1)
                elif name == "score":
                    reached(pe, h2t_out, b.n + 1)
                    for c in range(2):
                        last = mm(misc[:, c * (G + E):(c + 1) * (G + E)], h2_t[b.par][:, c, :], cent_t[:])
                    last.then_inc(sc_full, 1)
                elif name == "count":
                    reached(pe, chosen_ready, b.n + 1)
                    pe.wait_ge(earlier_ready, b.n + 1)
                    mm(misc[:, 0:E], before[:], chosen_any[:, 0, :], True, False)
                    mm(misc[:, 0:E], ones[:], earlier[b.par][:], False, True)
                    mm(misc[:, E:2 * E], before[:], chosen_any[:, 1, :], True, False)
                    mm(misc[:, E:2 * E], ones[:], chosen_any[:, 0, :], False, False)
                    mm(misc[:, E:2 * E], ones[:], earlier[b.par][:], False, True).then_inc(cnt_full, 1)

            def scores_for_max(b, s):
                gh, g2, jp, qc = s // 8, (s % 8) // 4, (s % 4) // 2, s % 2
                q, k = q_rows[2 * b.par + gh], k_rows[2 * b.par + gh]
                if s % 8 == 0:
                    reached(pe, rows_out, 4 * b.n + 2 * gh + 2)
                    reached(pe, k_landed[gh], 64 * (b.n + 1))
                reached(pe, sn_max, 16 * b.n + s - 1)
                mm(score_n[s % 2], q[:, g2, qc * P:(qc + 1) * P], k[:, 2 * jp:2 * jp + 2, g2, :]).then_inc(sn_full, 1)

            def scores_for_exp(b, u):
                gh, kc, j = u // 8, (u % 8) // 4, u % 4
                q, k = q_rows[2 * b.par + gh], k_rows[2 * b.par + gh]
                if u % 8 == 0:
                    reached(pe, m_landed[gh], 32 * (b.n + 1))
                reached(pe, exp_done, 16 * b.n + u - 1)
                for g2 in range(2):
                    last = mm(score_t[u % 2][:, g2 * S:(g2 + 1) * S], k[:, j, g2, kc * P:(kc + 1) * P], q[:, g2, :])
                last.then_inc(st_full, 1)

            def times_values(b, gh, piece):
                g2, kc = piece // 2, piece % 2
                if piece == 0:
                    reached(pe, v_out, b.n + 1)
                    reached(pe, raw_out, 2 * b.n + gh)
                if piece < 2:
                    reached(pe, exp_done, 16 * b.n + 8 * gh + 4 * kc + 4)
                for j in range(4):
                    last = mm(heads_ps[32 * j:32 * j + 32, g2 * S:(g2 + 1) * S], v_ext[b.par][:, kc, 4 * j + 2 * gh + g2, :],
                              probs[gh][:, kc, j // 2, j % 2, g2, :], kc == 0, kc == 1)
                last.then_inc(pv_done, 1)

            def step(t):
                for s in range(SLOTS):
                    if (t + 1).exists():
                        scores_for_max(t + 1, s)
                    if t.exists():
                        scores_for_exp(t, s)
                    for slot, gh, piece, off in TIMES_VALUES:
                        if slot == s and (t + off).exists():
                            times_values(t + off, gh, piece)
                    for at, (slot, name, off) in enumerate(ROUNDS):
                        if slot == s and (t + off).exists():
                            before_it = round_before(t, at)
                            if before_it:
                                reached(pe, *before_it)
                            do_round(name, t + off)

            def centroids():
                pe.wait_ge(set_dve, 3)
                nc.tensor.transpose(score_n[0][:, 0:G + E], cents[:], ident[0:G + E, 0:G + E]).then_inc(set_pe, 1)
                pe.wait_ge(set_act, 2)
                pe.wait_ge(consts, 2)

            pe.wait_ge(set_pool, 1)
            pe.wait_ge(in_w, 16 * 7)
            pe.wait_ge(consts, 1)
            steps(pe, step, centroids)

            g_ps, u_ps = ps[:, 0:2, :], ps[:, 2:4, :]
            y_ps = [ps[:, 6 + i, :] for i in range(2)]
            x_ps = [ps[:, 4 + i, :] for i in range(2)]
            pe.wait_ge(in_shared, 48)
            pe.wait_ge(exp_done, 16 * B)
            pe.wait_ge(sn_max, 16 * B)
            pe.wait_ge(cnt_used, B)
            for i in range(2):
                pe.wait_ge(kept_h[i], 16 * (B // 2))
            NQ = N // 512

            def shared_down(q):
                pe.wait_ge(sh_hid, q + 1)
                reached(pe, sh_out, q - 1)
                for tile in range(4):
                    for c in range(2):
                        last = mm(y_ps[q % 2][:, tile * D:(tile + 1) * D], hid[q % 2][:, c, tile * P:(tile + 1) * P],
                                  sd_sb[:, c, :], c == 0, c == 1)
                last.then_inc(sh_y, 1)

            for q in range(NQ):
                reached(pe, sh_silu, q)
                for c in range(2):
                    last = mm(g_ps[:, c, :], sg_sb[:, c * P:(c + 1) * P], h2t_all[:, q * 512:(q + 1) * 512])
                last.then_inc(sh_g, 1)
                reached(pe, sh_hid, q)
                for c in range(2):
                    last = mm(u_ps[:, c, :], su_sb[:, c * P:(c + 1) * P], h2t_all[:, q * 512:(q + 1) * 512])
                last.then_inc(sh_u, 1)
                if q:
                    shared_down(q - 1)
            shared_down(NQ - 1)
            pe.wait_ge(sh_out, NQ)

            def transposes(i, k):
                e, r = WR * i + k, k % WR
                pe.wait_ge(rows_in[r], 32 * (i + k // WR + 1))
                reached(pe, et_out, e - 1)
                for c, n in ((0, P), (1, P), (2, CAP - 2 * P)):
                    last = nc.tensor.transpose(x_ps[k % 2][:, c * P:c * P + n], e_rows[r][0:n, c, 0:D], ident[0:n, 0:n])
                last.then_inc(et_full, 1)

            def gate_up(i, k):
                e, r = WR * i + k, k % WR
                pe.wait_ge(w_in[r], 16 * (i + k // WR + 1))
                pe.wait_ge(et_out, e + 1)
                reached(pe, silu_done, e)
                for c in range(2):
                    last = mm(g_ps[:, c, 0:CAP], w_sb[r][:, c, :], e_t[k % 2][:])
                last.then_inc(g_full, 1)
                reached(pe, hid_ready, e)
                for c in range(2):
                    last = mm(u_ps[:, c, 0:CAP], w_sb[r][:, 2 + c, :], e_t[k % 2][:])
                last.then_inc(u_full, 1)

            def down(i, k):
                e, r = WR * i + k, k % WR
                pe.wait_ge(hid_ready, e + 1)
                reached(pe, y_out, e - 1)
                for tile, n in ((0, P), (1, P), (2, CAP - 2 * P)):
                    for c in range(2):
                        last = mm(y_ps[k % 2][0:n, tile * D:(tile + 1) * D], hid[k % 2][:, c, tile * P:tile * P + n],
                                  w_sb[r][:, 4 + c, :], c == 0, c == 1)
                last.then_inc(y_full, 1)

            def expert(i, k):
                gate_up(i, k)
                transposes(i, k + 1)
                down(i, k - 1)

            transposes(0, 0)
            gate_up(0, 0)
            transposes(0, 1)
            expert(0, 1)
            expert(0, 2)
            expert_steps(pe, expert)
            gate_up(0, E - 1)
            down(0, E - 2)
            down(0, E - 1)

        @block.scalar
        def _(act):
            def copy_out(dst, src, full, count, done, bias=None):
                reached(act, full, count)
                if bias is None:
                    nc.scalar.activation(dst, src, ACT.Copy).then_inc(done, 1)
                else:
                    nc.scalar.activation(dst, src, ACT.Identity, bias=bias).then_inc(done, 1)

            def do_round(name, b):
                misc = bank.get(name)
                n = b.n
                if name in ("max0", "max1"):
                    gh = int(name[-1])
                    reached(act, m_landed[gh], 32 * n)
                    copy_out(max_t[gh][:], misc[0:16, 0:S], mt_full, 2 * n + gh + 1, mt_out)
                elif name == "v":
                    reached(act, pv_done, 8 * (n - 1))
                    copy_out(v_ext[b.par][:, :, :, 0:DK],
                             misc[:, 0:2 * D].rearrange("p (c h d) -> p c h d", c=2, d=DK), v_full, n + 1, v_out)
                elif name == "t":
                    copy_out(hc_t[:].rearrange("p c t -> p (c t)"), misc, t_full, n + 1, t_out)
                elif name == "qk":
                    reached(act, qk_split, n)
                    copy_out(qk[:, 0, :], misc[:, 0:S], qk_full, n + 1, qk_out, bias=bq_sb[:])
                    copy_out(qk[:, 1, :], misc[:, S:2 * S], qk_full, n + 1, qk_out, bias=bk_sb[:])
                elif name in ("q0", "q1", "k0", "k1"):
                    gh, is_q = int(name[1]), name[0] == "q"
                    if is_q:
                        reached(act, st_full, 16 * (n - 2) + 8 * gh + 8)
                    else:
                        reached(act, k_landed[gh], 64 * n)
                    dst = (q_rows[2 * b.par + gh] if is_q else k_stage[gh])[:].rearrange("p g t -> p (g t)")
                    copy_out(dst, misc, rows_full, 4 * n + 2 * gh + is_q + 1, rows_out, bias=None if is_q else m_ones[:])
                elif name == "heads":
                    copy_out(heads_t[:].rearrange("p c t -> p (c t)"), misc[:, 0:S], ht_full, n + 1, ht_out, bias=bv_sb[:])
                elif name == "h2":
                    reached(act, h2t_free, n)
                    copy_out(h2_t[b.par][:].rearrange("p c t -> p (c t)"), misc[:, 0:S], h2t_full, n + 1, h2t_out)

            def raw_copy(b, gh):
                reached(act, hn_full, 2 * (b.n - 1) + gh + 1)
                copy_out(heads_raw[gh][:].rearrange("p g t -> p (g t)"), heads_ps, pv_done, 8 * b.n + 4 * gh + 4, raw_out)

            def exp_unit(b, u):
                gh, kc, j = u // 8, (u % 8) // 4, u % 4
                reached(act, st_full, 16 * b.n + u + 1)
                reached(act, pv_done, 8 * (b.n - 1) + 4 * gh + 4)
                nc.scalar.activation(probs[gh][:, kc, j // 2, j % 2].rearrange("p g t -> p (g t)"), score_t[u % 2],
                                     ACT.Exp, scale=SCALE).then_inc(exp_done, 1)

            def step(t):
                for s in range(SLOTS):
                    if t.exists():
                        exp_unit(t, s)
                    for slot, name, off in ROUNDS:
                        if slot == s and (t + off).exists():
                            do_round(name, t + off)
                    if s == 4 and (t + -1).exists():
                        raw_copy(t + -1, 1)
                    if s == 12 and t.exists():
                        raw_copy(t, 0)
                    if s == 4 and (t + -2).exists():
                        b = t + -2
                        reached(act, diff_ready, b.n + 1)
                        nc.scalar.activation(expd[:], diff[:], ACT.Exp).then_inc(exp_ready, 1)

            def centroids():
                act.wait_ge(set_pe, 1)
                nc.scalar.activation(cent_t[:], score_n[0][:, 0:G + E], ACT.Copy).then_inc(set_act, 1)

            act.wait_ge(in_w, 16 * 7)
            act.wait_ge(in_route, 16 * 6)
            nc.scalar.activation(gates[:], gates_in[:], ACT.Tanh).then_inc(set_act, 1)
            act.wait_ge(consts, 1)
            steps(act, step, centroids)

            for q in range(N // 512):
                act.wait_ge(sh_g, q + 1)
                reached(act, sh_hid, q)
                nc.scalar.activation(silu_g[:], ps[:, 0:2, :], ACT.Silu).then_inc(sh_silu, 1)

            def copy_rows(i, k):
                e = WR * i + k
                act.wait_ge(et_full, e + 1)
                reached(act, u_full, e - 1)
                nc.scalar.activation(e_t[k % 2][:], ps[:, 4 + k % 2, 0:CAP], ACT.Copy).then_inc(et_out, 1)

            def silu(i, k):
                e = WR * i + k
                act.wait_ge(g_full, e + 1)
                reached(act, hid_ready, e)
                nc.scalar.activation(silu_g[:, :, 0:CAP], ps[:, 0:2, 0:CAP], ACT.Silu).then_inc(silu_done, 1)

            def expert(i, k):
                silu(i, k)
                copy_rows(i, k + 1)

            act.wait_ge(sh_hid, N // 512)
            copy_rows(0, 0)
            silu(0, 0)
            copy_rows(0, 1)
            expert(0, 1)
            expert(0, 2)
            expert_steps(act, expert)
            silu(0, E - 1)

        @block.vector
        def _(dve):
            V = nc.vector

            def max_unit(b, s):
                gh, g2, jp, qc = s // 8, (s % 8) // 4, (s % 4) // 2, s % 2
                if s % 8 == 0:
                    reached(dve, neg_ready, 2 * (b.n - 1) + gh + 1)
                reached(dve, sn_full, 16 * b.n + s + 1)
                V.tensor_reduce(neg_max[gh][:, qc, g2, 2 * jp:2 * jp + 2], score_n[s % 2].rearrange("p (j t) -> p j t", j=2),
                                AX.X, ALU.max, negate=True).then_inc(sn_max, 1)

            def max_parts(b, gh):
                dve.wait_ge(sn_max, 16 * b.n + 8 * gh + 8)
                reached(dve, mt_full, 2 * (b.n - 1) + gh + 1)
                V.tensor_copy(neg_hl[gh][:, :, :, :, 0], neg_max[gh][:]).then_inc(neg_own, 1)
                dve.wait_ge(neg_own, 2 * b.n + gh + 1)
                V.tensor_tensor(neg_hl[gh][:, :, :, :, 1], neg_max[gh][:], f32(neg_hl[gh][:, :, :, :, 0]),
                                ALU.subtract).then_inc(neg_ready, 1)

            def norm_stats(b, src, stat, aggr, own, done):
                for c in range(2):
                    V.bn_stats(stat[:, c, :], src[:, c, :]).then_inc(own, 1)
                dve.wait_ge(own, 2 * b.n + 2)
                settle(dve)
                for c in range(2):
                    last = V.bn_aggr(aggr[:, c, :], stat[:, c, :])
                    last.then_inc(done, 1)

            def step(t):
                o, o2, p, m = t + -1, t + -2, t + 2, t + 1
                for s in range(SLOTS):
                    if s == 0 and t.exists():
                        max_parts(t, 1)
                    if s == 1 and p.exists():
                        dve.wait_ge(in_x[p.par], 16 * (p.half + 1))
                        reached(dve, rstd1_ready, p.n)
                        norm_stats(p, x_sb[p.par], stat1, aggr1, stat_own1, var1)
                    if s == 8 and m.exists():
                        max_parts(m, 0)
                    if m.exists():
                        max_unit(m, s)
                    if o2.exists() and s in STAGES:
                        STAGES[s](o2)
                    if s == 3 and p.exists():
                        dve.wait_ge(rstd1_ready, p.n + 1)
                        reached(dve, t_full, p.n)
                        dve.wait_ge(var1, 2 * p.n + 2)
                        V.tensor_scalar(h1[:, 0, :], x_sb[p.par][:, 0, :], aggr1[:, 0, 0:1], rstd1[:, 0:1],
                                        ALU.subtract, ALU.mult)
                        V.tensor_scalar(h1[:, 1, :], x_sb[p.par][:, 1, :], aggr1[:, 1, 0:1], rstd1[:, 1:2],
                                        ALU.subtract, ALU.mult).then_inc(h1_ready, 1)
                    if s == 6 and o.exists():
                        normalise(o, 1)
                    if s == 9 and p.exists():
                        reached(dve, rows_full, 4 * p.n)
                        dve.wait_ge(qk_out, 2 * p.n + 2)
                        V.tensor_copy(qk_hi[:], qk[:]).then_inc(split_own, 1)
                    if s == 10 and o.exists():
                        residual(o)
                    if s == 12 and o.exists():
                        second_norm(o)
                    if s == 15 and t.exists():
                        normalise(t, 0)

            def normalise(b, gh):
                misc = bank["norm" + str(gh)]
                raw = misc.rearrange("p (g c j r) -> p g c j r", g=2, c=2, j=4)
                dve.wait_ge(hn_full, 2 * b.n + gh + 1)
                V.reciprocal(inv_sum[:], misc.rearrange("p (a j r) -> p a j r", a=4, j=4)[:, :, :, DK]).then_inc(inv_own, 1)
                dve.wait_ge(inv_own, 2 * b.n + gh + 1)
                if gh == 0:
                    reached(dve, ht_full, b.n)
                for g2 in range(2):
                    g = 2 * gh + g2
                    dst = heads[:].rearrange("p c (j g d) -> p c j g d", j=4, g=NG)[:, :, :, g, :]
                    last = V.tensor_tensor(dst, raw[:, g2, :, :, 0:DK], spread(inv_sum[:, 2 * g2:2 * g2 + 2, :], 3, DK), ALU.mult)
                last.then_inc(heads_ready, 1)

            def residual(b):
                dve.wait_ge(wo_full, b.n + 1)
                dve.wait_ge(xb_ready, b.n + 1)
                reached(dve, x1_free, b.n)
                V.scalar_tensor_tensor(x1[b.par][:], bank["wo"][:, 0:2 * D].rearrange("p (c d) -> p c d", c=2), tanh_x,
                                       xb[b.par][:], ALU.mult, ALU.add).then_inc(x1_ready, 1)
                dve.wait_ge(x1_ready, b.n + 1)
                reached(dve, rstd2_ready, b.n)
                norm_stats(b, x1[b.par], stat2, aggr2, stat_own2, var2)

            def second_norm(b):
                dve.wait_ge(rstd2_ready, b.n + 1)
                reached(dve, rows_free, b.n)
                dve.wait_ge(var2, 2 * b.n + 2)
                for c in range(2):
                    ins = V.tensor_scalar(h2_rows[b.par][:, c, :, 0:D], spread(x1[b.par][:, c, :], 1, K),
                                          aggr2[:, c, 0:1], rstd2[:, c:c + 1], ALU.subtract, ALU.mult)
                ins.then_inc(h2_ready, 1)

            def route_groups(b):
                own = Chain(dve, route_own, ROUTE_OPS * b.n)
                sc = bank["score"][:, 0:2 * (G + E)].rearrange("p (c n) -> p c n", c=2)
                dve.wait_ge(sc_full, b.n + 1)
                settle(dve)
                for c in range(2):
                    own.add(V.max(top_g[:, c, :], sc[:, c, 0:G]))
                own.wait()
                settle(dve)
                for c in range(2):
                    own.add(V.max_index(top_gi[:, c, :], top_g[:, c, :], sc[:, c, 0:G]))
                dve.wait_ge(norm_ready, b.n + 1)
                for c in range(2):
                    last = V.scalar_tensor_tensor(score[:, c, :], sc[:, c, G:G + E], norm2[:, 2, c:c + 1], bias_bc[:],
                                                  ALU.mult, ALU.add)
                    if c:
                        last.then_inc(sc_used, 1)
                own.wait()
                own.add(V.tensor_tensor(is_g[:], spread(top_gi[:, :, 0:K], 2, G),
                                        spread(spread(iota_i[:, 0:G], 1, 2), 3, K), ALU.is_equal))

            def route_mask(b):
                own = Chain(dve, route_own, ROUTE_OPS * b.n + 5)
                own.wait()
                own.add(V.tensor_reduce(mask_g[:], is_g[:], AX.X, ALU.max))
                own.wait()
                own.add(V.tensor_scalar(gap_g[:], mask_g[:], 1e9, -1e9, ALU.mult, ALU.add))
                dve.wait_ge(sc_used, b.n + 1)
                own.add(V.tensor_tensor(masked[:].rearrange("p c (g i) -> p c g i", g=G),
                                        score[:].rearrange("p c (g i) -> p c g i", g=G), spread(mask_g[:], 3, EG), ALU.mult))
                own.wait()
                own.add(V.tensor_tensor(masked[:].rearrange("p c (g i) -> p c g i", g=G),
                                        masked[:].rearrange("p c (g i) -> p c g i", g=G), spread(gap_g[:], 3, EG), ALU.add))

            def route_experts(b):
                own = Chain(dve, route_own, ROUTE_OPS * b.n + 9)
                own.wait()
                settle(dve)
                for c in range(2):
                    own.add(V.max(top_e[:, c, :], masked[:, c, :]))
                own.wait()
                settle(dve)
                for c in range(2):
                    own.add(V.max_index(top_ei[:, c, :], top_e[:, c, :], masked[:, c, :]))
                V.tensor_tensor(diff[:], top_e[:, :, 0:K], top_e[:, :, 0:1].to_broadcast([P, 2, K]),
                                ALU.subtract).then_inc(diff_ready, 1)

            def route_chosen(b):
                own = Chain(dve, route_own, ROUTE_OPS * b.n + 13)
                own.wait()
                own.add(V.tensor_tensor(chosen[:], spread(top_ei[:, :, 0:K], 3, E),
                                        spread(spread(iota_i[:], 1, 2), 1, K).rearrange("p k c e -> p c k e"), ALU.is_equal))
                own.wait()
                dve.wait_ge(earlier_ready, b.n + 1)
                with nc.allow_low_precision(reason="zeros and ones"):
                    V.tensor_reduce(chosen_any[:], chosen[:].rearrange("p c k e -> p c e k"), AX.X, ALU.max).then_inc(chosen_ready, 1)

            def gates_of(b):
                own = Chain(dve, place_own, PLACE_OPS * b.n)
                dve.wait_ge(exp_ready, b.n + 1)
                own.add(V.tensor_reduce(gate_sum[:], expd[:], AX.X, ALU.add))
                own.wait()
                own.add(V.reciprocal(gate_inv[:], gate_sum[:]))
                own.wait()
                own.add(V.tensor_tensor(gate[:], expd[:], spread(gate_inv[:], 2, K), ALU.mult))

            def place(b):
                own = Chain(dve, place_own, PLACE_OPS * b.n + 3)
                dve.wait_ge(cnt_full, b.n + 1)
                dve.wait_ge(route_own, ROUTE_OPS * (b.n + 1))
                V.tensor_tensor(at_slot[:], chosen[:],
                                spread(bank["count"][:, 0:2 * E].rearrange("p (c e) -> p c e", c=2), 2, K), ALU.mult).then_inc(cnt_used, 1)
                dve.wait_ge(cnt_used, b.n + 1)
                own.add(V.tensor_reduce(pos[:], at_slot[:], AX.X, ALU.add))

            def slots(b):
                own = Chain(dve, place_own, PLACE_OPS * b.n + 4)
                own.wait()
                own.add(V.scalar_tensor_tensor(slot_f[:], top_ei[:, :, 0:K], float(CAP), pos[:], ALU.mult, ALU.add))
                own.add(V.tensor_scalar(keep[:], pos[:], float(CAP), None, ALU.is_lt))
                own.wait()
                own.add(V.scalar_tensor_tensor(slot_f[:], keep[:], -FAR, slot_f[:], ALU.mult, ALU.add))
                own.add(V.scalar_tensor_tensor(h2_rows[b.par][:, :, :, COL_GATE], gate[:], tanh_f, keep[:], ALU.mult, ALU.mult))
                own.wait()
                V.tensor_scalar(slot_i[b.par][:], slot_f[:], FAR, None, ALU.add).then_inc(slots_ready, 1)

            STAGES = {1: route_groups, 2: route_mask, 3: route_experts, 4: route_chosen, 5: gates_of, 6: place, 7: slots}

            dve.wait_ge(pool_const, 1)
            V.memset(pick[:].bitcast(fp32), 0.0).then_inc(set_dve, 1)
            V.tensor_reduce(m_ones[:], ident[:, M_ROW:P:M_STEP], AX.X, ALU.add)
            for i in range(2):
                V.memset(v_ext[i][:, :, :, DK:32], 0.0).then_inc(set_dve2, 1)
                dve.wait_ge(set_dve2, i + 1)
                V.memset(v_ext[i][:, :, :, DK], 1.0)
            dve.wait_ge(set_dve, 1)
            cols = ident[:].rearrange("p (j g d) -> p g j d", j=4, d=DK)
            def put(kind, at, first, n):
                dst = pick[:, kind].rearrange("p g (j r) -> p g j r", j=4)[:, :, :, at:at + n]
                return V.tensor_copy(dst, cols[:, :, :, first:first + n])
            for kind in (0, 2):
                put(kind, 0, 0, 8)
            for kind in (1, 2):
                put(kind, 8, 0, 7)
                put(kind, 16, 7, 1)
            for kind in (0, 3):
                last = put(kind, 17, 0, 8)
            last.then_inc(consts, 1)

            def more_constants():
                dve.wait_ge(in_route, 16 * 6)
                V.tensor_tensor(cent_sq[:], cents[:], cents[:], ALU.mult).then_inc(set_dve2, 1)
                dve.wait_ge(set_dve2, 3)
                V.tensor_reduce(cent_n[:, 0:1], cent_sq[:], AX.X, ALU.add).then_inc(set_dve, 1)
                V.memset(ones[:], 1.0)
                V.memset(earlier[0][:], 0.0).then_inc(earlier_ready, 1)
                V.tensor_copy(blank[:, :, COL_TOKEN].bitcast(u32), blank_i[:])
                for i in range(2):
                    last = V.memset(h2_rows[i][:, :, :, D:ROW], 0.0)
                last.then_inc(consts, 1)
                dve.wait_ge(consts, 2)
                dve.wait_ge(pool_const, 2)
                V.tensor_scalar(cents[:], cents[:], cent_n[:, 1:2], None, ALU.mult).then_inc(set_dve, 1)

            steps(dve, step, more_constants)

            def shared_out(q):
                dve.wait_ge(sh_y, q + 1)
                if q >= 2:
                    dve.wait_ge(base_out[q % 2], 16 * (q // 2))
                V.scalar_tensor_tensor(base[q % 2][:], ps[:, 6 + q % 2, :].rearrange("p (t d) -> p t d", d=D), tanh_f,
                                       x1_all[:, 4 * q:4 * q + 4, :], ALU.mult, ALU.add).then_inc(sh_out, 1)

            for i in range(2):
                dve.wait_ge(kept_x[i], 16 * (B // 2))
            for q in range(N // 512):
                dve.wait_ge(sh_silu, q + 1)
                dve.wait_ge(sh_u, q + 1)
                reached(dve, sh_y, q - 1)
                V.tensor_tensor(hid[q % 2][:], silu_g[:], ps[:, 2:4, :], ALU.mult).then_inc(sh_hid, 1)
                if q:
                    shared_out(q - 1)
            shared_out(N // 512 - 1)

            def hidden(i, k):
                e = WR * i + k
                dve.wait_ge(silu_done, e + 1)
                dve.wait_ge(u_full, e + 1)
                reached(dve, y_full, e - 1)
                V.tensor_tensor(hid[k % 2][:, :, 0:CAP], silu_g[:, :, 0:CAP], ps[:, 2:4, 0:CAP], ALU.mult).then_inc(hid_ready, 1)

            def scale_out(i, k):
                e, r = WR * i + k, k % WR
                dve.wait_ge(y_full, e + 1)
                reached(dve, added, 48 * (e - 1))
                for tile, n in ((0, P), (1, P), (2, CAP - 2 * P)):
                    last = V.tensor_scalar(y_sb[k % 2][0:n, tile, :], ps[0:n, 6 + k % 2, tile * D:(tile + 1) * D],
                                           e_rows[r][0:n, tile, COL_GATE:COL_GATE + 1], None, ALU.mult)
                last.then_inc(y_out, 1)

            def expert(i, k):
                hidden(i, k)
                scale_out(i, k - 1)

            hidden(0, 0)
            expert(0, 1)
            expert(0, 2)
            expert_steps(dve, expert)
            expert(0, E - 1)
            scale_out(0, E - 1)

        @block.gpsimd
        def _(pool):
            Q = nc.gpsimd

            def step(t):
                o, p, m, o2 = t + -1, t + 2, t + 1, t + -2
                for s in range(SLOTS):
                    if s == 1 and p.exists():
                        own = Chain(pool, pool_ln1, p.n)
                        pool.wait_ge(var1, 2 * p.n + 2)
                        reached(pool, h1_ready, p.n)
                        settle(pool)
                        own.add(Q.tensor_scalar(rstd1[:], aggr1[:, :, 1], 1e-5, None, ALU.add))
                        own.wait()
                        Q.tensor_tensor(rstd1[:], rstd1[:], neg_half[:], ALU.pow).then_inc(rstd1_ready, 1)
                    if s == 4 and o2.exists():
                        pool.wait_ge(chosen_ready, o2.n + 1)
                        old, new = earlier[o2.par], earlier[1 - o2.par]
                        with nc.allow_low_precision(reason="counts up to 16"):
                            Q.tensor_tensor(new[:], old[:], chosen_any[:, 0, :], ALU.add).then_inc(earlier_own, 1)
                            pool.wait_ge(earlier_own, o2.n + 1)
                            Q.tensor_tensor(new[:], new[:], chosen_any[:, 1, :], ALU.add).then_inc(earlier_ready, 1)
                        pool.wait_ge(h2_ready, o2.n + 1)
                        settle(pool)
                        Q.tensor_copy(h2_rows[o2.par][:, :, :, COL_TOKEN].bitcast(u32), spread(tok_f[:], 2, K)).then_inc(token_written, 1)
                        pool.wait_ge(token_written, o2.n + 1)
                        settle(pool)
                        Q.tensor_scalar(tok_f[:], tok_f[:], float(S), None, ALU.add).then_inc(tok_next, 1)
                        pool.wait_ge(tok_next, o2.n + 1)
                    if s == 9 and p.exists():
                        pool.wait_ge(split_own, p.n + 1)
                        Q.tensor_tensor(qk_lo[:], qk[:], f32(qk_hi[:]), ALU.subtract).then_inc(qk_split, 1)
                    if s == 10 and o.exists():
                        own = Chain(pool, pool_ln2, 4 * o.n)
                        pool.wait_ge(var2, 2 * o.n + 2)
                        reached(pool, h2_ready, o.n)
                        settle(pool)
                        own.add(Q.tensor_scalar(rstd2[:], aggr2[:, :, 1], 1e-5, None, ALU.add))
                        own.wait()
                        Q.tensor_tensor(rstd2[:], rstd2[:], neg_half[:], ALU.pow).then_inc(rstd2_ready, 1)
                        pool.wait_ge(rstd2_ready, o.n + 1)
                        own.add(Q.tensor_tensor(norm2[:, 0, :], aggr2[:, :, 1], rstd2[:], ALU.mult))
                        own.wait()
                        own.add(Q.tensor_tensor(norm2[:, 1, :], norm2[:, 0, :], rstd2[:], ALU.mult))
                        own.wait()
                        settle(pool)
                        own.add(Q.tensor_scalar(norm2[:, 0, :], norm2[:, 1, :], float(D), 1e-24, ALU.mult, ALU.max))
                        own.wait()
                        reached(pool, sc_used, o.n)
                        Q.tensor_tensor(norm2[:, 2, :], norm2[:, 0, :], neg_half[:], ALU.pow).then_inc(norm_ready, 1)
                        assert own.n == 4
                    if s == 11 and m.exists():
                        pool.wait_ge(in_x[m.par], 16 * (m.half + 1))
                        reached(pool, x1_ready, m.n - 1)
                        Q.tensor_tensor(xb[m.par][:], x_sb[m.par][:], spread(bo_bc[:], 1, 2), ALU.add).then_inc(xb_ready, 1)
                    if s in SCATTERS and o2.exists():
                        if s == 8:
                            pool.wait_ge(slots_ready, o2.n + 1)
                            settle(pool)
                        for c, k in (divmod(at, K) for at in SCATTERS[s]):
                            Q.indirect_dma_start(
                                out=dispatch[:, :], out_offset=bass.IndirectOffsetOnAxis(ap=slot_i[o2.par][:, c, k:k + 1], axis=0),
                                in_=h2_rows[o2.par][:, c, k, :], in_offset=None,
                                bounds_check=E * CAP - 1, oob_is_err=False).then_inc(scattered[o2.par], 16)
                    if s == 15 and o2.exists():
                        pool.wait_ge(scattered[o2.par], 16 * 2 * K * (o2.half + 1))
                        pool.sem_inc(rows_free, 1)

            own = Chain(pool, set_pool, 0)
            Q.memset(ident[:], 0.0).then_inc(zeroed, 1)
            pool.wait_ge(zeroed, 1)
            own.add(Q.affine_select(out=ident[:], in_=ident[:], compare_op=ALU.not_equal, fill=1.0, base=0,
                                    pattern=[[-1, P]], channel_multiplier=1))
            Q.memset(neg_half[:], -0.5).then_inc(pool_const, 1)
            pool.sem_inc(rows_free, 1)
            own.wait()
            for i in range(4):
                last = Q.memset(f32(k_rows[i][:]), 0.0)
            last.then_inc(k_blank, 1)
            own.add(Q.memset(before[:], 0.0))
            own.add(Q.memset(blank[:], 0.0))
            own.add(Q.iota(iota_i[:], [[1, E]], base=0, channel_multiplier=0))
            own.add(Q.iota(tok_i[:], [[P, 2]], base=0, channel_multiplier=1))
            own.add(Q.iota(blank_i[:], [[P, 3]], base=N, channel_multiplier=1))
            own.wait()
            own.add(Q.affine_select(out=before[:], in_=before[:], compare_op=ALU.is_ge, fill=1.0, base=0,
                                    pattern=[[-1, P]], channel_multiplier=1))
            own.add(Q.tensor_copy(tok_f[:], tok_i[:]))
            own.wait()
            pool.wait_ge(set_act, 1)
            own.add(Q.tensor_scalar(bo_bc[:], bo_bc[:], tanh_x, None, ALU.mult))
            own.wait()

            def more_constants():
                pool.wait_ge(set_dve, 2)
                own.add(Q.tensor_scalar(cent_n[:, 0:1], cent_n[:, 0:1], 1e-24, None, ALU.max))
                own.wait()
                Q.tensor_tensor(cent_n[:, 1:2], cent_n[:, 0:1], neg_half[0:G + E, 0:1], ALU.pow).then_inc(pool_const, 1)
                pool.wait_ge(consts, 2)
                pool.wait_ge(blanked, 48)

            steps(pool, step, more_constants)

            def add_rows(i, k):
                e, r = WR * i + k, k % WR
                pool.wait_ge(y_out, e + 1)
                reached(pool, added, 48 * e)
                settle(pool)
                for tile, n in ((0, P), (1, P), (2, CAP - 2 * P)):
                    Q.indirect_dma_start(
                        out=sums[:, :], out_offset=bass.IndirectOffsetOnAxis(
                            ap=e_rows[r][0:n, tile, COL_TOKEN:COL_TOKEN + 1].bitcast(u32), axis=0),
                        in_=y_sb[k % 2][0:n, tile, :], in_offset=None, bounds_check=N + DUMP - 1,
                        compute_op=ALU.add).then_inc(added, 16)

            for q in range(N // 512):
                pool.wait_ge(sh_out, q + 1)
                pool.dma_start(sums[512 * q:512 * (q + 1), :].rearrange("(t p) d -> p t d", p=P),
                               base[q % 2][:]).then_inc(base_out[q % 2], 16)
            for i in range(2):
                pool.wait_ge(base_out[i], 16 * (N // 1024))
            add_rows(0, 0)
            add_rows(0, 1)
            add_rows(0, 2)
            expert_steps(pool, add_rows)
            add_rows(0, E - 1)


_ARGS = ["x", "ctx_1024", "g_xattn", "g_ffn", "L0_xattn_Wq", "L0_xattn_bq", "L0_xattn_Wk", "L0_xattn_bk",
         "L0_xattn_Wv", "L0_xattn_bv", "L0_xattn_Wo", "L0_xattn_bo", "L0_ffn_group_centroids",
         "L0_ffn_expert_centroids", "L0_ffn_bias"]


def kernel(**inputs):
    import numpy as np
    import concourse.bacc as bacc
    from concourse.bass_utils import run_bass_kernel_spmd

    nc = bacc.Bacc("TRN2", target_bir_lowering=False, num_devices=1)
    arrays, args = {}, []

    def give(name, a):
        a = np.ascontiguousarray(a)
        arrays[name] = a
        args.append(nc.dram_tensor(name, a.shape, mybir.dt.from_np(a.dtype), kind="ExternalInput").ap())

    for name in _ARGS:
        a = np.asarray(inputs[name])
        give(name, a.T if name.split("_")[-1] in ("Wq", "Wk", "Wv", "Wo") else a)
    wg, wu, wd = (np.asarray(inputs[f"L0_ffn_{n}"]) for n in ("wg", "wu", "wd"))
    wd = wd.reshape(E, 2, P, D).transpose(0, 2, 1, 3)
    give("w_all", np.concatenate([wg.reshape(E, P, 2, P), wu.reshape(E, P, 2, P), wd], axis=2))
    for name in ("sg", "su", "sd"):
        give(name, inputs[f"L0_ffn_{name}"])
    args.append(nc.dram_tensor("out", (B, S, D), mybir.dt.float32, kind="ExternalOutput").ap())
    args.append(nc.dram_tensor("dispatch", (E * CAP, ROW), mybir.dt.float32, kind="Internal").ap())
    args.append(nc.dram_tensor("sums", (N + DUMP, D), mybir.dt.float32, kind="Internal").ap())
    gated_attention_and_experts(nc, *args)
    r = run_bass_kernel_spmd(nc, [arrays], core_ids=[0])
    return r.results[0]["out"]
```

```python
import concourse.bass as bass
from concourse import mybir
from contextlib import ExitStack

B, S, D = 8, 256, 128
H, DK = 16, 8
N = B * S
E, G, K = 32, 8, 4
F = 256
CAP = int(N / E * K * 1.25)
P = 128
EG = E // G
ROW = D + 4
COL_TOKEN, COL_GATE = D, D + 1
DUMP = CAP
NG = H // 4
M_ROW, M_STEP = 15, 16


class Batch:

    def __init__(self, i, k):
        self.half, self.par = i + k // 2, k % 2
        self.n = 2 * i + k
        self.i, self.k = i, k

    def __add__(self, d):
        return Batch(self.i, self.k + d)

    def first_two(self):
        return isinstance(self.n, int) and self.n < 2

    def exists(self):
        return not isinstance(self.n, int) or 0 <= self.n < B


class Chain:

    def __init__(self, eng, sem, start):
        self.eng, self.sem, self.start, self.n = eng, sem, start, 0

    def add(self, ins):
        ins.then_inc(self.sem, 1)
        self.n += 1

    def wait(self):
        self.eng.wait_ge(self.sem, self.start + self.n)


def reached(eng, sem, value):
    if not isinstance(value, int) or value > 0:
        eng.wait_ge(sem, value)


def gated_attention_and_experts(
    nc, x, ctx_in, g_xattn, g_ffn, wq_t, bq, wk_t, bk, wv_t, bv, wo_t, bo,
    group_centroids, expert_centroids, bias, w_all, sg, su, sd, sums0, out, dispatch,
):
    fp32, fp32r, bf16 = mybir.dt.float32, mybir.dt.float32r, mybir.dt.bfloat16
    u32, i32 = mybir.dt.uint32, mybir.dt.int32
    ALU, ACT, AX = mybir.AluOpType, mybir.ActivationFunctionType, mybir.AxisListType
    SCALE = float(DK) ** -0.5

    sums = [sums0, out]

    ctx = ExitStack()
    with ctx:
        def sb(name, shape, dt=fp32):
            return ctx.enter_context(nc.sbuf_tensor(name, shape, dt))

        def sem(name):
            return ctx.enter_context(nc.semaphore(name))

        def f32(ap):
            return ap.bitcast(fp32)

        def spread(ap, axis, n):
            ap = ap.unsqueeze(axis)
            shape = list(ap.shape)
            shape[axis] = n
            return ap.to_broadcast(shape)

        wq_sb, wk_sb, wv_sb, wo_sb = (sb(n, [P, D]) for n in ("wq_sb", "wk_sb", "wv_sb", "wo_sb"))
        bq_sb, bk_sb, bv_sb = (sb(n, [P, 1]) for n in ("bq_sb", "bk_sb", "bv_sb"))
        bo_bc, bias_bc = sb("bo_bc", [P, D]), sb("bias_bc", [P, E])
        gates_in, gates = sb("gates_in", [P, 2]), sb("gates", [P, 2])
        tanh_x, tanh_f = gates[:, 0:1], gates[:, 1:2]
        ident = sb("ident", [P, P])
        m_ones = sb("m_ones", [P, 1])
        pick = sb("pick", [P, 4, NG, P], fp32r)
        before = sb("before", [P, P], bf16)
        ones = sb("ones", [P, P], bf16)
        iota_i = sb("iota_i", [P, E], i32)
        tok_i, tok_f = sb("tok_i", [P, 2], i32), sb("tok_f", [P, 2])
        neg_half = sb("neg_half", [P, 2])
        cent_n = sb("cent_n", [G + E, 2])
        cent_t = sb("cent_t", [P, G + E])
        blank, blank_i = sb("blank", [P, 3, ROW]), sb("blank_i", [P, 3], i32)

        x_sb = [sb(f"x_sb{i}", [P, 2, D]) for i in range(2)]
        c_sb = [sb(f"c_sb{i}", [P, 2, D]) for i in range(2)]
        xr = [sb(f"xr{i}", [P, 2, D]) for i in range(2)]
        stat1, aggr1, rstd1 = sb("stat1", [P, 2, 6]), sb("aggr1", [P, 2, 2]), sb("rstd1", [P, 2])
        h1 = sb("h1", [P, 2, D])
        hc_t = sb("hc_t", [P, 4, P])
        qk = sb("qk", [P, 2, S])
        qk_hi, qk_lo = sb("qk_hi", [P, 2, S], fp32r), sb("qk_lo", [P, 2, S], fp32r)
        q_rows = [sb(f"q_rows{i}", [P, 2, S], fp32r) for i in range(4)]
        k_stage = [sb(f"k_stage{i}", [P, 2, S], fp32r) for i in range(2)]
        k_rows = [sb(f"k_rows{i}", [P, 4, 2, S], fp32r) for i in range(4)]
        v_ext = [sb(f"v_ext{i}", [P, 2, H, 32]) for i in range(2)]
        neg_max = [sb(f"neg_max{i}", [P, 2, 2, 4]) for i in range(2)]
        neg_hl = [sb(f"neg_hl{i}", [P, 2, 2, 4, 2], fp32r) for i in range(2)]
        max_t = [sb(f"max_t{i}", [16, S], fp32r) for i in range(2)]
        probs = [sb(f"probs{i}", [P, 2, 2, 2, 2, S]) for i in range(2)]
        heads_raw = [sb(f"heads_raw{i}", [P, 2, S]) for i in range(2)]
        inv_sum = sb("inv_sum", [P, 4, 4])
        heads = sb("heads", [P, 2, D])
        heads_t = sb("heads_t", [P, 2, P])

        x1 = [sb(f"x1_{i}", [P, 2, D]) for i in range(2)]
        stat2, aggr2, rstd2 = sb("stat2", [P, 2, 6]), sb("aggr2", [P, 2, 2]), sb("rstd2", [P, 2])
        norm2 = sb("norm2", [P, 3, 2])
        h2_rows = [sb(f"h2_rows{i}", [P, 2, K, ROW]) for i in range(2)]
        h2_t = [sb(f"h2_t{i}", [P, 2, P]) for i in range(2)]
        top_g, top_gi = sb("top_g", [P, 2, 8]), sb("top_gi", [P, 2, 8], u32)
        is_g, mask_g, gap_g = sb("is_g", [P, 2, G, K]), sb("mask_g", [P, 2, G]), sb("gap_g", [P, 2, G])
        score, masked = sb("score", [P, 2, E]), sb("masked", [P, 2, E])
        top_e, top_ei = sb("top_e", [P, 2, 8]), sb("top_ei", [P, 2, 8], u32)
        chosen = sb("chosen", [P, 2, K, E], bf16)
        chosen_two = sb("chosen_two", [P, 2, 2, E], bf16)
        chosen_any = sb("chosen_any", [P, 2, E], bf16)
        earlier = [sb(f"earlier{i}", [P, E], bf16) for i in range(2)]
        diff, expd, gate = sb("diff", [P, 2, K]), sb("expd", [P, 2, K]), sb("gate", [P, 2, K])
        gate_sum, gate_inv = sb("gate_sum", [P, 2]), sb("gate_inv", [P, 2])
        at_slot, pos, slot_f = sb("at_slot", [P, 2, K, E]), sb("pos", [P, 2, K]), sb("slot_f", [P, 2, K])
        keep = sb("keep", [P, 2, K])
        slot_i = [sb(f"slot_i{i}", [P, 2, K], u32) for i in range(2)]
        x1_all, h2t_all = sb("x1_all", [P, N // P, D]), sb("h2t_all", [P, N])

        WR = 4
        sg_sb, su_sb, sd_sb = sb("sg_sb", [P, F]), sb("su_sb", [P, F]), sb("sd_sb", [P, 2, D])
        w_sb = [sb(f"w_sb{i}", [P, 4, P]) for i in range(WR)]
        wd_sb = [sb(f"wd_sb{i}", [P, 2, P]) for i in range(WR)]
        w_hi, w_lo = ([sb(f"w_{n}{i}", [P, 4, P], fp32r) for i in range(2)] for n in ("hi", "lo"))
        e_rows = [sb(f"e_rows{i}", [P, 3, ROW]) for i in range(WR)]
        e_token = [sb(f"e_token{i}", [P, 3], u32) for i in range(2)]
        e_hi, e_lo = ([sb(f"e_{n}{i}", [P, CAP], fp32r) for i in range(2)] for n in ("hi", "lo"))
        silu_g = sb("silu_g", [P, 2, 512])
        hid = [sb(f"hid{i}", [P, 2, 512]) for i in range(2)]
        y_sb = [sb(f"y_sb{i}", [P, 3, D]) for i in range(2)]
        cents, cent_sq = y_sb[0][0:G + E, 0, :], y_sb[0][0:G + E, 1, :]
        base = [sb(f"base{i}", [P, 4, D]) for i in range(2)]

        ps = ctx.enter_context(nc.psum_tensor("ps", [P, 8, 512], fp32))
        score_t = [ps[:, i, :] for i in range(2)]
        score_n = [ps[:, 2 + i, :] for i in range(2)]
        heads_ps = ps[:, 7, :]

        in_x, in_c = [sem(f"in_x{i}") for i in range(2)], [sem(f"in_c{i}") for i in range(2)]
        in_w, in_route, in_shared = sem("in_w"), sem("in_route"), sem("in_shared")
        set_pool, set_dve, set_act = sem("set_pool"), sem("set_dve"), sem("set_act")
        set_pe = sem("set_pe")
        pool_const, zeroed = sem("pool_const"), sem("zeroed")
        consts = sem("consts")
        blank_ready = sem("blank_ready")
        blanked = sem("blanked")
        var1, rstd1_ready, h1_ready = sem("var1"), sem("rstd1_ready"), sem("h1_ready")
        in_xr, xr_ready = [sem(f"in_xr{i}") for i in range(2)], sem("xr_ready")
        t_full, t_out = sem("t_full"), sem("t_out")
        qk_full, qk_out = sem("qk_full"), sem("qk_out")
        qk_split = sem("qk_split")
        v_full, v_out = sem("v_full"), sem("v_out")
        rows_full, rows_out = sem("rows_full"), sem("rows_out")
        sn_full, sn_max = sem("sn_full"), sem("sn_max")
        neg_own, neg_ready = sem("neg_own"), sem("neg_ready")
        mt_full, mt_out = sem("mt_full"), sem("mt_out")
        k_landed = [[sem(f"k_landed{gh}{jp}") for jp in range(2)] for gh in range(2)]
        v_blank = sem("v_blank")
        k_blank = sem("k_blank")
        m_landed = [sem(f"m_landed{i}") for i in range(2)]
        st_full, exp_done = sem("st_full"), sem("exp_done")
        pv_done, raw_out = sem("pv_done"), sem("raw_out")
        hn_full, inv_own = sem("hn_full"), sem("inv_own")
        heads_ready = sem("heads_ready")
        ht_full, ht_out = sem("ht_full"), sem("ht_out")
        wo_full, x1_ready = sem("wo_full"), sem("x1_ready")
        var2, rstd2_ready, h2_ready = sem("var2"), sem("rstd2_ready"), sem("h2_ready")
        h2_copied = sem("h2_copied")
        pool_ln1, pool_ln2 = sem("pool_ln1"), sem("pool_ln2")
        h2t_full, h2t_out = sem("h2t_full"), sem("h2t_out")
        kept_x, kept_h = [sem(f"kept_x{i}") for i in range(2)], [sem(f"kept_h{i}") for i in range(2)]
        x1_free, h2t_free = sem("x1_free"), sem("h2t_free")
        sc_full, sc_used, route_own = sem("sc_full"), sem("sc_used"), sem("route_own")
        picked, picked_own, chosen_ready = sem("picked"), sem("picked_own"), sem("chosen_ready")
        diff_ready, exp_ready = sem("diff_ready"), sem("exp_ready")
        earlier_own, earlier_ready = sem("earlier_own"), sem("earlier_ready")
        cnt_full, cnt_used, place_own = sem("cnt_full"), sem("cnt_used"), sem("place_own")
        slots_ready = sem("slots_ready")
        token_written, tok_next = sem("token_written"), sem("tok_next")
        scattered = [sem(f"scattered{i}") for i in range(2)]
        sh_g, sh_u, sh_silu, sh_hid, sh_y, sh_out = (sem(n) for n in ("sh_g", "sh_u", "sh_silu", "sh_hid", "sh_y", "sh_out"))
        base_out = [sem(f"base_out{i}") for i in range(2)]
        w_in, rows_in = [sem(f"w_in{i}") for i in range(WR)], [sem(f"rows_in{i}") for i in range(WR)]
        wd_in = [sem(f"wd_in{i}") for i in range(WR)]
        w_high, w_split, e_high, e_split = sem("w_high"), sem("w_split"), sem("e_high"), sem("e_split")
        et_full, g_full, u_full = sem("et_full"), sem("g_full"), sem("u_full")
        silu_done, hid_ready, y_full = sem("silu_done"), sem("hid_ready"), sem("y_full")
        y_out = sem("y_out")
        added = [sem(f"added{i}") for i in range(2)]
        sums_in, written = sem("sums_in"), sem("written")
        passed = sem("passed")
        stat_own1, stat_own2, norm_ready = sem("stat_own1"), sem("stat_own2"), sem("norm_ready")
        set_dve2 = sem("set_dve2")
        ROUTE_OPS, PLACE_OPS = 13, 8
        FAR = 1048576.0

        SLOTS = 16
        FIRST, LAST = -2, B + 1
        LOOP_FROM, LOOP_PAIRS = 2, 2

        ROUNDS = [(0, "score", -2), (2, "k1", 1), (3, "max1", 0), (3, "q1", 1), (4, "v", 1),
                  (5, "t", 2), (6, "norm1", -1), (6, "count", -2), (7, "qk", 2), (8, "heads", -1),
                  (9, "max0", 1), (10, "wo", -1), (10, "k0", 2), (12, "q0", 2), (14, "norm0", 0),
                  (14, "h2", -1)]
        BANKS = 3
        bank = {name: ps[:, 4 + at % BANKS, :] for at, (_, name, _) in enumerate(ROUNDS)}
        TIMES_VALUES = [(1, 1, 1, -1), (2, 1, 2, -1), (3, 1, 3, -1), (6, 0, 0, 0), (9, 0, 1, 0),
                        (10, 0, 2, 0), (11, 0, 3, 0), (14, 1, 0, 0)]
        SCATTERS = {9: (0, 1, 2), 12: (3, 4), 14: (5, 6, 7)}

        SHARED_PE = ({3: "g0a", 6: "g0b", 8: "u0a", 10: "u0b g1a g1b u1a u1b"},
                     {0: "y0a y0b g2a g2b u2a", 6: "u2b y1a y1b g3a g3b u3a u3b y2a y2b y3a y3b"})
        SHARED_ACT = ({8: "s0", 12: "s1"}, {5: "s2", 8: "s3"})
        SHARED_DVE = ({12: "h0", 14: "h1"}, {5: "b0", 10: "h2 b1 h3 b2 b3"})
        SHARED_SP = ({}, {10: "b0 b1 b2 b3"})
        NQ = N // 512

        def shared_parts(table, t, s):
            last_steps = isinstance(t.n, int) and t.n >= B
            return table[t.n - B].get(s, "").split() if last_steps else ()

        def emptied(name, b):
            n = b.n
            return {"max0": (mt_out, 2 * n + 1), "max1": (mt_out, 2 * n + 2), "v": (v_out, n + 1),
                    "heads": (ht_out, n + 1), "wo": (x1_ready, n + 1), "t": (t_out, n + 1),
                    "k0": (rows_out, 4 * n + 1), "q0": (rows_out, 4 * n + 2),
                    "k1": (rows_out, 4 * n + 3), "q1": (rows_out, 4 * n + 4),
                    "norm0": (heads_ready, 2 * n + 1), "norm1": (heads_ready, 2 * n + 2),
                    "h2": (h2t_out, n + 1), "qk": (qk_out, 4 * n + 4), "score": (sc_used, n + 1),
                    "count": (cnt_used, n + 1)}[name]

        def round_before(t, at):
            mine = at % BANKS
            while True:
                at -= 1
                if at < 0:
                    at, t = len(ROUNDS) - 1, t + -1
                _, name, off = ROUNDS[at]
                if isinstance(t.n, int) and t.n < FIRST:
                    return None
                if at % BANKS == mine and (t + off).exists():
                    return emptied(name, t + off)

        def settle(eng):
            eng.sem_inc(passed, 1)

        def steps(eng, step, after_first=None, after_second=None):
            t = FIRST
            while t <= LAST:
                if t == FIRST + 1 and after_first:
                    after_first()
                if t == FIRST + 2 and after_second:
                    after_second()
                if t == LOOP_FROM:
                    with eng.Fori(0, LOOP_PAIRS) as i:
                        for k in range(2):
                            step(Batch(i, LOOP_FROM + k))
                    t += 2 * LOOP_PAIRS
                else:
                    step(Batch(0, t))
                    t += 1

        def exists(i, k):
            return not isinstance(i, int) or WR * i + k < E

        def expert_steps(eng, expert):
            expert(0, 1)
            expert(0, 2)
            with eng.Fori(0, E // WR - 2) as i:
                for k in range(3, WR + 3):
                    expert(i, k)
            for k in range(E - 5, E):
                expert(0, k)

        block = ctx.enter_context(nc.Block())

        @block.sync
        def _(sp):
            def load(b):
                if b.exists():
                    reached(sp, h1_ready, b.n - 1)
                    sp.dma_start(x_sb[b.par][:], x[b.n].rearrange("(c p) d -> p c d", p=P)).then_inc(in_x[b.par], 16)
                    reached(sp, t_full, b.n - 1)
                    sp.dma_start(c_sb[b.par][:], ctx_in[b.n].rearrange("(c p) d -> p c d", p=P)).then_inc(in_c[b.par], 16)

            def max_rows(b, gh):
                if b.exists():
                    reached(sp, mt_out, 2 * b.n + gh + 1)
                    for g in range(2):
                        dst = q_rows[2 * b.par + gh][M_ROW:P:M_STEP, g, :]
                        sp.dma_start(f32(dst), f32(max_t[gh][8 * g:8 * g + 8, :])).then_inc(m_landed[gh], 16)

            def key_rows(b, gh):
                if b.exists() and not b.first_two():
                    reached(sp, st_full, 16 * (b.n - 2) + 8 * gh + 8)
                    settle(sp)
                    sp.wait_ge(rows_out, 4 * b.n + 2 * gh + 1)
                    for j in range(4):
                        rows = slice(32 * j, 32 * j + 32)
                        sp.dma_start(f32(k_rows[2 * b.par + gh][rows, j, :, :]),
                                     f32(k_stage[gh][rows, :, :])).then_inc(k_landed[gh][j // 2], 16)

            BLANKS_FROM, BLANKS_TO = -2, 0
            BLANK_SLOTS = (1, 5, 7, 9, 14)
            PIECES = 8

            def weights_of(e, r):
                sp.dma_start(w_sb[r][:], w_all[e, :, 0:4, :]).then_inc(w_in[r], 16)

            def down_weights_of(e, r):
                sp.dma_start(wd_sb[r][:], w_all[e, :, 4:6, :]).then_inc(wd_in[r], 16)

            def blank_piece(at):
                rows = dispatch.rearrange("(e r) w -> e r w", r=CAP)
                n = E // PIECES
                if at < PIECES:
                    sp.dma_start(rows[at * n:at * n + n, 0:2 * P, :].rearrange("e (p c) w -> p e (c w)", c=2),
                                 spread(blank[:, 0:2, :].rearrange("p c w -> p (c w)"), 1, n)).then_inc(blanked, 16)
                elif at < PIECES + 2:
                    half = slice((at - PIECES) * E // 2, (at - PIECES + 1) * E // 2)
                    sp.dma_start(rows[half, 2 * P:CAP, :].rearrange("e p w -> p e w"),
                                 spread(blank[0:CAP - 2 * P, 2, :], 1, E // 2)).then_inc(blanked, 16)
                elif at == PIECES + 2:
                    sp.dma_start(sums[1][0:N, :].rearrange("(p r) d -> p r d", p=P),
                                 spread(blank[:, 0, 0:D], 1, N // P)).then_inc(blanked, 16)
                elif at == PIECES + 3:
                    sp.dma_start(sg_sb[:], sg).then_inc(in_shared, 16)
                    sp.dma_start(su_sb[:], su).then_inc(in_shared, 16)
                    sp.dma_start(sd_sb[:], sd.rearrange("(c p) d -> p c d", p=P)).then_inc(in_shared, 16)

            def step(t):
                for s in range(SLOTS):
                    if s == 0 and not (isinstance(t.n, int) and t.n + 2 < 2):
                        load(t + 2)
                    if isinstance(t.n, int) and BLANKS_FROM <= t.n <= BLANKS_TO and s in BLANK_SLOTS:
                        blank_piece((t.n - BLANKS_FROM) * len(BLANK_SLOTS) + BLANK_SLOTS.index(s))
                    if s == 3:
                        key_rows(t + 1, 1)
                        max_rows(t, 1)
                    if isinstance(t.n, int) and t.n == 1 and s in (5, 7, 9, 12):
                        r = (5, 7, 9, 12).index(s)
                        weights_of(r, r)
                        down_weights_of(r, r)
                    if s == 4 and (t + -2).exists():
                        b = t + -2
                        reached(sp, x1_ready, b.n + 1)
                        sp.dma_start(x1_all[:, bass.ds(2 * b.n, 2), :], x1[b.par][:]).then_inc(kept_x[b.par], 16)
                        reached(sp, h2t_out, b.n + 1)
                        sp.dma_start(h2t_all[:, bass.ds(S * b.n, S)],
                                     h2_t[b.par][:].rearrange("p c t -> p (c t)")).then_inc(kept_h[b.par], 16)
                    if s == 9:
                        max_rows(t + 1, 0)
                    if s == 10:
                        key_rows(t + 2, 0)
                    if s == 11 and (t + 1).exists():
                        b = t + 1
                        reached(sp, x1_ready, b.n - 1)
                        sp.dma_start(xr[b.par][:], x[b.n].rearrange("(c p) d -> p c d", p=P)).then_inc(in_xr[b.par], 16)
                    if s == 11 and (t + -2).exists():
                        b = t + -2
                        sp.wait_ge(kept_x[b.par], 16 * (b.half + 1))
                        sp.sem_inc(x1_free, 1)
                        sp.wait_ge(kept_h[b.par], 16 * (b.half + 1))
                        sp.sem_inc(h2t_free, 1)
                    for part in shared_parts(SHARED_SP, t, s):
                        q = int(part[1])
                        sp.wait_ge(sh_out, q + 1)
                        sp.dma_start(sums[0][512 * q:512 * (q + 1), :].rearrange("(t p) d -> p t d", p=P),
                                     base[q % 2][:]).then_inc(base_out[q % 2], 16)

            load(Batch(0, 0))
            load(Batch(0, 1))
            for dst, src in ((wq_sb, wq_t), (wk_sb, wk_t), (bq_sb, bq.rearrange("(p o) -> p o", o=1)),
                             (bk_sb, bk.rearrange("(p o) -> p o", o=1)), (wv_sb, wv_t), (wo_sb, wo_t),
                             (bv_sb, bv.rearrange("(p o) -> p o", o=1))):
                sp.dma_start(dst[:], src).then_inc(in_w, 16)
            for dst, src in ((gates_in[:, 0:1], g_xattn.partition_broadcast(P)),
                             (gates_in[:, 1:2], g_ffn.partition_broadcast(P)),
                             (bo_bc, bo.partition_broadcast(P)), (bias_bc, bias.partition_broadcast(P)),
                             (y_sb[0][0:G, 0, :], group_centroids), (y_sb[0][G:G + E, 0, :], expert_centroids)):
                sp.dma_start(dst[:], src).then_inc(in_route, 16)
            sp.sem_inc(x1_free, 1)
            sp.sem_inc(h2t_free, 1)
            sp.wait_ge(blank_ready, 1)
            steps(sp, step)

            def load_expert(i, r):
                e = WR * i + r
                sp.wait_ge(w_split, e - WR + 1)
                weights_of(e, r)
                sp.wait_ge(y_full, e - WR + 1)
                down_weights_of(e, r)
                sp.wait_ge(y_out, e - WR + 1)
                rows_of(sp, e, r)

            def rows_of(sp, e, r):
                rows_e = dispatch[bass.ds(e * CAP, CAP), :]
                sp.dma_start(e_rows[r][:, 0:2, :], rows_e[0:2 * P, :].rearrange("(p c) w -> p c w", c=2)).then_inc(rows_in[r], 16)
                sp.dma_start(e_rows[r][0:CAP - 2 * P, 2, :], rows_e[2 * P:CAP, :]).then_inc(rows_in[r], 16)

            for i in range(2):
                sp.wait_ge(scattered[i], 16 + 16 * 2 * K * (B // 2))
            for r in range(WR):
                rows_of(sp, r, r)
            with sp.Fori(1, E // WR) as i:
                for r in range(WR):
                    load_expert(i, r)
            sp.wait_ge(added[0], 48 * (E // 2))
            for at in range(0, N // P, 4):
                sp.dma_start(x1_all[:, at:at + 4, :],
                             sums[0][0:N, :].rearrange("(p r) d -> p r d", p=P)[:, at:at + 4, :]).then_inc(sums_in, 16)

        @block.tensor
        def _(pe):
            def mm(dst, lhs_t, rhs, start=True, stop=True):
                return nc.tensor.matmul(dst, lhs_t, rhs, start=start, stop=stop)

            def rows_round(kind, gh):
                misc = bank["qk"[kind] + str(gh)]
                for g2 in range(2):
                    g = 2 * gh + g2
                    dst = misc[:, g2 * S:(g2 + 1) * S]
                    mm(dst, pick[:, 2 * kind, g, :], qk_hi[:, kind, :], True, False)
                    last = mm(dst, pick[:, 2 * kind + 1, g, :], qk_lo[:, kind, :], False, True)
                last.then_inc(rows_full, 1)

            def max_round(b, gh):
                misc = bank["max" + str(gh)]
                reached(pe, neg_ready, 2 * b.n + gh + 1)
                for qc in range(2):
                    last = nc.tensor.transpose(misc[0:16, qc * P:(qc + 1) * P],
                                               f32(neg_hl[gh][:, qc].rearrange("p g j t -> p (g j t)")), ident[:])
                last.then_inc(mt_full, 1)

            def do_round(name, b):
                misc = bank[name]
                if name in ("max0", "max1"):
                    max_round(b, int(name[-1]))
                elif name == "t":
                    reached(pe, h1_ready, b.n + 1)
                    pe.wait_ge(in_c[b.par], 16 * (b.half + 1))
                    for c in range(4):
                        src = h1[:, c, :] if c < 2 else c_sb[b.par][:, c - 2, :]
                        last = nc.tensor.transpose(misc[:, c * P:(c + 1) * P], src, ident[:])
                    last.then_inc(t_full, 1)
                elif name == "qk":
                    if isinstance(b.n, int) and b.n == 0:
                        pe.wait_ge(in_w, 16 * 7)
                    reached(pe, t_out, b.n + 1)
                    mm(misc[:, 0:S], wq_sb[:], hc_t[:, 0:2, :].rearrange("p c t -> p (c t)"))
                    mm(misc[:, S:2 * S], wk_sb[:], hc_t[:, 2:4, :].rearrange("p c t -> p (c t)")).then_inc(qk_full, 1)
                elif name == "v":
                    for c in range(2):
                        last = mm(misc[:, c * P:(c + 1) * P], hc_t[:, 2 + c, :], wv_sb[:])
                    last.then_inc(v_full, 1)
                elif name in ("q0", "q1", "k0", "k1"):
                    if isinstance(b.n, int) and b.n == 0 and name == "k0":
                        pe.wait_ge(consts, 1)
                    reached(pe, qk_split, 2 * b.n + (1 if name[0] == "k" else 2))
                    rows_round("qk".index(name[0]), int(name[1]))
                elif name in ("norm0", "norm1"):
                    gh = int(name[-1])
                    reached(pe, raw_out, 2 * b.n + gh + 1)
                    for g2 in range(2):
                        for qc in range(2):
                            at = 2 * g2 + qc
                            last = nc.tensor.transpose(misc[:, at * P:(at + 1) * P],
                                                       heads_raw[gh][:, g2, qc * P:(qc + 1) * P], ident[:])
                    last.then_inc(hn_full, 1)
                elif name == "heads":
                    reached(pe, heads_ready, 2 * b.n + 2)
                    for c in range(2):
                        last = nc.tensor.transpose(misc[:, c * P:(c + 1) * P], heads[:, c, :], ident[:])
                    last.then_inc(ht_full, 1)
                elif name == "wo":
                    reached(pe, ht_out, b.n + 1)
                    for c in range(2):
                        last = mm(misc[:, c * P:(c + 1) * P], heads_t[:, c, :], wo_sb[:])
                    last.then_inc(wo_full, 1)
                elif name == "h2":
                    reached(pe, h2_ready, b.n + 1)
                    for c in range(2):
                        last = nc.tensor.transpose(misc[:, c * P:(c + 1) * P], h2_rows[b.par][:, c, 0, 0:D], ident[:])
                    last.then_inc(h2t_full, 1)
                elif name == "score":
                    reached(pe, h2t_out, b.n + 1)
                    for c in range(2):
                        last = mm(misc[:, c * (G + E):(c + 1) * (G + E)], h2_t[b.par][:, c, :], cent_t[:])
                    last.then_inc(sc_full, 1)
                elif name == "count":
                    reached(pe, chosen_ready, b.n + 1)
                    pe.wait_ge(earlier_ready, b.n + 1)
                    mm(misc[:, 0:E], before[:], chosen_any[:, 0, :], True, False)
                    mm(misc[:, 0:E], ones[:], earlier[b.par][:], False, True)
                    mm(misc[:, E:2 * E], before[:], chosen_any[:, 1, :], True, False)
                    mm(misc[:, E:2 * E], ones[:], chosen_any[:, 0, :], False, False)
                    mm(misc[:, E:2 * E], ones[:], earlier[b.par][:], False, True).then_inc(cnt_full, 1)

            g_ps, u_ps = ps[:, 0:2, :], ps[:, 2:4, :]
            y_ps = [ps[:, 6 + i, :] for i in range(2)]
            x_ps = [ps[:, 4 + i, :] for i in range(2)]

            def shared(part, q, c):
                tokens = h2t_all[:, q * 512:(q + 1) * 512]
                if part == "g":
                    if c == 0:
                        if q == 0:
                            pe.wait_ge(in_shared, 48)
                            pe.wait_ge(exp_done, 16 * B)
                            pe.wait_ge(sn_max, 16 * B)
                        for i in range(2):
                            pe.wait_ge(kept_h[i], 16 * (q + 1))
                        reached(pe, sh_silu, q)
                    mm(g_ps[:, c, :], sg_sb[:, c * P:(c + 1) * P], tokens).then_inc(sh_g, 1)
                elif part == "u":
                    if c == 0:
                        reached(pe, sh_hid, q)
                    mm(u_ps[:, c, :], su_sb[:, c * P:(c + 1) * P], tokens).then_inc(sh_u, 1)
                else:
                    if c == 0:
                        pe.wait_ge(sh_hid, q + 1)
                        pe.wait_ge(raw_out, 2 * B)
                        reached(pe, sh_out, q)
                    for tile in (2 * c, 2 * c + 1):
                        for k in range(2):
                            last = mm(y_ps[1][:, tile * D:(tile + 1) * D], hid[q % 2][:, k, tile * P:(tile + 1) * P],
                                      sd_sb[:, k, :], k == 0, k == 1)
                    last.then_inc(sh_y, 1)

            def scores_for_max(b, s):
                gh, g2, jp, qc = s // 8, (s % 8) // 4, (s % 4) // 2, s % 2
                q, k = q_rows[2 * b.par + gh], k_rows[2 * b.par + gh]
                if s % 8 == 0:
                    reached(pe, rows_out, 4 * b.n + 2 * gh + 2)
                if qc == 0 and g2 == 0 and not b.first_two():
                    pe.wait_ge(k_landed[gh][jp], 32 * (b.n - 1))
                reached(pe, sn_max, 16 * b.n + s - 1)
                mm(score_n[s % 2], q[:, g2, qc * P:(qc + 1) * P], k[:, 2 * jp:2 * jp + 2, g2, :]).then_inc(sn_full, 1)

            def scores_for_exp(b, u):
                gh, kc, j = u // 8, (u % 8) // 4, u % 4
                q, k = q_rows[2 * b.par + gh], k_rows[2 * b.par + gh]
                if u % 8 == 0:
                    reached(pe, m_landed[gh], 32 * (b.n + 1))
                reached(pe, exp_done, 16 * b.n + u - 1)
                for g2 in range(2):
                    last = mm(score_t[u % 2][:, g2 * S:(g2 + 1) * S], k[:, j, g2, kc * P:(kc + 1) * P], q[:, g2, :])
                last.then_inc(st_full, 1)

            def times_values(b, gh, piece):
                g2, kc = piece // 2, piece % 2
                if piece == 0:
                    reached(pe, v_out, b.n + 1)
                    reached(pe, raw_out, 2 * b.n + gh)
                if piece < 2:
                    reached(pe, exp_done, 16 * b.n + 8 * gh + 4 * kc + 4)
                for j in range(4):
                    last = mm(heads_ps[32 * j:32 * j + 32, g2 * S:(g2 + 1) * S], v_ext[b.par][:, kc, 4 * j + 2 * gh + g2, :],
                              probs[gh][:, kc, j // 2, j % 2, g2, :], kc == 0, kc == 1)
                last.then_inc(pv_done, 1)

            def step(t):
                for s in range(SLOTS):
                    if (t + 1).exists():
                        scores_for_max(t + 1, s)
                    if t.exists():
                        scores_for_exp(t, s)
                    for slot, gh, piece, off in TIMES_VALUES:
                        if slot == s and (t + off).exists():
                            times_values(t + off, gh, piece)
                    for at, (slot, name, off) in enumerate(ROUNDS):
                        if name == "count" and isinstance(t.n, int) and t.n == B:
                            slot = 9
                        if slot == s and (t + off).exists():
                            before_it = round_before(t, at)
                            if before_it:
                                reached(pe, *before_it)
                            do_round(name, t + off)
                    for part in shared_parts(SHARED_PE, t, s):
                        shared(part[0], int(part[1]), "ab".index(part[2]))

            def centroids():
                pe.wait_ge(set_dve, 3)
                nc.tensor.transpose(heads_ps[:, 0:G + E], cents, ident[0:G + E, 0:G + E]).then_inc(set_pe, 1)
                pe.wait_ge(set_act, 2)
                pe.wait_ge(consts, 2)

            pe.wait_ge(set_pool, 1)
            steps(pe, step, None, centroids)

            pe.wait_ge(sh_out, NQ)

            def transposes(i, k):
                e, r = WR * i + k, k % WR
                pe.wait_ge(rows_in[r], 32 * (i + k // WR + 1))
                reached(pe, e_split, e - 1)
                for c, n in ((0, P), (1, P), (2, CAP - 2 * P)):
                    last = nc.tensor.transpose(x_ps[k % 2][:, c * P:c * P + n], e_rows[r][0:n, c, 0:D], ident[0:n, 0:n])
                last.then_inc(et_full, 1)

            def gate_up(i, k):
                e = WR * i + k
                pe.wait_ge(w_split, e + 1)
                reached(pe, silu_done, e)
                pe.wait_ge(e_split, e + 1)

                def product(dst, first):
                    for c in range(2):
                        hi, lo = w_hi[k % 2][:, first + c, :], w_lo[k % 2][:, first + c, :]
                        mm(dst[:, c, 0:CAP], hi, e_hi[k % 2][:], True, False)
                        mm(dst[:, c, 0:CAP], lo, e_hi[k % 2][:], False, False)
                        last = mm(dst[:, c, 0:CAP], hi, e_lo[k % 2][:], False, True)
                    return last

                product(g_ps, 0).then_inc(g_full, 1)
                reached(pe, hid_ready, e)
                product(u_ps, 2).then_inc(u_full, 1)

            def down(i, k):
                e, r = WR * i + k, k % WR
                pe.wait_ge(wd_in[r], 16 * (i + k // WR + 1))
                pe.wait_ge(hid_ready, e + 1)
                reached(pe, y_out, e - 1)
                for tile, n in ((0, P), (1, P), (2, CAP - 2 * P)):
                    for c in range(2):
                        last = mm(y_ps[k % 2][0:n, tile * D:(tile + 1) * D], hid[k % 2][:, c, tile * P:tile * P + n],
                                  wd_sb[r][:, c, :], c == 0, c == 1)
                last.then_inc(y_full, 1)

            def expert(i, k):
                gate_up(i, k)
                if exists(i, k + 1):
                    transposes(i, k + 1)
                down(i, k - 1)

            transposes(0, 0)
            gate_up(0, 0)
            transposes(0, 1)
            expert_steps(pe, expert)
            down(0, E - 1)

        @block.scalar
        def _(act):
            def copy_out(dst, src, full, count, done, bias=None):
                reached(act, full, count)
                if bias is None:
                    nc.scalar.activation(dst, src, ACT.Copy).then_inc(done, 1)
                else:
                    nc.scalar.activation(dst, src, ACT.Identity, bias=bias).then_inc(done, 1)

            def do_round(name, b):
                misc = bank.get(name)
                n = b.n
                if name in ("max0", "max1"):
                    gh = int(name[-1])
                    reached(act, m_landed[gh], 32 * n)
                    copy_out(max_t[gh][:], misc[0:16, 0:S], mt_full, 2 * n + gh + 1, mt_out)
                elif name == "v":
                    if isinstance(n, int) and n < 2:
                        act.wait_ge(v_blank, 1)
                    reached(act, pv_done, 8 * (n - 1))
                    copy_out(v_ext[b.par][:, :, :, 0:DK],
                             misc[:, 0:2 * D].rearrange("p (c h d) -> p c h d", c=2, d=DK), v_full, n + 1, v_out)
                elif name == "t":
                    copy_out(hc_t[:].rearrange("p c t -> p (c t)"), misc, t_full, n + 1, t_out)
                elif name == "qk":
                    if isinstance(n, int) and n == 0:
                        act.wait_ge(in_w, 16 * 7)
                    reached(act, qk_split, 2 * n)
                    reached(act, rows_full, 4 * n)
                    for kind, bias in ((1, bk_sb), (0, bq_sb)):
                        for dst in (qk, qk_hi):
                            copy_out(dst[:, kind, :], misc[:, kind * S:(kind + 1) * S], qk_full, n + 1, qk_out, bias=bias[:])
                elif name in ("q0", "q1", "k0", "k1"):
                    gh, is_q = int(name[1]), name[0] == "q"
                    count = 4 * n + 2 * gh + is_q + 1
                    if is_q:
                        reached(act, st_full, 16 * (n - 2) + 8 * gh + 8)
                        copy_out(q_rows[2 * b.par + gh][:].rearrange("p g t -> p (g t)"), misc, rows_full, count, rows_out)
                    elif b.first_two():
                        act.wait_ge(consts, 1)
                        act.wait_ge(k_blank, 2 * n + gh + 1)
                        act.wait_ge(rows_full, count)
                        for j in range(4):
                            rows = slice(32 * j, 32 * j + 32)
                            last = nc.scalar.activation(k_rows[2 * b.par + gh][rows, j, :, :],
                                                        misc[rows, :].rearrange("p (g t) -> p g t", g=2),
                                                        ACT.Identity, bias=m_ones[rows, :])
                        last.then_inc(rows_out, 1)
                    else:
                        if not isinstance(n, int) or n > 2:
                            for jp in range(2):
                                act.wait_ge(k_landed[gh][jp], 32 * (n - 2))
                        copy_out(k_stage[gh][:].rearrange("p g t -> p (g t)"), misc, rows_full, count, rows_out, bias=m_ones[:])
                elif name == "heads":
                    copy_out(heads_t[:].rearrange("p c t -> p (c t)"), misc[:, 0:S], ht_full, n + 1, ht_out, bias=bv_sb[:])
                elif name == "h2":
                    reached(act, h2t_free, n)
                    copy_out(h2_t[b.par][:].rearrange("p c t -> p (c t)"), misc[:, 0:S], h2t_full, n + 1, h2t_out)

            def raw_copy(b, gh):
                reached(act, hn_full, 2 * (b.n - 1) + gh + 1)
                copy_out(heads_raw[gh][:].rearrange("p g t -> p (g t)"), heads_ps, pv_done, 8 * b.n + 4 * gh + 4, raw_out)

            def exp_unit(b, u):
                gh, kc, j = u // 8, (u % 8) // 4, u % 4
                reached(act, st_full, 16 * b.n + u + 1)
                reached(act, pv_done, 8 * (b.n - 1) + 4 * gh + 4)
                nc.scalar.activation(probs[gh][:, kc, j // 2, j % 2].rearrange("p g t -> p (g t)"), score_t[u % 2],
                                     ACT.Exp, scale=SCALE).then_inc(exp_done, 1)

            def step(t):
                for s in range(SLOTS):
                    if t.exists():
                        exp_unit(t, s)
                    if s == 4 and (t + -1).exists():
                        raw_copy(t + -1, 1)
                    if s == 12 and t.exists():
                        raw_copy(t, 0)
                    for slot, name, off in ROUNDS:
                        if slot == s and (t + off).exists():
                            do_round(name, t + off)
                    if s == 15 and (t + -1).exists():
                        b = t + -1
                        reached(act, h2_ready, b.n + 1)
                        nc.scalar.activation(h2_rows[b.par][:, :, 1:K, 0:D], spread(h2_rows[b.par][:, :, 0, 0:D], 2, K - 1),
                                             ACT.Copy).then_inc(h2_copied, 1)
                    if s == 4 and (t + -2).exists():
                        b = t + -2
                        reached(act, diff_ready, b.n + 1)
                        nc.scalar.activation(expd[:], diff[:], ACT.Exp).then_inc(exp_ready, 1)
                    for part in shared_parts(SHARED_ACT, t, s):
                        q = int(part[1])
                        act.wait_ge(sh_g, 2 * (q + 1))
                        reached(act, sh_hid, q)
                        nc.scalar.activation(silu_g[:], ps[:, 0:2, :], ACT.Silu).then_inc(sh_silu, 1)

            def tanh_of_gates():
                act.wait_ge(in_route, 16 * 6)
                nc.scalar.activation(gates[:], gates_in[:], ACT.Tanh).then_inc(set_act, 1)

            def centroids():
                act.wait_ge(set_pe, 1)
                nc.scalar.activation(cent_t[:], heads_ps[:, 0:G + E], ACT.Copy).then_inc(set_act, 1)

            steps(act, step, tanh_of_gates, centroids)

            def rows_high(i, k):
                e = WR * i + k
                act.wait_ge(et_full, e + 1)
                reached(act, u_full, e - 1)
                nc.scalar.activation(e_hi[k % 2][:], ps[:, 4 + k % 2, 0:CAP], ACT.Copy).then_inc(e_high, 1)

            def weights_high(i, k):
                e = WR * i + k
                act.wait_ge(w_in[k % WR], 16 * (i + k // WR + 1))
                reached(act, u_full, e - 1)
                nc.scalar.activation(w_hi[k % 2][:], w_sb[k % WR][:], ACT.Copy).then_inc(w_high, 1)

            def silu(i, k):
                e = WR * i + k
                act.wait_ge(g_full, e + 1)
                reached(act, hid_ready, e)
                nc.scalar.activation(silu_g[:, :, 0:CAP], ps[:, 0:2, 0:CAP], ACT.Silu).then_inc(silu_done, 1)

            def expert(i, k):
                silu(i, k)
                if exists(i, k + 1):
                    rows_high(i, k + 1)
                if exists(i, k + 2):
                    weights_high(i, k + 2)

            weights_high(0, 0)
            weights_high(0, 1)
            act.wait_ge(sh_hid, N // 512)
            rows_high(0, 0)
            silu(0, 0)
            rows_high(0, 1)
            weights_high(0, 2)
            expert_steps(act, expert)

        @block.vector
        def _(dve):
            V = nc.vector

            def max_unit(b, s):
                gh, g2, jp, qc = s // 8, (s % 8) // 4, (s % 4) // 2, s % 2
                if s % 8 == 0:
                    reached(dve, neg_ready, 2 * (b.n - 1) + gh + 1)
                reached(dve, sn_full, 16 * b.n + s + 1)
                V.tensor_reduce(neg_max[gh][:, qc, g2, 2 * jp:2 * jp + 2], score_n[s % 2].rearrange("p (j t) -> p j t", j=2),
                                AX.X, ALU.max, negate=True).then_inc(sn_max, 1)

            def max_high(b, gh):
                dve.wait_ge(sn_max, 16 * b.n + 8 * gh + 8)
                reached(dve, mt_full, 2 * (b.n - 1) + gh + 1)
                V.tensor_copy(neg_hl[gh][:, :, :, :, 0], neg_max[gh][:]).then_inc(neg_own, 1)

            def max_low(b, gh):
                dve.wait_ge(neg_own, 2 * b.n + gh + 1)
                V.tensor_tensor(neg_hl[gh][:, :, :, :, 1], neg_max[gh][:], f32(neg_hl[gh][:, :, :, :, 0]),
                                ALU.subtract).then_inc(neg_ready, 1)

            def norm_stats(src, stat, own):
                for c in range(2):
                    V.bn_stats(stat[:, c, :], src[:, c, :]).then_inc(own, 1)

            def norm_aggr(b, stat, aggr, own, done):
                dve.wait_ge(own, 2 * b.n + 2)
                settle(dve)
                for c in range(2):
                    V.bn_aggr(aggr[:, c, :], stat[:, c, :]).then_inc(done, 1)

            def first_stats(b):
                dve.wait_ge(in_x[b.par], 16 * (b.half + 1))
                norm_stats(x_sb[b.par], stat1, stat_own1)

            def first_aggr(b):
                reached(dve, rstd1_ready, b.n)
                norm_aggr(b, stat1, aggr1, stat_own1, var1)

            def first_norm(b):
                dve.wait_ge(rstd1_ready, b.n + 1)
                reached(dve, t_full, b.n)
                dve.wait_ge(var1, 2 * b.n + 2)
                for c in range(2):
                    last = V.tensor_scalar(h1[:, c, :], x_sb[b.par][:, c, :], aggr1[:, c, 0:1], rstd1[:, c:c + 1],
                                           ALU.subtract, ALU.mult)
                last.then_inc(h1_ready, 1)

            def shared(part, q):
                if part == "h":
                    dve.wait_ge(sh_silu, q + 1)
                    dve.wait_ge(sh_u, 2 * (q + 1))
                    reached(dve, sh_y, 2 * (q - 1))
                    V.tensor_tensor(hid[q % 2][:], silu_g[:], ps[:, 2:4, :], ALU.mult).then_inc(sh_hid, 1)
                else:
                    dve.wait_ge(sh_y, 2 * (q + 1))
                    for i in range(2):
                        dve.wait_ge(kept_x[i], 16 * (q + 1))
                    if q >= 2:
                        dve.wait_ge(base_out[q % 2], 16 * (q // 2))
                    V.scalar_tensor_tensor(base[q % 2][:], ps[:, 7, :].rearrange("p (t d) -> p t d", d=D), tanh_f,
                                           x1_all[:, 4 * q:4 * q + 4, :], ALU.mult, ALU.add).then_inc(sh_out, 1)

            def sum_inverses(b, gh):
                dve.wait_ge(hn_full, 2 * b.n + gh + 1)
                V.reciprocal(inv_sum[:], bank["norm" + str(gh)].rearrange("p (a j r) -> p a j r", a=4, j=4)[:, :, :, DK]).then_inc(inv_own, 1)

            def normalise(b, gh):
                raw = bank["norm" + str(gh)].rearrange("p (g c j r) -> p g c j r", g=2, c=2, j=4)
                dve.wait_ge(inv_own, 2 * b.n + gh + 1)
                if gh == 0:
                    reached(dve, ht_full, b.n)
                for g2 in range(2):
                    g = 2 * gh + g2
                    dst = heads[:].rearrange("p c (j g d) -> p c j g d", j=4, g=NG)[:, :, :, g, :]
                    last = V.tensor_tensor(dst, raw[:, g2, :, :, 0:DK], spread(inv_sum[:, 2 * g2:2 * g2 + 2, :], 3, DK), ALU.mult)
                last.then_inc(heads_ready, 1)

            def residual(b):
                dve.wait_ge(wo_full, b.n + 1)
                dve.wait_ge(xr_ready, b.n + 1)
                reached(dve, x1_free, b.n)
                V.scalar_tensor_tensor(x1[b.par][:], bank["wo"][:, 0:2 * D].rearrange("p (c d) -> p c d", c=2), tanh_x,
                                       xr[b.par][:], ALU.mult, ALU.add).then_inc(x1_ready, 1)

            def second_stats(b):
                dve.wait_ge(x1_ready, b.n + 1)
                norm_stats(x1[b.par], stat2, stat_own2)

            def second_aggr(b):
                reached(dve, rstd2_ready, b.n)
                norm_aggr(b, stat2, aggr2, stat_own2, var2)

            def second_norm(b):
                dve.wait_ge(rstd2_ready, b.n + 1)
                if not isinstance(b.n, int) or b.n >= 2:
                    dve.wait_ge(scattered[b.par], 16 + 16 * 2 * K * b.half)
                dve.wait_ge(var2, 2 * b.n + 2)
                for c in range(2):
                    last = V.tensor_scalar(h2_rows[b.par][:, c, 0, 0:D], x1[b.par][:, c, :],
                                           aggr2[:, c, 0:1], rstd2[:, c:c + 1], ALU.subtract, ALU.mult)
                last.then_inc(h2_ready, 1)

            scores = bank["score"][:, 0:2 * (G + E)].rearrange("p (c n) -> p c n", c=2)

            def best_groups(b):
                own = Chain(dve, route_own, ROUTE_OPS * b.n)
                dve.wait_ge(sc_full, b.n + 1)
                settle(dve)
                for c in range(2):
                    own.add(V.max(top_g[:, c, :], scores[:, c, 0:G]))

            def group_indices(b):
                own = Chain(dve, route_own, ROUTE_OPS * b.n + 2)
                own.wait()
                settle(dve)
                for c in range(2):
                    own.add(V.max_index(top_gi[:, c, :], top_g[:, c, :], scores[:, c, 0:G]))
                dve.wait_ge(norm_ready, b.n + 1)
                for c in range(2):
                    last = V.scalar_tensor_tensor(score[:, c, :], scores[:, c, G:G + E], norm2[:, 2, c:c + 1], bias_bc[:],
                                                  ALU.mult, ALU.add)
                last.then_inc(sc_used, 1)

            def group_choices(b):
                own = Chain(dve, route_own, ROUTE_OPS * b.n + 4)
                own.wait()
                own.add(V.tensor_tensor(is_g[:], spread(top_gi[:, :, 0:K], 2, G),
                                        spread(spread(iota_i[:, 0:G], 1, 2), 3, K), ALU.is_equal))

            def group_mask(b):
                own = Chain(dve, route_own, ROUTE_OPS * b.n + 5)
                own.wait()
                own.add(V.tensor_reduce(mask_g[:], is_g[:], AX.X, ALU.max))

            def masked_scores(b):
                own = Chain(dve, route_own, ROUTE_OPS * b.n + 6)
                own.wait()
                own.add(V.tensor_scalar(gap_g[:], mask_g[:], 1e9, -1e9, ALU.mult, ALU.add))
                dve.wait_ge(sc_used, b.n + 1)
                own.add(V.tensor_tensor(masked[:].rearrange("p c (g i) -> p c g i", g=G),
                                        score[:].rearrange("p c (g i) -> p c g i", g=G), spread(mask_g[:], 3, EG), ALU.mult))

            def masked_others(b):
                own = Chain(dve, route_own, ROUTE_OPS * b.n + 8)
                own.wait()
                own.add(V.tensor_tensor(masked[:].rearrange("p c (g i) -> p c g i", g=G),
                                        masked[:].rearrange("p c (g i) -> p c g i", g=G), spread(gap_g[:], 3, EG), ALU.add))

            def best_experts(b):
                own = Chain(dve, route_own, ROUTE_OPS * b.n + 9)
                own.wait()
                settle(dve)
                for c in range(2):
                    own.add(V.max(top_e[:, c, :], masked[:, c, :]))

            def expert_indices(b):
                own = Chain(dve, route_own, ROUTE_OPS * b.n + 11)
                own.wait()
                settle(dve)
                for c in range(2):
                    own.add(V.max_index(top_ei[:, c, :], top_e[:, c, :], masked[:, c, :]))
                V.tensor_tensor(diff[:], top_e[:, :, 0:K], top_e[:, :, 0:1].to_broadcast([P, 2, K]),
                                ALU.subtract).then_inc(diff_ready, 1)

            def expert_choices(b):
                own = Chain(dve, route_own, ROUTE_OPS * b.n + 13)
                own.wait()
                dve.wait_ge(earlier_ready, b.n + 1)
                V.tensor_tensor(chosen[:], spread(top_ei[:, :, 0:K], 3, E),
                                spread(spread(iota_i[:], 1, 2), 1, K).rearrange("p k c e -> p c k e"), ALU.is_equal).then_inc(picked, 1)

            def gate_sums(b):
                own = Chain(dve, place_own, PLACE_OPS * b.n)
                dve.wait_ge(exp_ready, b.n + 1)
                own.add(V.tensor_reduce(gate_sum[:], expd[:], AX.X, ALU.add))

            def gate_inverses(b):
                own = Chain(dve, place_own, PLACE_OPS * b.n + 1)
                own.wait()
                own.add(V.reciprocal(gate_inv[:], gate_sum[:]))

            def gate_values(b):
                own = Chain(dve, place_own, PLACE_OPS * b.n + 2)
                own.wait()
                own.add(V.tensor_tensor(gate[:], expd[:], spread(gate_inv[:], 2, K), ALU.mult))

            def counts_at_choices(b):
                dve.wait_ge(cnt_full, b.n + 1)
                dve.wait_ge(picked, b.n + 1)
                V.tensor_tensor(at_slot[:], chosen[:],
                                spread(bank["count"][:, 0:2 * E].rearrange("p (c e) -> p c e", c=2), 2, K), ALU.mult).then_inc(cnt_used, 1)

            def positions(b):
                own = Chain(dve, place_own, PLACE_OPS * b.n + 3)
                dve.wait_ge(cnt_used, b.n + 1)
                own.add(V.tensor_reduce(pos[:], at_slot[:], AX.X, ALU.add))

            def places(b):
                own = Chain(dve, place_own, PLACE_OPS * b.n + 4)
                own.wait()
                own.add(V.scalar_tensor_tensor(slot_f[:], top_ei[:, :, 0:K], float(CAP), pos[:], ALU.mult, ALU.add))
                own.add(V.tensor_scalar(keep[:], pos[:], float(CAP), None, ALU.is_lt))

            def kept_places(b):
                own = Chain(dve, place_own, PLACE_OPS * b.n + 6)
                own.wait()
                own.add(V.scalar_tensor_tensor(slot_f[:], keep[:], -FAR, slot_f[:], ALU.mult, ALU.add))
                own.add(V.scalar_tensor_tensor(h2_rows[b.par][:, :, :, COL_GATE], gate[:], tanh_f, keep[:], ALU.mult, ALU.mult))

            def place_indices(b):
                own = Chain(dve, place_own, PLACE_OPS * b.n + 8)
                own.wait()
                V.tensor_scalar(slot_i[b.par][:], slot_f[:], FAR, None, ALU.add).then_inc(slots_ready, 1)

            BEFORE = {0: [(max_high, 0, 1)], 1: [(group_indices, -2)], 2: [(group_mask, -2)],
                      3: [(masked_others, -2)], 4: [(expert_indices, -2)],
                      7: [(normalise, -1, 1), (gate_inverses, -2), (counts_at_choices, -2)], 8: [(max_high, 1, 0), (places, -2)],
                      9: [(place_indices, -2)], 11: [(second_stats, -1)],
                      15: [(sum_inverses, 0, 0)]}
            AFTER = {0: [(max_low, 0, 1), (best_groups, -2), (first_stats, 2)], 1: [(group_choices, -2), (first_aggr, 2)],
                     2: [(masked_scores, -2)], 3: [(best_experts, -2), (first_norm, 2)], 4: [(expert_choices, -2)],
                     6: [(sum_inverses, -1, 1), (gate_sums, -2)], 7: [(gate_values, -2), (positions, -2)],
                     8: [(max_low, 1, 0), (kept_places, -2)], 10: [(residual, -1)],
                     11: [(second_aggr, -1)], 13: [(second_norm, -1)], 15: [(normalise, 0, 0)]}

            def step(t):
                for s in range(SLOTS):
                    for work, off, *gh in BEFORE.get(s, ()):
                        if (t + off).exists():
                            work(t + off, *gh)
                    if (t + 1).exists():
                        max_unit(t + 1, s)
                    for work, off, *gh in AFTER.get(s, ()):
                        if (t + off).exists():
                            work(t + off, *gh)
                    for part in shared_parts(SHARED_DVE, t, s):
                        shared(part[0], int(part[1]))

            dve.wait_ge(pool_const, 1)
            dve.wait_ge(pool_const, 2)
            V.tensor_copy(blank[:, :, COL_TOKEN].bitcast(u32), blank_i[:]).then_inc(blank_ready, 1)

            def more_constants():
                V.memset(pick[:].bitcast(fp32), 0.0).then_inc(set_dve, 1)
                dve.wait_ge(set_dve, 1)
                V.tensor_reduce(m_ones[:], ident[:, M_ROW:P:M_STEP], AX.X, ALU.add)
                cols = ident[:].rearrange("p (j g d) -> p g j d", j=4, d=DK)
                def put(kind, at, first, n):
                    dst = pick[:, kind].rearrange("p g (j r) -> p g j r", j=4)[:, :, :, at:at + n]
                    return V.tensor_copy(dst, cols[:, :, :, first:first + n])
                for kind in (0, 2):
                    put(kind, 0, 0, 8)
                for kind in (1, 2):
                    put(kind, 8, 0, 7)
                    put(kind, 16, 7, 1)
                for kind in (0, 3):
                    last = put(kind, 17, 0, 8)
                last.then_inc(consts, 1)
                for i in range(2):
                    V.memset(v_ext[i][:, :, :, DK:32], 0.0).then_inc(set_dve2, 1)
                    dve.wait_ge(set_dve2, i + 1)
                    last = V.memset(v_ext[i][:, :, :, DK], 1.0)
                last.then_inc(v_blank, 1)
                dve.wait_ge(in_route, 16 * 6)
                V.tensor_tensor(cent_sq, cents, cents, ALU.mult).then_inc(set_dve2, 1)
                dve.wait_ge(set_dve2, 3)
                V.tensor_reduce(cent_n[:, 0:1], cent_sq, AX.X, ALU.add).then_inc(set_dve, 1)
                V.memset(ones[:], 1.0)
                V.memset(earlier[0][:], 0.0).then_inc(earlier_ready, 1)
                for i in range(2):
                    last = V.memset(h2_rows[i][:, :, :, D:ROW], 0.0)
                last.then_inc(consts, 1)
                dve.wait_ge(consts, 2)
                dve.wait_ge(pool_const, 4)
                V.tensor_scalar(cents, cents, cent_n[:, 1:2], None, ALU.mult).then_inc(set_dve, 1)

            steps(dve, step, more_constants)

            def hidden(i, k):
                e = WR * i + k
                dve.wait_ge(silu_done, e + 1)
                dve.wait_ge(u_full, e + 1)
                reached(dve, y_full, e - 1)
                V.tensor_tensor(hid[k % 2][:, :, 0:CAP], silu_g[:, :, 0:CAP], ps[:, 2:4, 0:CAP], ALU.mult).then_inc(hid_ready, 1)

            def scale_out(i, k):
                e, r = WR * i + k, k % WR
                dve.wait_ge(y_full, e + 1)
                reached(dve, added[k % 2], 48 * (2 * i + k // 2))
                for tile, n in ((0, P), (1, P), (2, CAP - 2 * P)):
                    V.tensor_copy(e_token[k % 2][0:n, tile:tile + 1], e_rows[r][0:n, tile, COL_TOKEN:COL_TOKEN + 1].bitcast(u32))
                    last = V.tensor_scalar(y_sb[k % 2][0:n, tile, :], ps[0:n, 6 + k % 2, tile * D:(tile + 1) * D],
                                           e_rows[r][0:n, tile, COL_GATE:COL_GATE + 1], None, ALU.mult)
                last.then_inc(y_out, 1)

            def rows_low(i, k):
                e = WR * i + k
                dve.wait_ge(e_high, e + 1)
                reached(dve, u_full, e - 1)
                V.tensor_tensor(e_lo[k % 2][:], ps[:, 4 + k % 2, 0:CAP], f32(e_hi[k % 2][:]), ALU.subtract).then_inc(e_split, 1)

            def weights_low(i, k):
                e = WR * i + k
                dve.wait_ge(w_high, e + 1)
                reached(dve, u_full, e - 1)
                V.tensor_tensor(w_lo[k % 2][:], w_sb[k % WR][:], f32(w_hi[k % 2][:]), ALU.subtract).then_inc(w_split, 1)

            def expert(i, k):
                hidden(i, k)
                if exists(i, k + 1):
                    rows_low(i, k + 1)
                scale_out(i, k - 1)
                if exists(i, k + 2):
                    weights_low(i, k + 2)

            weights_low(0, 0)
            weights_low(0, 1)
            rows_low(0, 0)
            hidden(0, 0)
            rows_low(0, 1)
            weights_low(0, 2)
            expert_steps(dve, expert)
            scale_out(0, E - 1)
        @block.gpsimd
        def _(pool):
            Q = nc.gpsimd

            def step(t):
                o, p, m, o2 = t + -1, t + 2, t + 1, t + -2
                for s in range(SLOTS):
                    if s == 2 and p.exists():
                        own = Chain(pool, pool_ln1, p.n)
                        pool.wait_ge(var1, 2 * p.n + 2)
                        reached(pool, h1_ready, p.n)
                        settle(pool)
                        own.add(Q.tensor_scalar(rstd1[:], aggr1[:, :, 1], 1e-5, None, ALU.add))
                        own.wait()
                        Q.tensor_tensor(rstd1[:], rstd1[:], neg_half[:], ALU.pow).then_inc(rstd1_ready, 1)
                    if s == 4 and isinstance(t.n, int) and t.n == FIRST:
                        for i in range(2):
                            Q.memset(f32(k_rows[i][:]), 0.0).then_inc(k_blank, 1)
                    if s == 3 and o.exists():
                        pool.wait_ge(in_xr[o.par], 16 * (o.half + 1))
                        Q.tensor_tensor(xr[o.par][:], xr[o.par][:], spread(bo_bc[:], 1, 2), ALU.add).then_inc(xr_ready, 1)
                    if s == 5 and o2.exists():
                        pool.wait_ge(picked, o2.n + 1)
                        with nc.allow_low_precision(reason="zeros and ones"):
                            Q.tensor_tensor(chosen_two[:], chosen[:, :, 0:2, :], chosen[:, :, 2:4, :], ALU.add).then_inc(picked_own, 1)
                            pool.wait_ge(picked_own, o2.n + 1)
                            Q.tensor_tensor(chosen_any[:], chosen_two[:, :, 0, :], chosen_two[:, :, 1, :], ALU.add).then_inc(chosen_ready, 1)
                        pool.wait_ge(chosen_ready, o2.n + 1)
                        old, new = earlier[o2.par], earlier[1 - o2.par]
                        with nc.allow_low_precision(reason="counts up to 16"):
                            Q.tensor_tensor(new[:], old[:], chosen_any[:, 0, :], ALU.add).then_inc(earlier_own, 1)
                            pool.wait_ge(earlier_own, o2.n + 1)
                            Q.tensor_tensor(new[:], new[:], chosen_any[:, 1, :], ALU.add).then_inc(earlier_ready, 1)
                        pool.wait_ge(h2_ready, o2.n + 1)
                        settle(pool)
                        Q.tensor_copy(h2_rows[o2.par][:, :, :, COL_TOKEN].bitcast(u32), spread(tok_f[:], 2, K)).then_inc(token_written, 1)
                        pool.wait_ge(token_written, o2.n + 1)
                        settle(pool)
                        Q.tensor_scalar(tok_f[:], tok_f[:], float(S), None, ALU.add).then_inc(tok_next, 1)
                        pool.wait_ge(tok_next, o2.n + 1)
                    if s == 8 and p.exists():
                        reached(pool, rows_full, 4 * p.n)
                        for i in (1, 0):
                            pool.wait_ge(qk_out, 4 * p.n + (2 if i else 4))
                            Q.tensor_tensor(qk_lo[:, i, :], qk[:, i, :], f32(qk_hi[:, i, :]), ALU.subtract).then_inc(qk_split, 1)
                    if s == 11 and o.exists():
                        own = Chain(pool, pool_ln2, 4 * o.n)
                        pool.wait_ge(var2, 2 * o.n + 2)
                        reached(pool, h2_ready, o.n)
                        settle(pool)
                        own.add(Q.tensor_scalar(rstd2[:], aggr2[:, :, 1], 1e-5, None, ALU.add))
                        own.wait()
                        Q.tensor_tensor(rstd2[:], rstd2[:], neg_half[:], ALU.pow).then_inc(rstd2_ready, 1)
                    if s == 13 and o.exists():
                        own = Chain(pool, pool_ln2, 4 * o.n + 1)
                        pool.wait_ge(rstd2_ready, o.n + 1)
                        own.add(Q.tensor_tensor(norm2[:, 0, :], aggr2[:, :, 1], rstd2[:], ALU.mult))
                        own.wait()
                        own.add(Q.tensor_tensor(norm2[:, 1, :], norm2[:, 0, :], rstd2[:], ALU.mult))
                        own.wait()
                        settle(pool)
                        own.add(Q.tensor_scalar(norm2[:, 0, :], norm2[:, 1, :], float(D), 1e-24, ALU.mult, ALU.max))
                        own.wait()
                        reached(pool, sc_used, o.n)
                        Q.tensor_tensor(norm2[:, 2, :], norm2[:, 0, :], neg_half[:], ALU.pow).then_inc(norm_ready, 1)
                    if s in SCATTERS and o2.exists():
                        if s == 9:
                            pool.wait_ge(h2_copied, o2.n + 1)
                            settle(pool)
                            pool.wait_ge(slots_ready, o2.n + 1)
                            settle(pool)
                        for c, k in (divmod(at, K) for at in SCATTERS[s]):
                            Q.indirect_dma_start(
                                out=dispatch[:, :], out_offset=bass.IndirectOffsetOnAxis(ap=slot_i[o2.par][:, c, k:k + 1], axis=0),
                                in_=h2_rows[o2.par][:, c, k, :], in_offset=None,
                                bounds_check=E * CAP - 1, oob_is_err=False).then_inc(scattered[o2.par], 16)
                if isinstance(t.n, int) and t.n == 1:
                    pool.wait_ge(blanked, 16 * 11)
                    for i in range(2):
                        pool.wait_ge(scattered[i], 16)

            own = Chain(pool, set_pool, 0)
            Q.memset(ident[:], 0.0).then_inc(zeroed, 1)
            pool.wait_ge(zeroed, 1)
            own.add(Q.affine_select(out=ident[:], in_=ident[:], compare_op=ALU.not_equal, fill=1.0, base=0,
                                    pattern=[[-1, P]], channel_multiplier=1))
            Q.memset(neg_half[:], -0.5).then_inc(pool_const, 1)
            own.wait()
            Q.memset(blank[:], 0.0)
            Q.iota(blank_i[:], [[P, 3]], base=N, channel_multiplier=1).then_inc(pool_const, 1)

            def more_constants():
                own = Chain(pool, set_pool, 1)
                for i in range(2, 4):
                    Q.memset(f32(k_rows[i][:]), 0.0).then_inc(k_blank, 1)
                own.add(Q.memset(before[:], 0.0))
                own.add(Q.iota(iota_i[:], [[1, E]], base=0, channel_multiplier=0))
                own.add(Q.iota(tok_i[:], [[P, 2]], base=0, channel_multiplier=1))
                own.wait()
                own.add(Q.affine_select(out=before[:], in_=before[:], compare_op=ALU.is_ge, fill=1.0, base=0,
                                        pattern=[[-1, P]], channel_multiplier=1))
                own.add(Q.tensor_copy(tok_f[:], tok_i[:]))
                own.wait()
                pool.sem_inc(pool_const, 1)
                pool.wait_ge(set_act, 1)
                own.add(Q.tensor_scalar(bo_bc[:], bo_bc[:], tanh_x, None, ALU.mult))
                own.wait()
                pool.wait_ge(set_dve, 2)
                own.add(Q.tensor_scalar(cent_n[:, 0:1], cent_n[:, 0:1], 1e-24, None, ALU.max))
                own.wait()
                Q.tensor_tensor(cent_n[:, 1:2], cent_n[:, 0:1], neg_half[0:G + E, 0:1], ALU.pow).then_inc(pool_const, 1)
                own.wait()

            def zero_dump_rows():
                for i in range(2):
                    pool.dma_start(sums[i][N:N + DUMP, :].rearrange("(p r) d -> p r d", p=64),
                                   spread(blank[0:64, 0, 0:D], 1, DUMP // 64)).then_inc(scattered[i], 16)

            steps(pool, step, more_constants, zero_dump_rows)

            def add_rows(i, k):
                e = WR * i + k
                pool.wait_ge(y_out, e + 1)
                reached(pool, added[k % 2], 48 * (2 * i + k // 2))
                settle(pool)
                for tile, n in ((0, P), (1, P), (2, CAP - 2 * P)):
                    Q.indirect_dma_start(
                        out=sums[k % 2][:, :], out_offset=bass.IndirectOffsetOnAxis(
                            ap=e_token[k % 2][0:n, tile:tile + 1], axis=0),
                        in_=y_sb[k % 2][0:n, tile, :], in_offset=None, bounds_check=N + DUMP - 1,
                        compute_op=ALU.add).then_inc(added[k % 2], 16)

            for i in range(2):
                pool.wait_ge(base_out[i], 16 * (N // 1024))
            add_rows(0, 0)
            expert_steps(pool, add_rows)
            pool.wait_ge(sums_in, 16 * 4)
            pool.wait_ge(added[1], 48 * (E // 2))
            pool.dma_start(sums[1][0:N, :].rearrange("(p r) d -> p r d", p=P), x1_all[:],
                           accum_op=ALU.add).then_inc(written, 16)
            pool.wait_ge(written, 16)

_ARGS = ["x", "ctx_1024", "g_xattn", "g_ffn", "L0_xattn_Wq", "L0_xattn_bq", "L0_xattn_Wk", "L0_xattn_bk",
         "L0_xattn_Wv", "L0_xattn_bv", "L0_xattn_Wo", "L0_xattn_bo", "L0_ffn_group_centroids",
         "L0_ffn_expert_centroids", "L0_ffn_bias"]


def kernel(**inputs):
    import numpy as np
    import concourse.bacc as bacc
    from concourse.bass_utils import run_bass_kernel_spmd

    nc = bacc.Bacc("TRN2", target_bir_lowering=False, num_devices=1)
    arrays, args = {}, []

    def give(name, a):
        a = np.ascontiguousarray(a)
        arrays[name] = a
        args.append(nc.dram_tensor(name, a.shape, mybir.dt.from_np(a.dtype), kind="ExternalInput").ap())

    for name in _ARGS:
        a = np.asarray(inputs[name])
        give(name, a.T if name.split("_")[-1] in ("Wq", "Wk", "Wv", "Wo") else a)
    wg, wu, wd = (np.asarray(inputs[f"L0_ffn_{n}"]) for n in ("wg", "wu", "wd"))
    wd = wd.reshape(E, 2, P, D).transpose(0, 2, 1, 3)
    give("w_all", np.concatenate([wg.reshape(E, P, 2, P), wu.reshape(E, P, 2, P), wd], axis=2))
    for name in ("sg", "su", "sd"):
        give(name, inputs[f"L0_ffn_{name}"])
    args.append(nc.dram_tensor("sums0", (N + DUMP, D), mybir.dt.float32, kind="Internal").ap())
    args.append(nc.dram_tensor("out", (N + DUMP, D), mybir.dt.float32, kind="ExternalOutput").ap())
    args.append(nc.dram_tensor("dispatch", (E * CAP, ROW), mybir.dt.float32, kind="Internal").ap())
    gated_attention_and_experts(nc, *args)
    r = run_bass_kernel_spmd(nc, [arrays], core_ids=[0])
    return r.results[0]["out"][:N].reshape(B, S, D)
```
